# Optimizing a Trainium2 kernel written in Bass

```python
import numpy as np
import jax
import jax.numpy as jnp

def _softmax(x, axis=-1):
    return jax.nn.softmax(x, axis=axis)

def _gelu(x):
    return jax.nn.gelu(x, approximate=True)

def _silu(x):
    return jax.nn.silu(x)

def _sigmoid(x):
    return jax.nn.sigmoid(x)

def _layernorm(x, axis=-1, eps=1e-05):
    m = jnp.mean(x, axis=axis, keepdims=True)
    v = jnp.var(x, axis=axis, keepdims=True)
    return (x - m) / jnp.sqrt(v + eps)

def _scatter_add(tgt, idx, src, axis=0):
    return tgt.at[idx].add(src)

def _segment_sum(src, seg, n):
    return jax.ops.segment_sum(src, seg, n)
kernel_name = 'mk_conv_attn_hybrid_d2_conv_nchw384_r2_b8c695'

def setup_inputs(seed: int=0):
    np.random.seed(seed)
    _w = jnp.asarray

    def _rec_inputs():
        import jax
        import jax.numpy as jnp
        _gk = jax.random.key(seed)
        x = -0.0004039 + 1 * jax.random.normal(jax.random.fold_in(_gk, 1), (8, 192, 32, 32), jnp.float32)
        return x
    x = _rec_inputs()

    def _L0_conv_setup():
        import jax, jax.numpy as jnp
        import numpy as np
        MIN_V, MAX_V, NORM = (0.0, 4.0, 4.0)
        NUM_HEADS = 8
        BN_EPS = 1e-05

        @jax.custom_vjp
        def quant(x):
            return jnp.round(jnp.clip(x, MIN_V, MAX_V))

        def _quant_fwd(x):
            return (jnp.round(jnp.clip(x, MIN_V, MAX_V)), x)

        def _quant_bwd(x, g):
            return (jnp.where((x < MIN_V) | (x > MAX_V), 0.0, g),)
        quant.defvjp(_quant_fwd, _quant_bwd)

        def spike(x):
            return quant(x) / NORM

        def conv_bn(x, w, gamma, beta, mean, var):
            y = jnp.einsum('oc,bchw->bohw', w, x)
            s = gamma / jnp.sqrt(var + BN_EPS)
            return y * s[None, :, None, None] + (beta - mean * s)[None, :, None, None]
        key = jax.random.key(seed)
        B, C, H, W = (8, 192, 32, 32)
        ks = jax.random.split(key, 21)
        d = {'x': jax.random.normal(ks[0], (B, C, H, W), jnp.float32)}
        i = 1
        for p in ('q', 'k', 'v', 'p'):
            d[f'{p}_w'] = jax.random.normal(ks[i], (C, C), jnp.float32) * 0.05
            i += 1
            d[f'{p}_gamma'] = jax.random.uniform(ks[i], (C,), jnp.float32, 0.5, 1.5)
            i += 1
            d[f'{p}_beta'] = jax.random.normal(ks[i], (C,), jnp.float32) * 0.1
            i += 1
            d[f'{p}_mean'] = jax.random.normal(ks[i], (C,), jnp.float32) * 0.1
            i += 1
            d[f'{p}_var'] = jax.random.uniform(ks[i], (C,), jnp.float32, 0.5, 1.5)
            i += 1
        return d
    _L0_conv_all = _L0_conv_setup()
    _L0_conv_in = {k: v for k, v in _L0_conv_all.items() if k in ('q_w', 'q_gamma', 'q_beta', 'q_mean', 'q_var', 'k_w', 'k_gamma', 'k_beta', 'k_mean', 'k_var', 'v_w', 'v_gamma', 'v_beta', 'v_mean', 'v_var', 'p_w', 'p_gamma', 'p_beta', 'p_mean', 'p_var')}
    del _L0_conv_all

    def _L1_attn_setup():
        import jax, jax.numpy as jnp
        import numpy as np
        B, S, E, H = (8, 1024, 192, 6)
        D = E // H
        key = jax.random.key(seed)
        ks = jax.random.split(key, 5)
        s = 1.0 / np.sqrt(E)
        return {'x': jax.random.normal(ks[0], (B, S, E), dtype=jnp.float32), 'Wq': jax.random.normal(ks[1], (E, E), dtype=jnp.float32) * s, 'Wk': jax.random.normal(ks[2], (E, E), dtype=jnp.float32) * s, 'Wv': jax.random.normal(ks[3], (E, E), dtype=jnp.float32) * s, 'Wo': jax.random.normal(ks[4], (E, E), dtype=jnp.float32) * s, 'bo': jnp.zeros((E,), dtype=jnp.float32)}
    _L1_attn_all = _L1_attn_setup()
    _L1_attn_in = {k: v for k, v in _L1_attn_all.items() if k in ('Wq', 'Wk', 'Wv', 'Wo', 'bo')}
    del _L1_attn_all

    def _L1_ffn_setup():
        import jax, jax.numpy as jnp
        import numpy as np
        NUM_EXPERTS = 4
        TOP_K = 2
        DIM = 192
        HID = 4 * DIM
        key = jax.random.key(seed)
        ks = jax.random.split(key, 5)
        B, S = (16, 1024)
        scale_in = 1.0 / np.sqrt(DIM)
        scale_hid = 1.0 / np.sqrt(HID)
        return {'x': jax.random.normal(ks[0], (B, S, DIM), dtype=jnp.float32), 'gate_w': jax.random.normal(ks[1], (DIM, NUM_EXPERTS), dtype=jnp.float32) * scale_in, 'gate_b': jnp.zeros((NUM_EXPERTS,), dtype=jnp.float32), 'w1': jax.random.normal(ks[2], (NUM_EXPERTS, DIM, HID), dtype=jnp.float32) * scale_in, 'b1': jnp.zeros((NUM_EXPERTS, HID), dtype=jnp.float32), 'w2': jax.random.normal(ks[3], (NUM_EXPERTS, HID, DIM), dtype=jnp.float32) * scale_hid, 'b2': jnp.zeros((NUM_EXPERTS, DIM), dtype=jnp.float32)}
    _L1_ffn_all = _L1_ffn_setup()
    _L1_ffn_in = {k: v for k, v in _L1_ffn_all.items() if k in ('gate_w', 'gate_b', 'w1', 'b1', 'w2', 'b2')}
    del _L1_ffn_all
    return {'x': x, 'L0_conv_q_w': _L0_conv_in['q_w'], 'L0_conv_q_gamma': _L0_conv_in['q_gamma'], 'L0_conv_q_beta': _L0_conv_in['q_beta'], 'L0_conv_q_mean': _L0_conv_in['q_mean'], 'L0_conv_q_var': _L0_conv_in['q_var'], 'L0_conv_k_w': _L0_conv_in['k_w'], 'L0_conv_k_gamma': _L0_conv_in['k_gamma'], 'L0_conv_k_beta': _L0_conv_in['k_beta'], 'L0_conv_k_mean': _L0_conv_in['k_mean'], 'L0_conv_k_var': _L0_conv_in['k_var'], 'L0_conv_v_w': _L0_conv_in['v_w'], 'L0_conv_v_gamma': _L0_conv_in['v_gamma'], 'L0_conv_v_beta': _L0_conv_in['v_beta'], 'L0_conv_v_mean': _L0_conv_in['v_mean'], 'L0_conv_v_var': _L0_conv_in['v_var'], 'L0_conv_p_w': _L0_conv_in['p_w'], 'L0_conv_p_gamma': _L0_conv_in['p_gamma'], 'L0_conv_p_beta': _L0_conv_in['p_beta'], 'L0_conv_p_mean': _L0_conv_in['p_mean'], 'L0_conv_p_var': _L0_conv_in['p_var'], 'L1_attn_Wq': _L1_attn_in['Wq'], 'L1_attn_Wk': _L1_attn_in['Wk'], 'L1_attn_Wv': _L1_attn_in['Wv'], 'L1_attn_Wo': _L1_attn_in['Wo'], 'L1_attn_bo': _L1_attn_in['bo'], 'L1_ffn_gate_w': _L1_ffn_in['gate_w'], 'L1_ffn_gate_b': _L1_ffn_in['gate_b'], 'L1_ffn_w1': _L1_ffn_in['w1'], 'L1_ffn_b1': _L1_ffn_in['b1'], 'L1_ffn_w2': _L1_ffn_in['w2'], 'L1_ffn_b2': _L1_ffn_in['b2']}

def reference(x, L0_conv_q_w, L0_conv_q_gamma, L0_conv_q_beta, L0_conv_q_mean, L0_conv_q_var, L0_conv_k_w, L0_conv_k_gamma, L0_conv_k_beta, L0_conv_k_mean, L0_conv_k_var, L0_conv_v_w, L0_conv_v_gamma, L0_conv_v_beta, L0_conv_v_mean, L0_conv_v_var, L0_conv_p_w, L0_conv_p_gamma, L0_conv_p_beta, L0_conv_p_mean, L0_conv_p_var, L1_attn_Wq, L1_attn_Wk, L1_attn_Wv, L1_attn_Wo, L1_attn_bo, L1_ffn_gate_w, L1_ffn_gate_b, L1_ffn_w1, L1_ffn_b1, L1_ffn_w2, L1_ffn_b2):
    import jax
    import jax.numpy as jnp

    def _L0_conv_ref(x, q_w, q_gamma, q_beta, q_mean, q_var, k_w, k_gamma, k_beta, k_mean, k_var, v_w, v_gamma, v_beta, v_mean, v_var, p_w, p_gamma, p_beta, p_mean, p_var):
        import jax, jax.numpy as jnp
        import numpy as np
        MIN_V, MAX_V, NORM = (0.0, 4.0, 4.0)
        NUM_HEADS = 8
        BN_EPS = 1e-05

        @jax.custom_vjp
        def quant(x):
            return jnp.round(jnp.clip(x, MIN_V, MAX_V))

        def _quant_fwd(x):
            return (jnp.round(jnp.clip(x, MIN_V, MAX_V)), x)

        def _quant_bwd(x, g):
            return (jnp.where((x < MIN_V) | (x > MAX_V), 0.0, g),)
        quant.defvjp(_quant_fwd, _quant_bwd)

        def spike(x):
            return quant(x) / NORM

        def conv_bn(x, w, gamma, beta, mean, var):
            y = jnp.einsum('oc,bchw->bohw', w, x)
            s = gamma / jnp.sqrt(var + BN_EPS)
            return y * s[None, :, None, None] + (beta - mean * s)[None, :, None, None]
        B, C, H, W = x.shape
        N = H * W
        hd = C // NUM_HEADS
        scale = hd ** (-0.5)
        xs = spike(x)
        q = spike(conv_bn(xs, q_w, q_gamma, q_beta, q_mean, q_var))
        k = spike(conv_bn(xs, k_w, k_gamma, k_beta, k_mean, k_var))
        v = spike(conv_bn(xs, v_w, v_gamma, v_beta, v_mean, v_var))

        def to_heads(t):
            return t.reshape(B, NUM_HEADS, hd, N).transpose(0, 1, 3, 2)
        q, k, v = (to_heads(q), to_heads(k), to_heads(v))
        kv = jnp.einsum('bhnd,bhne->bhde', k, v)
        attn = jnp.einsum('bhnd,bhde->bhne', q, kv) * (scale * 2)
        a = attn.transpose(0, 1, 3, 2).reshape(B, C, N)
        a = spike(a).reshape(B, C, H, W)
        out = conv_bn(a, p_w, p_gamma, p_beta, p_mean, p_var)
        return out

    def _L1_attn_ref(x, Wq, Wk, Wv, Wo, bo):
        import jax, jax.numpy as jnp
        import numpy as np
        B, S, E, H = (8, 1024, 192, 6)
        D = E // H
        b, s, e = x.shape
        q = (x @ Wq).reshape(b, s, H, D).transpose(0, 2, 1, 3)
        k = (x @ Wk).reshape(b, s, H, D).transpose(0, 2, 1, 3)
        v = (x @ Wv).reshape(b, s, H, D).transpose(0, 2, 1, 3)
        scores = jnp.einsum('bhqd,bhkd->bhqk', q, k) / jnp.sqrt(jnp.asarray(D, x.dtype))
        causal = jnp.tril(jnp.ones((s, s), dtype=bool))
        scores = jnp.where(causal, scores, -jnp.inf)
        attn = jax.nn.softmax(scores, axis=-1)
        out = jnp.einsum('bhqk,bhkd->bhqd', attn, v)
        out = out.transpose(0, 2, 1, 3).reshape(b, s, e)
        return out @ Wo + bo

    def _L1_ffn_ref(x, gate_w, gate_b, w1, b1, w2, b2):
        import jax, jax.numpy as jnp
        import numpy as np
        NUM_EXPERTS = 4
        TOP_K = 2
        DIM = 192
        HID = 4 * DIM
        scores = jnp.einsum('bsd,de->bse', x, gate_w) + gate_b
        probs = jax.nn.softmax(scores, axis=-1)
        topk_vals, topk_idx = jax.lax.top_k(probs, TOP_K)
        mask = jnp.sum(jax.nn.one_hot(topk_idx, NUM_EXPERTS, dtype=probs.dtype), axis=-2)
        masked = probs * mask
        masked = masked / (jnp.sum(masked, axis=-1, keepdims=True) + 1e-09)
        h = jax.nn.gelu(jnp.einsum('bsd,edh->ebsh', x, w1) + b1[:, None, None, :], approximate=False)
        y = jnp.einsum('ebsh,ehd->ebsd', h, w2) + b2[:, None, None, :]
        out = jnp.einsum('bse,ebsd->bsd', masked, y)
        return out

    def _gn(v, G=32, eps=1e-05):
        B_, C_, H_, W_ = v.shape
        g = v.reshape(B_, G, C_ // G, H_, W_)
        m = jnp.mean(g, axis=(2, 3, 4), keepdims=True)
        s = jnp.var(g, axis=(2, 3, 4), keepdims=True)
        return ((g - m) / jnp.sqrt(s + eps)).reshape(v.shape)

    def _ln_c(v, eps=1e-06):
        m = jnp.mean(v, axis=1, keepdims=True)
        s = jnp.var(v, axis=1, keepdims=True)
        return (v - m) / jnp.sqrt(s + eps)

    def _ln_t(v, eps=1e-05):
        m = jnp.mean(v, axis=-1, keepdims=True)
        s = jnp.var(v, axis=-1, keepdims=True)
        return (v - m) / jnp.sqrt(s + eps)

    def _to_tokens(v):
        B_, C_, H_, W_ = v.shape
        return v.reshape(B_, C_, H_ * W_).transpose(0, 2, 1)

    def _from_tokens(t, like):
        B_, C_, H_, W_ = like.shape
        return t.transpose(0, 2, 1).reshape(B_, C_, H_, W_)
    x = x + _L0_conv_ref(_gn(x), L0_conv_q_w, L0_conv_q_gamma, L0_conv_q_beta, L0_conv_q_mean, L0_conv_q_var, L0_conv_k_w, L0_conv_k_gamma, L0_conv_k_beta, L0_conv_k_mean, L0_conv_k_var, L0_conv_v_w, L0_conv_v_gamma, L0_conv_v_beta, L0_conv_v_mean, L0_conv_v_var, L0_conv_p_w, L0_conv_p_gamma, L0_conv_p_beta, L0_conv_p_mean, L0_conv_p_var)
    t = _to_tokens(x)
    t = t + _L1_attn_ref(_ln_t(t), L1_attn_Wq, L1_attn_Wk, L1_attn_Wv, L1_attn_Wo, L1_attn_bo)
    t = t + _L1_ffn_ref(_ln_t(t), L1_ffn_gate_w, L1_ffn_gate_b, L1_ffn_w1, L1_ffn_b1, L1_ffn_w2, L1_ffn_b2)
    x = _from_tokens(t, x)
    return x

_drawn_inputs = setup_inputs


def setup_inputs(seed=0):
    import zlib

    import numpy as np

    out = dict(_drawn_inputs(seed))
    spreads = {'L1_attn_bo': (0.0, 0.1),
     'L1_ffn_gate_b': (0.0, 0.1),
     'L1_ffn_b1': (0.0, 0.1),
     'L1_ffn_b2': (0.0, 0.1)}
    factors = {'L0_conv_q_w': 8.0,
     'L0_conv_k_w': 4.038,
     'L0_conv_k_gamma': 8.0,
     'L0_conv_k_mean': 8.0,
     'L0_conv_k_beta': 5.176,
     'L0_conv_k_var': 3.166}
    for name, (base, spread) in spreads.items():
        noise = np.random.default_rng([zlib.crc32(name.encode()), seed]).standard_normal(out[name].shape)
        drawn = base * np.exp(spread * noise) if base else spread * noise
        out[name] = jnp.asarray(drawn.astype(out[name].dtype))
    for name, factor in factors.items():
        out[name] = (out[name] * factor).astype(out[name].dtype)
    return out
```

```python
from contextlib import ExitStack

import numpy as np

import concourse.bass as bass
from concourse import mybir

F32 = mybir.dt.float32
F16 = mybir.dt.float16
BF16 = mybir.dt.bfloat16
ALU = mybir.AluOpType
ACT = mybir.ActivationFunctionType
AX = mybir.AxisListType

B, C, N = 8, 192, 1024
P = 128
CC = C // 2
NT = N // P
QB = 512
NB = N // QB
TB = QB // P
TAIL = C - P
GROUPS = 32
SPIKE_HEADS = 8
HEADS, D = 6, C // 6
PAIRS = HEADS // 2
EXPERTS, HID = 4, 4 * C
HC = HID // P
CHUNKS = EXPERTS * HC

COL_Q, COL_K, COL_V = 0, C, 2 * C
COL_GATE = 3 * C
COL_W1 = COL_GATE + EXPERTS
IN_COLS = COL_W1 + EXPERTS * HID
OUT_CHUNKS = CHUNKS + 2

W_SCALE = 2.0 ** 6
U_SCALE = 2.0 ** 8
A_SCALE = 2.0 ** 4
P_SCALE = 2.0 ** 10
M_SCALE = 2.0 ** 8
SPIKE_SCALE = W_SCALE * 4
MAGIC = 1.5 * 2.0 ** 23
MASKED = -1.0e30
SPIKE_ATTN = float(np.float32((C // SPIKE_HEADS) ** -0.5 * 2)) / 64

K_ID, K_MKQ, K_MQK, K_GRP, K_BLK = 0, P, 2 * P, 3 * P, 3 * P + CC
K_ROW, K_TIE = 3 * P + 2 * CC, 3 * P + 2 * CC + 1
K_COLS = K_TIE + EXPERTS * EXPERTS

DVE_STEPS = 100

M_ITEMS = [(b, t, half, pair) for b in range(NB) for t in range(b * TB, (b + 1) * TB)
           for half in range(b + 1) for pair in range(PAIRS)]
E_ITEMS = [(b, pair, kc) for b in range(NB) for pair in range(PAIRS) for kc in range((b + 1) * TB)]
NM, NE = len(M_ITEMS), len(E_ITEMS)
PV_LAG = 2
F_LAG = 2
N_P32, N_P16, N_H = 3, 4, 4


class Count:

    def __init__(self):
        self.n = 0

    def more(self, n):
        self.n += n
        return self.n


def run_ends():
    return [j for j, (b, pair, kc) in enumerate(E_ITEMS) if kc == (b + 1) * TB - 1]


def build(nc, x_ch, x_tok, consts, w_conv, bn_rows, bn_q, w_in, w_out, b1, b2, gate_b, out):
    with ExitStack() as ctx:
        def sb(name, shape, dt):
            return ctx.enter_context(nc.sbuf_tensor(name, shape, dt))

        per_image = {}

        def sem(name, gain=0):
            handle = ctx.enter_context(nc.semaphore(name))
            per_image[handle.name] = gain
            return handle

        def at(s, img, n):
            return img * per_image[s.name] + n

        def whole(s):
            return per_image[s.name]

        kst = sb("kst", [P, K_COLS], F32)
        ident16 = sb("ident16", [P, P], F16)
        identb = sb("identb", [P, P], BF16)
        mask_kq = sb("mask_kq", [P, P], BF16)
        mask_qk = sb("mask_qk", [P, P], BF16)
        ones16 = sb("ones16", [P, P], F16)
        exp_bias = sb("exp_bias", [P, 1], F32)
        ident = kst[:, K_ID:K_ID + P]
        group = kst[0:CC, K_GRP:K_GRP + CC]
        block_diag = kst[0:CC, K_BLK:K_BLK + CC]
        NCV = 4 * C
        wc_h = sb("wc_h", [CC + 1, 2, NCV], F16)
        wc_l = sb("wc_l", [CC + 1, 2, NCV], F16)
        q_sb = sb("q_sb", [CC, 2, 2], F32)
        win_h = sb("win_h", [P, IN_COLS], F16)
        win_l = sb("win_l", [P, IN_COLS], F16)
        win_t = sb("win_t", [P, IN_COLS], F16)
        wout_h = sb("wout_h", [P, OUT_CHUNKS, C], F16)
        wout_l = sb("wout_l", [P, OUT_CHUNKS, C], F16)
        b1_sb = sb("b1_sb", [P, CHUNKS], F32)
        b2_sb = sb("b2_sb", [2, EXPERTS * C], F16)
        gb_sb = sb("gb_sb", [P, NT, EXPERTS], F32)

        xc = sb("xc", [CC, 2, N], F32)
        xt = sb("xt", [P, NT, C], F32)
        tmp = sb("tmp", [P, NT * 2 * C], F32)
        xs = sb("xs", [CC + 1, 2, N], F16)
        ai = sb("ai", [CC + 1, 2, N], F16)
        kv32 = sb("kv32", [CC, 2, CC], F32)
        kv_h = sb("kv_h", [CC, 2, CC], F16)
        kv_l = sb("kv_l", [CC, 2, CC], F16)
        acc = sb("acc", [P, NT, C], F32)
        u = sb("u", [P, NT, 2 * P], F32)
        uh = sb("uh", [P, 2, N], F16)
        ul = sb("ul", [P, 2, N], F16)
        qk_all = sb("qk_all", [P, 8 * N], F16)
        qk_h = qk_all[:, 0:4 * N].rearrange("p (j n) -> p j n", j=4)
        qk_l = qk_all[:, 4 * N:8 * N].rearrange("p (j n) -> p j n", j=4)
        q4 = sb("q4", [CC + 2, HEADS, N], F16)
        k4 = sb("k4", [CC + 2, HEADS, N], F16)
        v_h = sb("v_h", [P, NT, C], F16)
        v_l = sb("v_l", [P, NT, C], F16)
        room32 = sb("room32", [P, N_P32 * 2 * QB], F32)
        p32 = room32[:, :].rearrange("p (s a n) -> p s a n", s=N_P32, a=2)
        as16 = room32[:, :].bitcast(F16)
        kvi = as16[:, 0:NT * 2 * C].rearrange("p (t c) -> p t c", t=NT)
        qi = as16[0:CC, 2 * NT * C:2 * NT * C + 2 * N].rearrange("p (c n) -> p c n", c=2)
        room16 = sb("room16", [P, 2 * N_P16 * 2 * QB], F16)
        half = N_P16 * 2 * QB
        p_h = room16[:, 0:half].rearrange("p (s a n) -> p s a n", s=N_P16, a=2)
        p_l = room16[:, half:2 * half].rearrange("p (s a n) -> p s a n", s=N_P16, a=2)
        h32 = room16[:, 0:half].bitcast(F32).rearrange("p (s n) -> p s n", s=N_H)
        h_h = room16[:, half:half + N_H * QB].rearrange("p (s n) -> p s n", s=N_H)
        h_l = room16[:, half + N_H * QB:2 * half].rearrange("p (s n) -> p s n", s=N_H)
        stage = room16[:, :].bitcast(F32).rearrange("p (s n) -> p s n", s=2)
        rden = sb("rden", [2 * D, QB], F32)
        o32 = tmp[:, 0:2 * N].rearrange("p (c n) -> p c n", c=2)
        o_h = sb("o_h", [P, 2, N], F16)
        o_l = sb("o_l", [P, 2, N], F16)

        gn_st = sb("gn_st", [CC, 2, 2, 6], F32)
        gn_s = sb("gn_s", [CC, 2], F32)
        gn_d = sb("gn_d", [CC, 2, 4], F32)
        gn_v = sb("gn_v", [CC, 2], F32)
        gn_m = sb("gn_m", [CC, 2], F32)
        gn_b = sb("gn_b", [CC, 2], F32)
        ln_st = sb("ln_st", [P, NT, 6], F32)
        ln_s = sb("ln_s", [P, 3, NT], F32)
        ln_m = sb("ln_m", [P, NT], F32)
        veps = sb("veps", [P, NT], F32)
        rs0 = sb("rs0", [P, NT], F32)
        rs1 = sb("rs1", [P, NT], F32)
        rstd = sb("rstd", [P, NT], F32)
        minus_half = sb("minus_half", [P, NT], F32)
        mx = sb("mx", [P, 2, NT, HEADS], F32)
        m16 = sb("m16", [P, NT, HEADS, 2], F16)
        mrow = sb("mrow", [2 * HEADS, N], F16)
        gsc = sb("gsc", [P, NT, EXPERTS], F32)
        gex = sb("gex", [P, NT, EXPERTS], F32)
        gpr = sb("gpr", [P, NT, EXPERTS], F32)
        gt1 = sb("gt1", [P, NT], F32)
        gt2 = sb("gt2", [P, NT], F32)
        gcmp = sb("gcmp", [P, NT, EXPERTS, EXPERTS], F32)
        gcm2 = sb("gcm2", [P, NT, EXPERTS, EXPERTS], F32)
        gcnt = sb("gcnt", [P, NT, EXPERTS], F32)
        gate = sb("gate", [P, NT, EXPERTS], F32)

        b2_ones = sb("b2_ones", [2, P], F16)

        bn_st = qk_all[0:CC + 1, 0:8 * N].bitcast(F32)[:, 0:12 * C].rearrange("p (k c) -> p k c", k=4)
        bn_t = room32[0:CC + 1, 0:9 * C].rearrange("p (k c) -> p k c", k=3)
        bq_st = sb("bq_st", [CC, 2, 4], F32)
        bq_t = sb("bq_t", [CC, 4, 2], F32)
        b2_st = sb("b2_st", [2, EXPERTS * C], F32)
        b2_t = sb("b2_t", [2, EXPERTS * C], F16)

        ps = ctx.enter_context(nc.psum_tensor("ps", [P, 8, QB], F32))

        small_in = sem("small_in")
        stage_in = [sem("stage_in0"), sem("stage_in1")]
        stage_hi = sem("stage_hi")
        stage_lo = sem("stage_lo")
        setup_dve = sem("setup_dve")
        setup_pool = sem("setup_pool")
        consts_ready = sem("consts_ready")

        x_ch_in = sem("x_ch_in", 16)
        x_tok_in = sem("x_tok_in", 16)
        xt_used = sem("xt_used", 1)
        dve_step = sem("dve_step", DVE_STEPS)
        gn_rhs = sem("gn_rhs", 2)
        gn_ps = sem("gn_ps", 2)
        var_ready = sem("var_ready", 3)
        pow_done = sem("pow_done", 3)
        gn_ready = sem("gn_ready", 1)
        x_relu = sem("x_relu", 2)
        xs_ready = sem("xs_ready", 2)
        q_ps = sem("q_ps", 2 * NB)
        q_relu = sem("q_relu", 2 * NB)
        kv_ps = sem("kv_ps", NT)
        kv_relu = sem("kv_relu", NT)
        q_int = sem("q_int", NB)
        kv_int = sem("kv_int", NT // 2)
        kvm_ps = sem("kvm_ps", 1)
        kv_split = sem("kv_split", 1)
        at_ps = sem("at_ps", NB)
        a_int = sem("a_int", NB)
        p_ps = sem("p_ps", NT // 2)
        u_ready = sem("u_ready", 2 * NB)
        tr_ps = sem("tr_ps", 2 * NB)
        uh_done = sem("uh_done", 2 * NB)
        ul_done = sem("ul_done", 2 * NB)
        qk_ps = sem("qk_ps", 4 * NB)
        qk_hi = sem("qk_hi", 4 * NB)
        qk_lo = sem("qk_lo", 4 * NB)
        heads_in = sem("heads_in", 16 * 6 * HEADS)
        v_ps = sem("v_ps", NT // 2)
        v_hi = sem("v_hi", NT // 2)
        v_lo = sem("v_lo", NT // 2)
        m_ps = sem("m_ps", NM)
        m_used = sem("m_used", NM)
        m_split = sem("m_split", NB)
        mrow_ps = sem("mrow_ps", NB)
        mrow_done = sem("mrow_done", NB)
        mrow_in = [sem("mrow_in0", 16 * HEADS), sem("mrow_in1", 16 * HEADS)]
        e_ps = sem("e_ps", NE)
        e_done = sem("e_done", NE)
        p_hi = sem("p_hi", NE)
        p_lo_dve = sem("p_lo_dve", (NE + 1) // 2)
        p_lo_pool = sem("p_lo_pool", NE // 2)
        pv_done = sem("pv_done", NE)
        o_done = sem("o_done", NB * PAIRS)
        o_hi = sem("o_hi", NB * PAIRS)
        o_lo = sem("o_lo", NB * PAIRS)
        wo_ps = sem("wo_ps", NT // 2)
        gate_ps = sem("gate_ps", 1)
        gate_used = sem("gate_used", 1)
        gate_sub = sem("gate_sub", 1)
        gate_exp = sem("gate_exp", 1)
        h_ps = sem("h_ps", NB * CHUNKS)
        h_act = sem("h_act", NB * CHUNKS)
        h_hi = sem("h_hi", NB * CHUNKS)
        h_lo = sem("h_lo", NB * CHUNKS)
        f2_done = sem("f2_done", NB * CHUNKS)
        y_used = sem("y_used", NB * EXPERTS)
        stored = sem("stored", 16 * NB)

        W = 2048
        pieces = [(kind, c0, min(W, IN_COLS - c0)) for kind in ("head", "tail")
                  for c0 in range(0, IN_COLS, W)]
        FLAT = OUT_CHUNKS * C
        pieces += [("out", c0, min(W, FLAT - c0)) for c0 in range(0, FLAT, W)]
        wconv_pieces = 2
        n_small = 7
        wout_h_flat = wout_h[:, :, :].rearrange("p k c -> p (k c)")
        wout_l_flat = wout_l[:, :, :].rearrange("p k c -> p (k c)")

        block = ctx.enter_context(nc.Block())

        @block.sync
        def _(sp):
            for dst, src in ((kst[:, :], consts), (bn_st[:, :, :], bn_rows), (bq_st[:, :, :], bn_q),
                             (b1_sb[:, :], b1), (b2_st[:, :], b2), (gb_sb[:, :, :], gate_b),
                             (tmp[0:CC + 1, 0:2 * NCV], w_conv)):
                sp.dma_start(dst, src).then_inc(small_in, 16)
            for n, (kind, c0, w) in enumerate(pieces):
                if n >= 2:
                    sp.wait_ge(stage_lo, n - 1)
                src = {"head": w_in[0], "tail": w_in[1], "out": w_out}[kind][:, c0:c0 + w]
                sp.dma_start(stage[:, n % 2, 0:w], src).then_inc(stage_in[n % 2], 16)

            with sp.Fori(0, B) as img:
                sp.wait_ge(xs_ready, at(xs_ready, img, 0))
                sp.dma_start(xc[:, :, :], x_ch[img]).then_inc(x_ch_in, 16)
                sp.wait_ge(xt_used, at(xt_used, img, 0))
                sp.dma_start(xt[:, :, :], x_tok[img]).then_inc(x_tok_in, 16)
                sp.wait_ge(qk_hi, at(qk_hi, img, 4 * NB))
                sp.wait_ge(qk_lo, at(qk_lo, img, 4 * NB))
                for dst, first, parts in ((k4, 2, (qk_h, qk_l, qk_h)), (q4, 0, (qk_h, qk_h, qk_l))):
                    for h in range(HEADS):
                        row = D * (h % 4)
                        for n, part in enumerate(parts):
                            sp.dma_start(dst[D * n:D * n + D, h, :],
                                         part[row:row + D, first + h // 4, :]).then_inc(heads_in, 16)
                for b in range(NB):
                    sp.wait_ge(mrow_done, at(mrow_done, img, b + 1))
                    for h in range(HEADS):
                        sp.dma_start(q4[3 * D:3 * D + 2, h, b * QB:(b + 1) * QB],
                                     mrow[2 * h:2 * h + 2, b * QB:(b + 1) * QB])\
                          .then_inc(mrow_in[b], 16)

        @block.tensor
        def _(pe):
            pe.wait_ge(consts_ready, 1)

            with pe.Fori(0, B) as img:
                def project(dst, cols, tok, tokens_stationary):
                    for n, (w, a, c) in enumerate(((win_h, uh, 0), (win_l, uh, 0), (win_h, ul, 0),
                                                   (win_t, uh, 1), (win_t, ul, 1))):
                        lhs, rhs = w[:, cols], a[:, c, tok]
                        if tokens_stationary:
                            lhs, rhs = rhs, lhs
                        mm = pe.matmul(dst, lhs, rhs, start=(n == 0), stop=(n == 4))
                    return mm

                def transpose_block(k, b):
                    pe.wait_ge(u_ready, at(u_ready, img, k * NB + b + 1))
                    for t in range(TB):
                        for c in range(2):
                            mm = pe.transpose(ps[:, 4 + 2 * b + c, t * P:(t + 1) * P],
                                              u[:, b * TB + t, c * P:(c + 1) * P], ident)
                    mm.then_inc(tr_ps, 1)

                pe.wait_ge(gn_rhs, at(gn_rhs, img, 1))
                pe.wait_ge(y_used, at(y_used, img, 0))
                pe.matmul(ps[0:CC, 7, 0:2], group, gn_s[:, :], start=True, stop=True)\
                  .then_inc(gn_ps, 1)
                pe.wait_ge(gn_rhs, at(gn_rhs, img, 2))
                pe.matmul(ps[0:CC, 7, 2:4], group, gn_v[:, :], start=True, stop=True)\
                  .then_inc(gn_ps, 1)

                pe.wait_ge(xs_ready, at(xs_ready, img, 2))
                pe.wait_ge(h_act, at(h_act, img, 0))
                for b in range(NB):
                    for m in range(2):
                        for n, (w, c) in enumerate(((wc_h, 0), (wc_l, 0), (wc_h, 1), (wc_l, 1))):
                            mm = pe.matmul(ps[0:CC, 2 * b + m, :], w[0:CC, c, m * CC:(m + 1) * CC],
                                           xs[0:CC, c, b * QB:(b + 1) * QB], start=(n == 0), stop=(n == 3))
                        mm.then_inc(q_ps, 1)
                for t in range(NT):
                    if t >= 4:
                        pe.wait_ge(kv_relu, at(kv_relu, img, t - 3))
                    for n, (w, c) in enumerate(((wc_h, 0), (wc_l, 0), (wc_h, 1), (wc_l, 1))):
                        rows = CC + 1 if c == 0 else CC
                        mm = pe.matmul(ps[:, 4 + t % 4, 0:2 * C], xs[0:rows, c, t * P:(t + 1) * P],
                                       w[0:rows, c, C:3 * C], start=(n == 0), stop=(n == 3))
                    mm.then_inc(kv_ps, 1)
                pe.wait_ge(kv_int, at(kv_int, img, NT // 2))
                pe.wait_ge(q_relu, at(q_relu, img, 1))
                for m in range(2):
                    for t in range(NT):
                        mm = pe.matmul(ps[0:CC, 0, m * CC:(m + 1) * CC], kvi[:, t, m * CC:(m + 1) * CC],
                                       kvi[:, t, C + m * CC:C + (m + 1) * CC],
                                       start=(t == 0), stop=(t == NT - 1))
                mm.then_inc(kvm_ps, 1)
                pe.wait_ge(kv_split, at(kv_split, img, 1))
                pe.wait_ge(kv_relu, at(kv_relu, img, NT))
                for b in range(NB):
                    pe.wait_ge(q_int, at(q_int, img, b + 1))
                    for m in range(2):
                        for n, w in enumerate((kv_h, kv_l)):
                            mm = pe.matmul(ps[0:CC, 4 + 2 * b + m, :], w[:, m, :],
                                           qi[:, m, b * QB:(b + 1) * QB], start=(n == 0), stop=(n == 1))
                    mm.then_inc(at_ps, 1)
                pe.wait_ge(q_relu, at(q_relu, img, 2 * NB))
                for t in range(NT):
                    pe.wait_ge(a_int, at(a_int, img, t // TB + 1))
                    for n, (w, c) in enumerate(((wc_h, 0), (wc_l, 0), (wc_h, 1), (wc_l, 1))):
                        rows = CC + 1 if c == 0 else CC
                        mm = pe.matmul(ps[:, t // 2, (t % 2) * C:(t % 2 + 1) * C],
                                       ai[0:rows, c, t * P:(t + 1) * P], w[0:rows, c, 3 * C:4 * C],
                                       start=(n == 0), stop=(n == 3))
                    if t % 2:
                        mm.then_inc(p_ps, 1)

                pe.wait_ge(stage_lo, len(pieces))
                for b in range(NB):
                    transpose_block(0, b)
                for b in range(NB):
                    pe.wait_ge(ul_done, at(ul_done, img, b + 1))
                    for j in range(4):
                        if b:
                            pe.wait_ge(qk_lo, at(qk_lo, img, j + 1))
                        col = (COL_Q, COL_K)[j // 2] + (j % 2) * P
                        width = P if j % 2 == 0 else TAIL
                        project(ps[0:width, j, :], slice(col, col + width),
                                slice(b * QB, (b + 1) * QB), False).then_inc(qk_ps, 1)
                for t in range(NT):
                    mm = project(ps[:, 4 + t // 2, (t % 2) * C:(t % 2 + 1) * C],
                                 slice(COL_V, COL_V + C), slice(t * P, (t + 1) * P), True)
                    if t % 2:
                        mm.then_inc(v_ps, 1)

                def maximum_rows(b):
                    pe.wait_ge(m_split, at(m_split, img, b + 1))
                    for t in range(TB):
                        mm = pe.matmul(ps[0:2 * HEADS, 7, t * P:(t + 1) * P],
                                       m16[:, b * TB + t, :, :].rearrange("p h two -> p (h two)"),
                                       ident16[:, :], start=True, stop=True)
                    mm.then_inc(mrow_ps, 1)

                pe.wait_ge(heads_in, at(heads_in, img, whole(heads_in)))
                for i, (b, t, half, pair) in enumerate(M_ITEMS):
                    if i >= 2:
                        pe.wait_ge(m_used, at(m_used, img, i - 1))
                    diagonal = half == b
                    width = (t % TB + 1) * P if diagonal else QB
                    for a in range(2):
                        h = 2 * pair + a
                        dst = ps[:, 2 * (i % 2) + a, 0:width]
                        mm = pe.matmul(dst, q4[0:3 * D, h, t * P:(t + 1) * P],
                                       k4[0:3 * D, h, half * QB:half * QB + width],
                                       start=True, stop=not diagonal)
                        if diagonal:
                            mm = pe.matmul(ps[:, 2 * (i % 2) + a, width - P:width], identb[:, :],
                                           mask_qk[:, :], start=False, stop=True)
                    mm.then_inc(m_ps, 1)
                    if b == 1 and i == NM // 2:
                        pe.wait_ge(v_lo, at(v_lo, img, NT // 2))
                        maximum_rows(0)

                def scores(j):
                    b, pair, kc = E_ITEMS[j]
                    if j < 2:
                        pe.wait_ge(m_used, at(m_used, img, NM))
                    else:
                        pe.wait_ge(e_done, at(e_done, img, j - 1))
                    if pair == 0 and kc == 0:
                        pe.wait_ge(mrow_in[b], at(mrow_in[b], img, whole(mrow_in[b])))
                    q0 = max(0, kc - b * TB) * P
                    for a in range(2):
                        h = 2 * pair + a
                        diagonal = kc >= b * TB
                        mm = pe.matmul(ps[:, 2 * (j % 2) + a, q0:QB], k4[:, h, kc * P:(kc + 1) * P],
                                       q4[:, h, b * QB + q0:(b + 1) * QB], start=True, stop=not diagonal)
                        if diagonal:
                            mm = pe.matmul(ps[:, 2 * (j % 2) + a, q0:q0 + P], identb[:, :],
                                           mask_kq[:, :], start=False, stop=True)
                    mm.then_inc(e_ps, 1)

                def weigh(j):
                    b, pair, kc = E_ITEMS[j]
                    run = b * PAIRS + pair
                    bank = 4 + run % 3
                    q0 = max(0, kc - b * TB) * P
                    last = kc == (b + 1) * TB - 1
                    if kc == 0 and run >= 3:
                        pe.wait_ge(o_done, at(o_done, img, run - 2))
                    pe.wait_ge(p_hi, at(p_hi, img, j + 1))
                    if j % 2:
                        pe.wait_ge(p_lo_pool, at(p_lo_pool, img, j // 2 + 1))
                    else:
                        pe.wait_ge(p_lo_dve, at(p_lo_dve, img, j // 2 + 1))
                    s = j % N_P16
                    for n, (probs, low_v) in enumerate(((p_h, False), (p_l, False), (p_h, True))):
                        for a in range(2):
                            h = 2 * pair + a
                            v = (v_l if low_v else v_h)[:, kc, h * D:(h + 1) * D]
                            mm = pe.matmul(ps[a * D:(a + 1) * D, bank, q0:QB], v, probs[:, s, a, q0:QB],
                                           start=(kc == 0 and n == 0), stop=(last and n == 2))
                        if not low_v:
                            for a in range(2):
                                pe.matmul(ps[(2 + a) * D:(3 + a) * D, bank, q0:QB], ones16[:, 0:D],
                                          probs[:, s, a, q0:QB], start=(kc == 0 and n == 0),
                                          stop=(last and n == 1))
                    mm.then_inc(pv_done, 1)

                for j in range(NE + PV_LAG):
                    if j < NE:
                        scores(j)
                    if j == 2:
                        maximum_rows(1)
                    if j >= PV_LAG:
                        weigh(j - PV_LAG)

                pe.wait_ge(e_done, at(e_done, img, NE))
                pe.wait_ge(o_hi, at(o_hi, img, NB * PAIRS))
                pe.wait_ge(o_lo, at(o_lo, img, NB * PAIRS))
                A, BB = CHUNKS, CHUNKS + 1
                for t in range(NT):
                    tok = slice(t * P, (t + 1) * P)
                    terms = ((o_h[:, 0, tok], wout_h[:, A, :]), (o_h[:, 0, tok], wout_l[:, A, :]),
                             (o_l[:, 0, tok], wout_h[:, A, :]),
                             (o_h[0:TAIL + 1, 1, tok], wout_h[0:TAIL + 1, BB, :]),
                             (o_h[0:TAIL + 1, 1, tok], wout_l[0:TAIL + 1, BB, :]),
                             (o_l[0:TAIL + 1, 1, tok], wout_h[0:TAIL + 1, BB, :]))
                    for n, (lhs, rhs) in enumerate(terms):
                        mm = pe.matmul(ps[:, t // 2, (t % 2) * C:(t % 2 + 1) * C], lhs, rhs,
                                       start=(n == 0), stop=(n == 5))
                    if t % 2:
                        mm.then_inc(wo_ps, 1)

                pe.wait_ge(o_done, at(o_done, img, NB * PAIRS))
                for b in range(NB):
                    transpose_block(1, b)
                for b in range(NB):
                    pe.wait_ge(ul_done, at(ul_done, img, NB + b + 1))
                for t in range(NT):
                    mm = project(ps[:, 0, t * EXPERTS:(t + 1) * EXPERTS],
                                 slice(COL_GATE, COL_GATE + EXPERTS), slice(t * P, (t + 1) * P), True)
                mm.then_inc(gate_ps, 1)

                def hidden(i):
                    b, n = divmod(i, CHUNKS)
                    if i == 0:
                        pe.wait_ge(gate_used, at(gate_used, img, 1))
                    if i >= 4:
                        pe.wait_ge(h_act, at(h_act, img, i - 3))
                    col = COL_W1 + n * P
                    project(ps[:, i % 4, :], slice(col, col + P), slice(b * QB, (b + 1) * QB), False)\
                        .then_inc(h_ps, 1)

                def expert_out(i):
                    b, n = divmod(i, CHUNKS)
                    e, k = divmod(n, HC)
                    y = b * EXPERTS + e
                    bank = 4 + 2 * (y % 2)
                    if k == 0 and y >= 2:
                        pe.wait_ge(y_used, at(y_used, img, y - 1))
                    pe.wait_ge(h_hi, at(h_hi, img, i + 1))
                    pe.wait_ge(h_lo, at(h_lo, img, i + 1))
                    s = i % N_H
                    for t in range(TB):
                        dst = ps[:, bank + t // 2, (t % 2) * C:(t % 2 + 1) * C]
                        tok = slice(t * P, (t + 1) * P)
                        for m, (hid, w) in enumerate(((h_h, wout_h), (h_h, wout_l), (h_l, wout_h))):
                            mm = pe.matmul(dst, hid[:, s, tok], w[:, n, :],
                                           start=(k == 0 and m == 0 and t % 2 == 0), stop=False,
                                           skip_group_check=True)
                        if k == HC - 1:
                            mm = pe.matmul(dst, b2_ones[:, :], b2_sb[:, e * C:(e + 1) * C],
                                           start=False, stop=True, skip_group_check=True)
                    mm.then_inc(f2_done, 1)

                for i in range(NB * CHUNKS + F_LAG):
                    if i < NB * CHUNKS:
                        hidden(i)
                    if i >= F_LAG:
                        expert_out(i - F_LAG)

        @block.scalar
        def _(act):
            for n, (kind, c0, w) in enumerate(pieces):
                act.wait_ge(stage_in[n % 2], 16 * (n // 2 + 1))
                src = stage[:, n % 2, 0:w]
                dst = {"head": win_h, "tail": win_t, "out": wout_h_flat}[kind][:, c0:c0 + w]
                act.activation(dst, src, ACT.Copy, scale=W_SCALE).then_inc(stage_hi, 1)
            act.wait_ge(consts_ready, 1)

            with act.Fori(0, B) as img:
                act.wait_ge(gn_ready, at(gn_ready, img, 1))
                tx = tmp[0:CC, 0:2 * N].rearrange("p (c n) -> p c n", c=2)
                for c in range(2):
                    act.activation(tx[:, c, :], xc[:, c, :], ACT.Relu, scale=rstd[0:CC, c:c + 1],
                                   bias=gn_b[:, c:c + 1]).then_inc(x_relu, 1)
                for i in range(2 * NB):
                    b, m = divmod(i, 2)
                    act.wait_ge(q_ps, at(q_ps, img, i + 1))
                    act.activation(tx[:, m, b * QB:(b + 1) * QB], ps[0:CC, i, :], ACT.Relu,
                                   scale=q_sb[:, m, 0:1], bias=q_sb[:, m, 1:2]).then_inc(q_relu, 1)
                act.wait_ge(q_int, at(q_int, img, NB))
                for t in range(NT):
                    act.wait_ge(kv_ps, at(kv_ps, img, t + 1))
                    act.activation(tmp[:, t * 2 * C:(t + 1) * 2 * C], ps[:, 4 + t % 4, 0:2 * C],
                                   ACT.Relu, scale=1 / SPIKE_SCALE).then_inc(kv_relu, 1)

                def high_of_block(k, b):
                    act.wait_ge(tr_ps, at(tr_ps, img, k * NB + b + 1))
                    act.activation(uh[:, :, b * QB:(b + 1) * QB], ps[:, 4 + 2 * b:6 + 2 * b, :],
                                   ACT.Copy, scale=U_SCALE).then_inc(uh_done, 1)

                for b in range(NB):
                    high_of_block(0, b)
                for i in range(4 * NB):
                    b, j = divmod(i, 4)
                    width = P if j % 2 == 0 else TAIL
                    act.wait_ge(qk_ps, at(qk_ps, img, i + 1))
                    act.activation(qk_h[0:width, j, b * QB:(b + 1) * QB], ps[0:width, j, :], ACT.Copy,
                                   scale=A_SCALE / (U_SCALE * W_SCALE)).then_inc(qk_hi, 1)
                for t in range(0, NT, 2):
                    act.wait_ge(v_ps, at(v_ps, img, t // 2 + 1))
                    act.activation(v_h[:, t:t + 2, :],
                                   ps[:, 4 + t // 2, 0:2 * C].rearrange("p (t c) -> p t c", t=2), ACT.Copy,
                                   scale=A_SCALE / (U_SCALE * W_SCALE)).then_inc(v_hi, 1)

                def rows_of_maxima(b):
                    act.wait_ge(mrow_ps, at(mrow_ps, img, b + 1))
                    act.activation(mrow[:, b * QB:(b + 1) * QB], ps[0:2 * HEADS, 7, :], ACT.Copy)\
                       .then_inc(mrow_done, 1)

                def high_of_output(run):
                    b, pair = divmod(run, PAIRS)
                    act.wait_ge(o_done, at(o_done, img, run + 1))
                    rows = slice(2 * D * (pair % 2), 2 * D * (pair % 2) + 2 * D)
                    act.activation(o_h[rows, pair // 2, b * QB:(b + 1) * QB],
                                   o32[rows, pair // 2, b * QB:(b + 1) * QB], ACT.Copy)\
                       .then_inc(o_hi, 1)

                rows_of_maxima(0)
                ends = run_ends()
                run = 0
                for j, (b, pair, kc) in enumerate(E_ITEMS):
                    act.wait_ge(e_ps, at(e_ps, img, j + 1))
                    if j >= N_P32:
                        act.wait_ge(p_hi, at(p_hi, img, j - N_P32 + 1))
                        i = j - N_P32
                        if i % 2:
                            act.wait_ge(p_lo_pool, at(p_lo_pool, img, i // 2 + 1))
                        else:
                            act.wait_ge(p_lo_dve, at(p_lo_dve, img, i // 2 + 1))
                    q0 = max(0, kc - b * TB) * P
                    act.activation(p32[:, j % N_P32, :, q0:QB], ps[:, 2 * (j % 2):2 * (j % 2) + 2, q0:QB],
                                   ACT.Exp, bias=exp_bias[:, :],
                                   scale=float(1 / (A_SCALE * A_SCALE * np.sqrt(D)))).then_inc(e_done, 1)
                    if j == 2:
                        rows_of_maxima(1)
                    if run < len(ends) and j == ends[run] + 4:
                        high_of_output(run)
                        run += 1
                for run in range(run, len(ends)):
                    high_of_output(run)

                for b in range(NB):
                    high_of_block(1, b)
                act.wait_ge(gate_sub, at(gate_sub, img, 1))
                act.activation(gex[:, :, :], gsc[:, :, :], ACT.Exp).then_inc(gate_exp, 1)
                for i in range(NB * CHUNKS):
                    n = i % CHUNKS
                    act.wait_ge(h_ps, at(h_ps, img, i + 1))
                    if i >= N_H:
                        act.wait_ge(h_lo, at(h_lo, img, i - N_H + 1))
                    act.activation(h32[:, i % N_H, :], ps[:, i % 4, :], ACT.Gelu,
                                   scale=1 / (U_SCALE * W_SCALE), bias=b1_sb[:, n:n + 1])\
                       .then_inc(h_act, 1)

        @block.gpsimd
        def _(pool):
            fills = ((minus_half[:, :], -0.5), (ones16[:, :], 1.0), (exp_bias[:, :], float(np.log(P_SCALE))),
                     (xs[CC:CC + 1, :, :], 1.0), (ai[CC:CC + 1, :, :], 1.0),
                     (k4[3 * D:3 * D + 2, :, :], M_SCALE), (o_h[TAIL:TAIL + 1, 1, :], A_SCALE),
                     (o_l[TAIL:TAIL + 1, 1, :], 0.0), (b2_ones[:, :], A_SCALE))
            for n, (dst, value) in enumerate(fills):
                nc.gpsimd.memset(dst, value).then_inc(setup_pool, 1)
                pool.wait_ge(setup_pool, n + 1)
            pool.wait_ge(setup_dve, 2)
            nc.gpsimd.tensor_tensor(bn_t[:, 1, :], bn_t[:, 0, :],
                                    minus_half[0:CC + 1, 0:1].broadcast_to([CC + 1, 3 * C]), ALU.pow)\
              .then_inc(setup_pool, 1)
            nc.gpsimd.tensor_tensor(bq_t[:, 1, :], bq_t[:, 0, :], minus_half[0:CC, 0:2], ALU.pow)\
              .then_inc(setup_pool, 1)

            with pool.Fori(0, B) as img:
                def rsqrt(k, rows, cols):
                    pool.wait_ge(var_ready, at(var_ready, img, k + 1))
                    nc.gpsimd.tensor_tensor(rs0[0:rows, 0:cols], veps[0:rows, 0:cols],
                                            minus_half[0:rows, 0:cols], ALU.pow).then_inc(pow_done, 1)

                def low_of_output(run, halves):
                    b, pair = divmod(run, PAIRS)
                    pool.wait_ge(p_lo_pool, at(p_lo_pool, img, halves))
                    if run:
                        pool.wait_ge(o_lo, at(o_lo, img, run))
                    pool.wait_ge(o_hi, at(o_hi, img, run + 1))
                    rows = slice(2 * D * (pair % 2), 2 * D * (pair % 2) + 2 * D)
                    where = (rows, pair // 2, slice(b * QB, (b + 1) * QB))
                    nc.gpsimd.tensor_tensor(o_l[where], o32[where], o_h[where], ALU.subtract).then_inc(o_lo, 1)

                rsqrt(0, CC, 2)
                rsqrt(1, P, NT)
                ends = run_ends()
                run = 0
                for j in range(1, NE, 2):
                    b, pair, kc = E_ITEMS[j]
                    q0 = max(0, kc - b * TB) * P
                    pool.wait_ge(p_hi, at(p_hi, img, j + 1))
                    if j >= N_P16:
                        pool.wait_ge(pv_done, at(pv_done, img, j - N_P16 + 1))
                    nc.gpsimd.tensor_tensor(p_l[:, j % N_P16, :, q0:QB], p32[:, j % N_P32, :, q0:QB],
                                            p_h[:, j % N_P16, :, q0:QB], ALU.subtract)\
                      .then_inc(p_lo_pool, 1)
                    if run < len(ends) and j >= ends[run] + 6:
                        low_of_output(run, (j + 1) // 2)
                        run += 1
                        pool.wait_ge(o_lo, at(o_lo, img, run))
                for run in range(run, len(ends)):
                    low_of_output(run, NE // 2)
                pool.wait_ge(o_lo, at(o_lo, img, len(ends)))
                rsqrt(2, P, NT)
                for b in range(NB):
                    pool.wait_ge(y_used, at(y_used, img, (b + 1) * EXPERTS))
                    pool.dma_start(out[img, :, b * TB:(b + 1) * TB, :], acc[:, b * TB:(b + 1) * TB, :])\
                        .then_inc(stored, 16)
            pool.wait_ge(stored, B * whole(stored))

        @block.vector
        def _(dve):
            V = nc.vector
            dve.wait_ge(small_in, 16 * n_small)
            setup = Count()

            V.tensor_scalar(bn_t[:, 0, :], bn_st[:, 3, :], 1e-5, None, ALU.add).then_inc(setup_dve, 1)
            dve.wait_ge(setup_dve, setup.more(1))
            V.tensor_scalar(bq_t[:, 0, :], bq_st[:, :, 3], 1e-5, None, ALU.add).then_inc(setup_dve, 1)
            dve.wait_ge(setup_dve, setup.more(1))
            V.tensor_copy(ident16[:, :], ident).then_inc(setup_dve, 1)
            dve.wait_ge(setup_dve, setup.more(1))
            V.tensor_copy(identb[:, :], ident).then_inc(setup_dve, 1)
            dve.wait_ge(setup_dve, setup.more(1))
            V.tensor_scalar(mask_kq[:, :], kst[:, K_MKQ:K_MKQ + P], MASKED, None, ALU.mult).then_inc(setup_dve, 1)
            dve.wait_ge(setup_dve, setup.more(1))
            V.tensor_scalar(mask_qk[:, :], kst[:, K_MQK:K_MQK + P], MASKED, None, ALU.mult).then_inc(setup_dve, 1)
            dve.wait_ge(setup_dve, setup.more(1))
            V.tensor_scalar(b2_t[:, :], b2_st[:, :], W_SCALE, None, ALU.mult).then_inc(setup_dve, 1)
            dve.wait_ge(setup_dve, setup.more(1))
            V.tensor_scalar(b2_st[:, :], b2_st[:, :], W_SCALE, None, ALU.mult).then_inc(setup_dve, 1)
            dve.wait_ge(setup_dve, setup.more(1))
            V.tensor_scalar(b2_t[:, :], b2_t[:, :], kst[0:2, K_ROW:K_ROW + 1], None, ALU.mult).then_inc(setup_dve, 1)
            dve.wait_ge(setup_dve, setup.more(1))
            V.tensor_tensor(b2_sb[:, :], b2_st[:, :], b2_t[:, :], ALU.subtract).then_inc(setup_dve, 1)
            dve.wait_ge(setup_dve, setup.more(1))

            def newton(y, v, a, into):
                V.tensor_tensor(a, y, y, ALU.mult).then_inc(setup_dve, 1)
                dve.wait_ge(setup_dve, setup.more(1))
                V.scalar_tensor_tensor(out=a, in0=a, scalar=-0.5, in1=v, op0=ALU.mult, op1=ALU.mult).then_inc(setup_dve, 1)
                dve.wait_ge(setup_dve, setup.more(1))
                V.scalar_tensor_tensor(out=into, in0=a, scalar=1.5, in1=y, op0=ALU.add, op1=ALU.mult).then_inc(setup_dve, 1)
                dve.wait_ge(setup_dve, setup.more(1))

            dve.wait_ge(setup_pool, 11)
            newton(bq_t[:, 1, :], bq_t[:, 0, :], bq_t[:, 2, :], bq_t[:, 1, :])
            V.tensor_tensor(bq_t[:, 2, :], bq_t[:, 1, :], bq_st[:, :, 0], ALU.mult).then_inc(setup_dve, 1)
            dve.wait_ge(setup_dve, setup.more(1))
            V.tensor_tensor(bq_t[:, 3, :], bq_t[:, 2, :], bq_st[:, :, 2], ALU.mult).then_inc(setup_dve, 1)
            dve.wait_ge(setup_dve, setup.more(1))
            V.tensor_tensor(q_sb[:, :, 1], bq_st[:, :, 1], bq_t[:, 3, :], ALU.subtract).then_inc(setup_dve, 1)
            dve.wait_ge(setup_dve, setup.more(1))
            V.tensor_scalar(q_sb[:, :, 0], bq_t[:, 2, :], 1 / SPIKE_SCALE, None, ALU.mult).then_inc(setup_dve, 1)
            dve.wait_ge(setup_dve, setup.more(1))
            newton(bn_t[:, 1, :], bn_t[:, 0, :], bn_t[:, 2, :], bn_t[:, 1, :])
            V.tensor_tensor(bn_t[:, 0, :], bn_t[:, 1, :], bn_st[:, 0, :], ALU.mult).then_inc(setup_dve, 1)
            dve.wait_ge(setup_dve, setup.more(1))
            V.tensor_tensor(bn_t[:, 1, :], bn_t[:, 0, :], bn_st[:, 2, :], ALU.mult).then_inc(setup_dve, 1)
            dve.wait_ge(setup_dve, setup.more(1))
            V.tensor_tensor(bn_t[:, 2, :], bn_st[:, 1, :], bn_t[:, 1, :], ALU.subtract).then_inc(setup_dve, 1)
            dve.wait_ge(setup_dve, setup.more(1))
            wc = tmp[0:CC + 1, 0:2 * NCV].rearrange("p (c n) -> p c n", c=2)
            for c in range(2):
                V.tensor_scalar(wc[0:CC, c, 0:C], wc[0:CC, c, 0:C], W_SCALE, None, ALU.mult).then_inc(setup_dve, 1)
                dve.wait_ge(setup_dve, setup.more(1))
                V.scalar_tensor_tensor(out=wc[0:CC, c, C:], in0=wc[0:CC, c, C:], scalar=W_SCALE,
                                            in1=bn_t[0:CC, 0, :], op0=ALU.mult, op1=ALU.mult).then_inc(setup_dve, 1)
                dve.wait_ge(setup_dve, setup.more(1))
            V.tensor_scalar(wc[CC:CC + 1, 0, C:], bn_t[CC:CC + 1, 2, :], SPIKE_SCALE, None, ALU.mult).then_inc(setup_dve, 1)
            dve.wait_ge(setup_dve, setup.more(1))
            V.tensor_copy(wc_h[:, :, :], wc).then_inc(setup_dve, 1)
            dve.wait_ge(setup_dve, setup.more(1))
            V.tensor_tensor(wc_l[:, :, :], wc, wc_h[:, :, :], ALU.subtract).then_inc(setup_dve, 1)
            dve.wait_ge(setup_dve, setup.more(1))
            V.memset(rstd[:, :], 0.0).then_inc(consts_ready, 1)
            for n, (kind, c0, w) in enumerate(pieces):
                dve.wait_ge(stage_hi, n + 1)
                rows = slice(TAIL, P) if kind == "tail" else slice(0, P)
                hi = {"head": win_h, "tail": win_t, "out": wout_h_flat}[kind][rows, c0:c0 + w]
                lo = {"head": win_l, "tail": win_t, "out": wout_l_flat}[kind][rows, c0:c0 + w]
                V.scalar_tensor_tensor(out=lo, in0=stage[rows, n % 2, 0:w], scalar=W_SCALE, in1=hi,
                                       op0=ALU.mult, op1=ALU.subtract).then_inc(stage_lo, 1)

            with dve.Fori(0, B) as img:
                steps = Count()

                def rsqrt_refined(k, rows, cols):
                    v, y = veps[0:rows, 0:cols], rs0[0:rows, 0:cols]
                    a = rs1[0:rows, 0:cols]
                    dve.wait_ge(pow_done, at(pow_done, img, k + 1))
                    V.tensor_tensor(a, y, y, ALU.mult).then_inc(dve_step, 1)
                    dve.wait_ge(dve_step, at(dve_step, img, steps.more(1)))
                    V.scalar_tensor_tensor(out=a, in0=a, scalar=-0.5, in1=v, op0=ALU.mult, op1=ALU.mult).then_inc(dve_step, 1)
                    dve.wait_ge(dve_step, at(dve_step, img, steps.more(1)))
                    V.scalar_tensor_tensor(out=rstd[0:rows, 0:cols], in0=a, scalar=1.5, in1=y,
                                                op0=ALU.add, op1=ALU.mult).then_inc(dve_step, 1)
                    dve.wait_ge(dve_step, at(dve_step, img, steps.more(1)))

                dve.wait_ge(x_ch_in, at(x_ch_in, img, 16))
                for c in range(2):
                    for s in range(2):
                        V.bn_stats(gn_st[:, c, s, :], xc[:, c, s * 512:(s + 1) * 512]).then_inc(dve_step, 1)
                dve.wait_ge(dve_step, at(dve_step, img, steps.more(4)))
                part = gn_st[:, :, :, :].rearrange("p c s (o k) -> p c (s o) k", o=2)
                V.tensor_reduce(gn_s[:, :], part[:, :, :, 1], AX.X, ALU.add).then_inc(gn_rhs, 1)
                dve.wait_ge(gn_ps, at(gn_ps, img, 1))
                V.tensor_scalar(gn_m[:, :], ps[0:CC, 7, 0:2], 1 / 4, None, ALU.mult).then_inc(dve_step, 1)
                dve.wait_ge(dve_step, at(dve_step, img, steps.more(1)))
                V.tensor_tensor(gn_d[:, :, :], part[:, :, :, 1],
                                     gn_m[:, :, None].broadcast_to([CC, 2, 4]), ALU.subtract).then_inc(dve_step, 1)
                dve.wait_ge(dve_step, at(dve_step, img, steps.more(1)))
                V.tensor_tensor(gn_d[:, :, :], gn_d[:, :, :], gn_d[:, :, :], ALU.mult).then_inc(dve_step, 1)
                dve.wait_ge(dve_step, at(dve_step, img, steps.more(1)))
                V.scalar_tensor_tensor(out=gn_d[:, :, :], in0=part[:, :, :, 2], scalar=4 / N,
                                            in1=gn_d[:, :, :], op0=ALU.mult, op1=ALU.add).then_inc(dve_step, 1)
                dve.wait_ge(dve_step, at(dve_step, img, steps.more(1)))
                V.tensor_reduce(gn_v[:, :], gn_d[:, :, :], AX.X, ALU.add).then_inc(gn_rhs, 1)
                dve.wait_ge(gn_ps, at(gn_ps, img, 2))
                V.tensor_scalar(veps[0:CC, 0:2], ps[0:CC, 7, 2:4], 1 / 4, 1e-5, ALU.mult, ALU.add)\
                 .then_inc(var_ready, 1)
                rsqrt_refined(0, CC, 2)
                V.scalar_tensor_tensor(out=gn_b[:, :], in0=gn_m[:, :], scalar=-1.0, in1=rstd[0:CC, 0:2],
                                       op0=ALU.mult, op1=ALU.mult).then_inc(gn_ready, 1)

                tx = tmp[0:CC, 0:2 * N].rearrange("p (c n) -> p c n", c=2)

                def spike(dst, t, signal):
                    V.tensor_scalar(t, t, 4.0, MAGIC, ALU.min, ALU.add).then_inc(dve_step, 1)
                    dve.wait_ge(dve_step, at(dve_step, img, steps.more(1)))
                    V.tensor_scalar(dst, t, MAGIC, None, ALU.subtract).then_inc(signal, 1)

                for c in range(2):
                    dve.wait_ge(x_relu, at(x_relu, img, c + 1))
                    spike(xs[0:CC, c, :], tx[:, c, :], xs_ready)
                for b in range(NB):
                    dve.wait_ge(q_relu, at(q_relu, img, 2 * b + 2))
                    spike(qi[:, :, b * QB:(b + 1) * QB], tx[:, :, b * QB:(b + 1) * QB], q_int)
                for i in range(NT // 2):
                    dve.wait_ge(kv_relu, at(kv_relu, img, 2 * i + 2))
                    spike(kvi[:, 2 * i:2 * i + 2, :].rearrange("p t c -> p (t c)"),
                          tmp[:, i * 4 * C:(i + 1) * 4 * C], kv_int)
                dve.wait_ge(kvm_ps, at(kvm_ps, img, 1))
                V.tensor_tensor(kv32[:, :, :], ps[0:CC, 0, 0:C].rearrange("p (m e) -> p m e", m=2),
                                     block_diag[:, None, :].broadcast_to([CC, 2, CC]), ALU.mult).then_inc(dve_step, 1)
                dve.wait_ge(dve_step, at(dve_step, img, steps.more(1)))
                V.tensor_copy(kv_h[:, :, :], kv32[:, :, :]).then_inc(dve_step, 1)
                dve.wait_ge(dve_step, at(dve_step, img, steps.more(1)))
                V.tensor_tensor(kv_l[:, :, :], kv32[:, :, :], kv_h[:, :, :], ALU.subtract)\
                 .then_inc(kv_split, 1)
                for b in range(NB):
                    dve.wait_ge(at_ps, at(at_ps, img, b + 1))
                    V.tensor_scalar(tx[:, :, b * QB:(b + 1) * QB], ps[0:CC, 4 + 2 * b:6 + 2 * b, :],
                                         SPIKE_ATTN, 4.0, ALU.mult, ALU.min).then_inc(dve_step, 1)
                    dve.wait_ge(dve_step, at(dve_step, img, steps.more(1)))
                    V.tensor_scalar(ai[0:CC, :, b * QB:(b + 1) * QB], tx[:, :, b * QB:(b + 1) * QB],
                                    MAGIC, MAGIC, ALU.add, ALU.subtract).then_inc(a_int, 1)
                dve.wait_ge(x_tok_in, at(x_tok_in, img, 16))
                dve.wait_ge(stored, at(stored, img, 0))
                for i in range(NT // 2):
                    dve.wait_ge(p_ps, at(p_ps, img, i + 1))
                    ins = V.scalar_tensor_tensor(
                        out=acc[:, 2 * i:2 * i + 2, :],
                        in0=ps[:, i, 0:2 * C].rearrange("p (t c) -> p t c", t=2), scalar=1 / SPIKE_SCALE,
                        in1=xt[:, 2 * i:2 * i + 2, :], op0=ALU.mult, op1=ALU.add)
                ins.then_inc(xt_used, 1)
                dve.wait_ge(xt_used, at(xt_used, img, 1))

                def layer_norm(k):
                    for t in range(NT):
                        V.bn_stats(ln_st[:, t, :], acc[:, t, :]).then_inc(dve_step, 1)
                    dve.wait_ge(dve_step, at(dve_step, img, steps.more(NT)))
                    even, odd = ln_st[:, :, 0:3], ln_st[:, :, 3:6]
                    V.tensor_tensor(ln_s[:, 0, :], even[:, :, 1], odd[:, :, 1], ALU.add).then_inc(dve_step, 1)
                    V.tensor_tensor(ln_s[:, 1, :], even[:, :, 1], odd[:, :, 1], ALU.subtract).then_inc(dve_step, 1)
                    V.tensor_tensor(ln_s[:, 2, :], even[:, :, 2], odd[:, :, 2], ALU.add).then_inc(dve_step, 1)
                    dve.wait_ge(dve_step, at(dve_step, img, steps.more(3)))
                    V.tensor_scalar(ln_m[:, :], ln_s[:, 0, :], 1 / 2, None, ALU.mult).then_inc(dve_step, 1)
                    V.scalar_tensor_tensor(out=ln_s[:, 1, :], in0=ln_s[:, 1, :], scalar=1 / 4,
                                                in1=ln_s[:, 1, :], op0=ALU.mult, op1=ALU.mult).then_inc(dve_step, 1)
                    V.tensor_scalar(ln_s[:, 2, :], ln_s[:, 2, :], 1 / C, 1e-5, ALU.mult, ALU.add).then_inc(dve_step, 1)
                    dve.wait_ge(dve_step, at(dve_step, img, steps.more(3)))
                    V.tensor_tensor(veps[:, :], ln_s[:, 1, :], ln_s[:, 2, :], ALU.add).then_inc(var_ready, 1)
                    rsqrt_refined(k + 1, P, NT)
                    for b in range(NB):
                        for t in range(b * TB, (b + 1) * TB):
                            V.tensor_scalar(u[:, t, 0:C], acc[:, t, :], ln_m[:, t:t + 1],
                                                 rstd[:, t:t + 1], ALU.subtract, ALU.mult).then_inc(dve_step, 1)
                        dve.wait_ge(dve_step, at(dve_step, img, steps.more(4)))
                        V.tensor_copy(u[:, b * TB:(b + 1) * TB, C:], u[:, b * TB:(b + 1) * TB, P:C])\
                         .then_inc(u_ready, 1)
                    for b in range(NB):
                        dve.wait_ge(uh_done, at(uh_done, img, k * NB + b + 1))
                        V.scalar_tensor_tensor(out=ul[:, :, b * QB:(b + 1) * QB],
                                               in0=ps[:, 4 + 2 * b:6 + 2 * b, :], scalar=U_SCALE,
                                               in1=uh[:, :, b * QB:(b + 1) * QB], op0=ALU.mult,
                                               op1=ALU.subtract).then_inc(ul_done, 1)

                layer_norm(0)
                for i in range(4 * NB):
                    b, j = divmod(i, 4)
                    width = P if j % 2 == 0 else TAIL
                    dve.wait_ge(qk_hi, at(qk_hi, img, i + 1))
                    V.scalar_tensor_tensor(out=qk_l[0:width, j, b * QB:(b + 1) * QB],
                                           in0=ps[0:width, j, :], scalar=A_SCALE / (U_SCALE * W_SCALE),
                                           in1=qk_h[0:width, j, b * QB:(b + 1) * QB], op0=ALU.mult,
                                           op1=ALU.subtract).then_inc(qk_lo, 1)
                for t in range(0, NT, 2):
                    dve.wait_ge(v_hi, at(v_hi, img, t // 2 + 1))
                    V.scalar_tensor_tensor(out=v_l[:, t:t + 2, :],
                                           in0=ps[:, 4 + t // 2, 0:2 * C].rearrange("p (t c) -> p t c", t=2),
                                           scalar=A_SCALE / (U_SCALE * W_SCALE), in1=v_h[:, t:t + 2, :],
                                           op0=ALU.mult, op1=ALU.subtract).then_inc(v_lo, 1)
                for i, (b, t, half, pair) in enumerate(M_ITEMS):
                    dve.wait_ge(m_ps, at(m_ps, img, i + 1))
                    width = (t % TB + 1) * P if half == b else QB
                    V.tensor_reduce(mx[:, half, t, 2 * pair:2 * pair + 2],
                                    ps[:, 2 * (i % 2):2 * (i % 2) + 2, 0:width], AX.X, ALU.max)\
                     .then_inc(m_used, 1)
                    if i + 1 in (NM // 3, NM):
                        dve.wait_ge(m_used, at(m_used, img, i + 1))
                        rows = slice(b * TB, (b + 1) * TB)
                        if b:
                            V.tensor_tensor(mx[:, 0, rows, :], mx[:, 0, rows, :], mx[:, 1, rows, :], ALU.max).then_inc(dve_step, 1)
                            dve.wait_ge(dve_step, at(dve_step, img, steps.more(1)))
                        V.tensor_scalar(m16[:, rows, :, 0], mx[:, 0, rows, :], -1 / M_SCALE, None, ALU.mult).then_inc(dve_step, 1)
                        dve.wait_ge(dve_step, at(dve_step, img, steps.more(1)))
                        V.scalar_tensor_tensor(out=m16[:, rows, :, 1], in0=mx[:, 0, rows, :],
                                               scalar=-1 / M_SCALE, in1=m16[:, rows, :, 0],
                                               op0=ALU.mult, op1=ALU.subtract).then_inc(m_split, 1)

                def normalize(run):
                    b, pair = divmod(run, PAIRS)
                    dve.wait_ge(pv_done, at(pv_done, img, run_ends()[run] + 1))
                    bank = 4 + run % 3
                    V.reciprocal(rden[:, :], ps[2 * D:4 * D, bank, :]).then_inc(dve_step, 1)
                    dve.wait_ge(dve_step, at(dve_step, img, steps.more(1)))
                    rows = slice(2 * D * (pair % 2), 2 * D * (pair % 2) + 2 * D)
                    V.tensor_tensor(o32[rows, pair // 2, b * QB:(b + 1) * QB], ps[0:2 * D, bank, :],
                                    rden[:, :], ALU.mult).then_inc(o_done, 1)

                ends = run_ends()
                run = 0
                for j, (b, pair, kc) in enumerate(E_ITEMS):
                    q0 = max(0, kc - b * TB) * P
                    dve.wait_ge(e_done, at(e_done, img, j + 1))
                    if j >= N_P16:
                        dve.wait_ge(pv_done, at(pv_done, img, j - N_P16 + 1))
                    V.tensor_copy(p_h[:, j % N_P16, :, q0:QB], p32[:, j % N_P32, :, q0:QB])\
                     .then_inc(p_hi, 1)
                    if j % 2 == 0:
                        dve.wait_ge(p_hi, at(p_hi, img, j + 1))
                        V.tensor_tensor(p_l[:, j % N_P16, :, q0:QB], p32[:, j % N_P32, :, q0:QB],
                                        p_h[:, j % N_P16, :, q0:QB], ALU.subtract).then_inc(p_lo_dve, 1)
                    if run < len(ends) and j == ends[run] + 3:
                        normalize(run)
                        run += 1
                for run in range(run, len(ends)):
                    normalize(run)
                for i in range(NT // 2):
                    dve.wait_ge(wo_ps, at(wo_ps, img, i + 1))
                    V.scalar_tensor_tensor(
                        out=acc[:, 2 * i:2 * i + 2, :],
                        in0=ps[:, i, 0:2 * C].rearrange("p (t c) -> p t c", t=2),
                        scalar=1 / (A_SCALE * W_SCALE), in1=acc[:, 2 * i:2 * i + 2, :],
                        op0=ALU.mult, op1=ALU.add).then_inc(dve_step, 1)
                dve.wait_ge(dve_step, at(dve_step, img, steps.more(4)))

                layer_norm(1)
                dve.wait_ge(gate_ps, at(gate_ps, img, 1))
                V.scalar_tensor_tensor(
                    out=gsc[:, :, :], in0=ps[:, 0, 0:NT * EXPERTS].rearrange("p (t e) -> p t e", t=NT),
                    scalar=1 / (U_SCALE * W_SCALE), in1=gb_sb[:, :, :], op0=ALU.mult, op1=ALU.add).then_inc(dve_step, 1)
                dve.wait_ge(dve_step, at(dve_step, img, steps.more(1)))
                V.tensor_reduce(gt1[:, :], gsc[:, :, :], AX.X, ALU.max).then_inc(gate_used, 1)
                dve.wait_ge(gate_used, at(gate_used, img, 1))
                each = [P, NT, EXPERTS]
                V.tensor_tensor(gsc[:, :, :], gsc[:, :, :], gt1[:, :, None].broadcast_to(each), ALU.subtract)\
                 .then_inc(gate_sub, 1)
                dve.wait_ge(gate_exp, at(gate_exp, img, 1))
                V.tensor_reduce(gt1[:, :], gex[:, :, :], AX.X, ALU.add).then_inc(dve_step, 1)
                dve.wait_ge(dve_step, at(dve_step, img, steps.more(1)))
                V.reciprocal(gt2[:, :], gt1[:, :]).then_inc(dve_step, 1)
                dve.wait_ge(dve_step, at(dve_step, img, steps.more(1)))
                V.tensor_tensor(gpr[:, :, :], gex[:, :, :], gt2[:, :, None].broadcast_to(each), ALU.mult).then_inc(dve_step, 1)
                dve.wait_ge(dve_step, at(dve_step, img, steps.more(1)))
                square = [P, NT, EXPERTS, EXPERTS]
                other = gpr[:, :, None, :].broadcast_to(square)
                own = gpr[:, :, :, None].broadcast_to(square)
                tie = kst[:, None, K_TIE:K_TIE + EXPERTS * EXPERTS].broadcast_to([P, NT, EXPERTS * EXPERTS])
                flat = "p t i j -> p t (i j)"
                V.tensor_tensor(gcmp[:, :, :, :], other, own, ALU.is_equal).then_inc(dve_step, 1)
                dve.wait_ge(dve_step, at(dve_step, img, steps.more(1)))
                V.tensor_tensor(gcmp[:, :, :, :].rearrange(flat), gcmp[:, :, :, :].rearrange(flat),
                                     tie, ALU.mult).then_inc(dve_step, 1)
                V.tensor_tensor(gcm2[:, :, :, :], other, own, ALU.is_gt).then_inc(dve_step, 1)
                dve.wait_ge(dve_step, at(dve_step, img, steps.more(2)))
                V.tensor_tensor(gcmp[:, :, :, :], gcmp[:, :, :, :], gcm2[:, :, :, :], ALU.add).then_inc(dve_step, 1)
                dve.wait_ge(dve_step, at(dve_step, img, steps.more(1)))
                V.tensor_reduce(gcnt[:, :, :], gcmp[:, :, :, :], AX.X, ALU.add).then_inc(dve_step, 1)
                dve.wait_ge(dve_step, at(dve_step, img, steps.more(1)))
                V.scalar_tensor_tensor(out=gpr[:, :, :], in0=gcnt[:, :, :], scalar=2.0,
                                            in1=gpr[:, :, :], op0=ALU.is_lt, op1=ALU.mult).then_inc(dve_step, 1)
                dve.wait_ge(dve_step, at(dve_step, img, steps.more(1)))
                V.tensor_reduce(gt1[:, :], gpr[:, :, :], AX.X, ALU.add).then_inc(dve_step, 1)
                dve.wait_ge(dve_step, at(dve_step, img, steps.more(1)))
                V.tensor_scalar(gt1[:, :], gt1[:, :], 1e-9, None, ALU.add).then_inc(dve_step, 1)
                dve.wait_ge(dve_step, at(dve_step, img, steps.more(1)))
                V.reciprocal(gt2[:, :], gt1[:, :]).then_inc(dve_step, 1)
                dve.wait_ge(dve_step, at(dve_step, img, steps.more(1)))
                V.scalar_tensor_tensor(out=gate[:, :, :], in0=gpr[:, :, :],
                                            scalar=1 / (A_SCALE * W_SCALE),
                                            in1=gt2[:, :, None].broadcast_to(each),
                                            op0=ALU.mult, op1=ALU.mult).then_inc(dve_step, 1)
                dve.wait_ge(dve_step, at(dve_step, img, steps.more(1)))

                def add_expert(y):
                    b, e = divmod(y, EXPERTS)
                    dve.wait_ge(f2_done, at(f2_done, img, (y + 1) * HC))
                    bank = 4 + 2 * (y % 2)
                    for t in range(TB):
                        n = b * TB + t
                        if y and t == 0:
                            dve.wait_ge(y_used, at(y_used, img, y))
                        ins = V.scalar_tensor_tensor(
                            out=acc[:, n, :], in0=ps[:, bank + t // 2, (t % 2) * C:(t % 2 + 1) * C],
                            scalar=gate[:, n, e:e + 1], in1=acc[:, n, :], op0=ALU.mult, op1=ALU.add)
                    ins.then_inc(y_used, 1)

                for i in range(NB * CHUNKS):
                    dve.wait_ge(h_act, at(h_act, img, i + 1))
                    if i >= N_H:
                        dve.wait_ge(f2_done, at(f2_done, img, i - N_H + 1))
                    s = i % N_H
                    V.tensor_scalar(h_h[:, s, :], h32[:, s, :], A_SCALE, None, ALU.mult)\
                     .then_inc(h_hi, 1)
                    dve.wait_ge(h_hi, at(h_hi, img, i + 1))
                    V.scalar_tensor_tensor(out=h_l[:, s, :], in0=h32[:, s, :], scalar=A_SCALE,
                                           in1=h_h[:, s, :], op0=ALU.mult, op1=ALU.subtract)\
                     .then_inc(h_lo, 1)
                    if i >= HC + 2 and (i - 3) % HC == HC - 1:
                        add_expert((i - 3) // HC)
                add_expert(NB * EXPERTS - 1)
                assert steps.n == DVE_STEPS, steps.n


def constants():
    k = np.zeros((P, K_COLS), np.float32)
    i = np.arange(P)
    k[:, K_ID:K_ID + P] = np.eye(P)
    k[:, K_MKQ:K_MKQ + P] = i[:, None] > i[None, :]
    k[:, K_MQK:K_MQK + P] = i[None, :] > i[:, None]
    c = np.arange(CC)
    per = C // GROUPS
    k[:CC, K_GRP:K_GRP + CC] = (c[:, None] // per == c[None, :] // per) / per
    hd = C // SPIKE_HEADS
    k[:CC, K_BLK:K_BLK + CC] = c[:, None] // hd == c[None, :] // hd
    k[:, K_ROW] = i
    e = np.arange(EXPERTS)
    k[:, K_TIE:] = (e[None, :] < e[:, None]).ravel()
    return k


def kernel(**inputs):
    import concourse.bacc as bacc
    from concourse.bass_utils import run_bass_kernel_spmd

    g = {k: np.asarray(v) for k, v in inputs.items()}
    x = g["x"].reshape(B, C, N)

    def halves(a):
        return a.reshape(2, CC, -1).transpose(1, 0, 2)

    conv = np.concatenate([g[f"L0_conv_{p}_w"].T for p in "qkvp"], axis=1)
    conv = np.concatenate([halves(conv), np.zeros((1, 2, 4 * C), np.float32)])
    rows = np.stack([np.concatenate([g[f"L0_conv_{p}_{what}"] for p in "kvp"])
                     for what in ("gamma", "beta", "mean", "var")])
    bn_q = halves(np.stack([g[f"L0_conv_q_{what}"] for what in ("gamma", "beta", "mean", "var")], axis=1))
    w_in = np.concatenate([g["L1_attn_Wq"], g["L1_attn_Wk"], g["L1_attn_Wv"], g["L1_ffn_gate_w"],
                           g["L1_ffn_w1"].transpose(1, 0, 2).reshape(C, EXPERTS * HID)], axis=1)
    w_in = np.stack([w_in[:P], np.concatenate([w_in[P:], w_in[P:]])])
    w_out = np.zeros((P, OUT_CHUNKS, C), np.float32)
    w_out[:, :CHUNKS] = g["L1_ffn_w2"].reshape(CHUNKS, P, C).transpose(1, 0, 2)
    w_out[:, CHUNKS] = g["L1_attn_Wo"][:P]
    w_out[:TAIL, CHUNKS + 1] = g["L1_attn_Wo"][P:]
    w_out[TAIL, CHUNKS + 1] = g["L1_attn_bo"]
    arrays = {
        "x_ch": x.reshape(B, 2, CC, N).transpose(0, 2, 1, 3),
        "x_tok": x.transpose(0, 2, 1).reshape(B, NT, P, C).transpose(0, 2, 1, 3),
        "consts": constants(),
        "w_conv": conv.reshape(CC + 1, 8 * C),
        "bn_rows": np.broadcast_to(rows, (CC + 1, 4, 3 * C)),
        "bn_q": bn_q,
        "w_in": w_in,
        "w_out": w_out.reshape(P, OUT_CHUNKS * C),
        "b1": g["L1_ffn_b1"].reshape(CHUNKS, P).T,
        "b2": np.broadcast_to(g["L1_ffn_b2"].reshape(1, EXPERTS * C), (2, EXPERTS * C)),
        "gate_b": np.broadcast_to(g["L1_ffn_gate_b"], (P, NT, EXPERTS)),
    }
    arrays = {k: np.ascontiguousarray(v) for k, v in arrays.items()}

    nc = bacc.Bacc("TRN2", target_bir_lowering=False, num_devices=1)
    aps = [nc.dram_tensor(k, a.shape, mybir.dt.from_np(a.dtype), kind="ExternalInput").ap()
           for k, a in arrays.items()]
    out = nc.dram_tensor("out", (B, P, NT, C), F32, kind="ExternalOutput").ap()
    build(nc, *aps, out)
    r = run_bass_kernel_spmd(nc, [arrays], core_ids=[0])
    y = r.results[0]["out"]
    return y.transpose(0, 3, 2, 1).reshape(B, C, 32, 32)
```

```python
from contextlib import ExitStack

import numpy as np

import concourse.bass as bass
from concourse import mybir

F32 = mybir.dt.float32
F16 = mybir.dt.float16
BF16 = mybir.dt.bfloat16
ALU = mybir.AluOpType
ACT = mybir.ActivationFunctionType
AX = mybir.AxisListType

B, C, N = 8, 192, 1024
P = 128
CC = C // 2
NT = N // P
QB = 512
NB = N // QB
TB = QB // P
TAIL = C - P
GROUPS = 32
SPIKE_HEADS = 8
HEADS, D = 6, C // 6
PAIRS = HEADS // 2
EXPERTS, HID = 4, 4 * C
HC = HID // P
CHUNKS = EXPERTS * HC

COL_Q, COL_K, COL_V = 0, C, 2 * C
COL_GATE = 3 * C
COL_W1 = COL_GATE + EXPERTS
IN_COLS = COL_W1 + EXPERTS * HID
OUT_CHUNKS = CHUNKS + 2

W_SCALE = 2.0 ** 6
U_SCALE = 2.0 ** 8
A_SCALE = 2.0 ** 4
P_SCALE = 2.0 ** 10
M_SCALE = 2.0 ** 8
SPIKE_SCALE = W_SCALE * 4
MAGIC = 1.5 * 2.0 ** 23
MASKED = -1.0e30
SPIKE_ATTN = float(np.float32((C // SPIKE_HEADS) ** -0.5 * 2)) / 64

K_ID, K_MKQ, K_MQK, K_GRP, K_BLK = 0, P, 2 * P, 3 * P, 3 * P + CC
K_ROW, K_TIE = 3 * P + 2 * CC, 3 * P + 2 * CC + 1
K_COLS = K_TIE + EXPERTS * EXPERTS

FRONT_STEPS, TAIL_STEPS = 51, 33

M_ITEMS = [(b, t, half, pair) for b in range(NB) for t in range(b * TB, (b + 1) * TB)
           for half in range(b + 1) for pair in range(PAIRS)]
E_ITEMS = [(b, pair, kc) for b in range(NB) for pair in range(PAIRS) for kc in range((b + 1) * TB)]
NM, NE = len(M_ITEMS), len(E_ITEMS)
PV_LAG = 2
F_LAG = 2
N_P32, N_P16, N_H = 3, 4, 4

TAIL_AT = ({"wo": 18, "residual": 19, "norm": 21, "turn": 22, "high": 22, "low": 23, "scores": 25,
            "gate": 26, "exp": 26, "best": 27},
           {"wo": 1, "residual": 2, "norm": 3, "turn": 4, "high": 4, "low": 5, "scores": 6,
            "gate": 7, "exp": 7, "best": 8})
FRONT_AT = {"stats": 1, "sums": 2, "sums2": 3, "variance": 3, "clip": 4, "xs": 5, "q": 7, "q_int": 7,
            "kv": 9, "kv_int": 9, "kvm": 13, "kvm_split": 13, "attn": 15, "attn_int": 15, "p": 17,
            "residual": 18, "norm": 19, "turn": 20, "high": 20, "low": 21, "qk": 22, "qk_lo": 22,
            "v": 26, "v_lo": 26, "maxima": 29}
PIECE_AT = tuple(3 * (n + 1) for n in range(7))
PER_CHUNK = 2


class Aside:

    def __init__(self, part):
        self.part = part
        self.due = next(part, None)

    def until(self, step):
        while self.due is not None and self.due <= step:
            self.due = next(self.part, None)

    def finish(self):
        while self.due is not None:
            self.due = next(self.part, None)


class Count:

    def __init__(self):
        self.n = 0

    def more(self, n):
        self.n += n
        return self.n


def run_ends():
    return [j for j, (b, pair, kc) in enumerate(E_ITEMS) if kc == (b + 1) * TB - 1]


def build(nc, x_ch, x_tok, consts, w_conv, bn_rows, bn_q, w_in, w_out, b1, b2, gate_b, out):
    with ExitStack() as ctx:
        def sb(name, shape, dt):
            return ctx.enter_context(nc.sbuf_tensor(name, shape, dt))

        per_image = {}

        def sem(name, gain=0):
            handle = ctx.enter_context(nc.semaphore(name))
            per_image[handle.name] = gain
            return handle

        def at(s, img, n):
            return img * per_image[s.name] + n

        def whole(s):
            return per_image[s.name]

        kst = sb("kst", [P, K_COLS], F32)
        ident16 = sb("ident16", [P, P], F16)
        identb = sb("identb", [P, P], BF16)
        mask_kq = sb("mask_kq", [P, P], BF16)
        mask_qk = sb("mask_qk", [P, P], BF16)
        ones16 = sb("ones16", [P, P], F16)
        exp_bias = sb("exp_bias", [P, 1], F32)
        ident = kst[:, K_ID:K_ID + P]
        group = kst[0:CC, K_GRP:K_GRP + CC]
        block_diag = kst[0:CC, K_BLK:K_BLK + CC]
        NCV = 4 * C
        wc_h = sb("wc_h", [CC + 1, 2, NCV], F16)
        wc_l = sb("wc_l", [CC + 1, 2, NCV], F16)
        q_sb = sb("q_sb", [CC, 2, 2], F32)
        win_h = sb("win_h", [P, IN_COLS], F16)
        win_l = sb("win_l", [P, IN_COLS], F16)
        win_t = sb("win_t", [P, IN_COLS], F16)
        wout_h = sb("wout_h", [P, OUT_CHUNKS, C], F16)
        wout_l = sb("wout_l", [P, OUT_CHUNKS, C], F16)
        b1_sb = sb("b1_sb", [P, CHUNKS], F32)
        b2_sb = sb("b2_sb", [2, EXPERTS * C], F16)
        gb_sb = sb("gb_sb", [P, NT, EXPERTS], F32)

        xc = sb("xc", [CC, 2, N], F32)
        xt = sb("xt", [P, NT, C], F32)
        tmp = sb("tmp", [P, NT * 2 * C], F32)
        xs = sb("xs", [CC + 1, 2, N], F16)
        ai = xs
        kv32 = sb("kv32", [CC, 2, CC], F32)
        kv_h = sb("kv_h", [CC, 2, CC], F16)
        kv_l = sb("kv_l", [CC, 2, CC], F16)
        t1 = sb("t1", [P, NT, C], F32)
        acc = sb("acc", [P, NT, C], F32)
        u = sb("u", [P, NT, 2 * P], F32)
        ah = sb("ah", [P, 2, N], F16)
        al = sb("al", [P, 2, N], F16)
        uh = sb("uh", [P, 2, N], F16)
        ul = sb("ul", [P, 2, N], F16)
        qk_all = sb("qk_all", [P, 8 * N], F16)
        qk_h = qk_all[:, 0:4 * N].rearrange("p (j n) -> p j n", j=4)
        qk_l = qk_all[:, 4 * N:8 * N].rearrange("p (j n) -> p j n", j=4)
        q4 = sb("q4", [CC + 2, HEADS, N], F16)
        k4 = sb("k4", [CC + 2, HEADS, N], F16)
        v_h = sb("v_h", [P, NT, C], F16)
        v_l = sb("v_l", [P, NT, C], F16)
        room32 = sb("room32", [P, N_P32 * 2 * QB], F32)
        p32 = room32[:, :].rearrange("p (s a n) -> p s a n", s=N_P32, a=2)
        as16 = room32[:, :].bitcast(F16)
        kvi = as16[:, 0:NT * 2 * C].rearrange("p (t c) -> p t c", t=NT)
        qi = as16[0:CC, 2 * NT * C:2 * NT * C + 2 * N].rearrange("p (c n) -> p c n", c=2)
        room16 = sb("room16", [P, 2 * N_P16 * 2 * QB], F16)
        half = N_P16 * 2 * QB
        p_h = room16[:, 0:half].rearrange("p (s a n) -> p s a n", s=N_P16, a=2)
        p_l = room16[:, half:2 * half].rearrange("p (s a n) -> p s a n", s=N_P16, a=2)
        h32 = room16[:, 0:half].bitcast(F32).rearrange("p (s n) -> p s n", s=N_H)
        h_h = room16[:, half:half + N_H * QB].rearrange("p (s n) -> p s n", s=N_H)
        h_l = room16[:, half + N_H * QB:2 * half].rearrange("p (s n) -> p s n", s=N_H)
        stage = room16[:, :].bitcast(F32).rearrange("p (s n) -> p s n", s=2)
        o32 = tmp[:, 0:2 * N].rearrange("p (c n) -> p c n", c=2)
        rden = tmp[0:2 * D, 2 * N:2 * N + QB]
        o_h = sb("o_h", [P, 2, N], F16)
        o_l = sb("o_l", [P, 2, N], F16)

        gn_st = sb("gn_st", [CC, 2, 2, 6], F32)
        gn_s = sb("gn_s", [CC, 2], F32)
        gn_d = sb("gn_d", [CC, 2, 4], F32)
        gn_v = sb("gn_v", [CC, 2], F32)
        gn_m = sb("gn_m", [CC, 2], F32)
        gn_b = sb("gn_b", [CC, 2], F32)
        g_st = [sb("g_var", [CC, 2], F32), sb("g_pow", [CC, 2], F32), sb("g_tmp", [CC, 2], F32)]
        g_rstd = sb("g_rstd", [CC, 2], F32)

        class Norm:

            def __init__(self, name, tiles):
                self.stats = sb(name + "_stats", [P, tiles, 6], F32)
                self.sums = sb(name + "_sums", [P, 3, tiles], F32)
                self.mean = sb(name + "_mean", [P, tiles], F32)
                self.var = sb(name + "_var", [P, tiles], F32)
                self.pow = sb(name + "_pow", [P, tiles], F32)
                self.tmp = sb(name + "_tmp", [P, tiles], F32)
                self.rstd = sb(name + "_rstd", [P, tiles], F32)

        norm1, norm2 = Norm("norm1", NT), Norm("norm2", TB)
        minus_half = sb("minus_half", [P, NT], F32)
        mx = sb("mx", [P, 2, NT, HEADS], F32)
        m16 = sb("m16", [P, NT, HEADS, 2], F16)
        mrow = sb("mrow", [2 * HEADS, N], F16)
        gsc = sb("gsc", [P, TB, EXPERTS], F32)
        gex = sb("gex", [P, TB, EXPERTS], F32)
        gpr = sb("gpr", [P, TB, EXPERTS], F32)
        gt1 = sb("gt1", [P, TB], F32)
        gt2 = sb("gt2", [P, TB], F32)
        gcmp = sb("gcmp", [P, TB, EXPERTS, EXPERTS], F32)
        gcm2 = sb("gcm2", [P, TB, EXPERTS, EXPERTS], F32)
        gcnt = sb("gcnt", [P, TB, EXPERTS], F32)
        gate = sb("gate", [P, NT, EXPERTS], F32)

        b2_ones = sb("b2_ones", [2, P], F16)

        bn_st = qk_all[0:CC + 1, 0:8 * N].bitcast(F32)[:, 0:12 * C].rearrange("p (k c) -> p k c", k=4)
        bn_t = room32[0:CC + 1, 0:9 * C].rearrange("p (k c) -> p k c", k=3)
        bq_st = sb("bq_st", [CC, 2, 4], F32)
        bq_t = sb("bq_t", [CC, 4, 2], F32)
        b2_st = room32[0:2, 9 * C:13 * C]
        b2_t = room32[0:2, 13 * C:15 * C].bitcast(F16)

        ps = ctx.enter_context(nc.psum_tensor("ps", [P, 8, QB], F32))

        small_in = sem("small_in")
        stage_in = [sem("stage_in0"), sem("stage_in1")]
        stage_hi = sem("stage_hi")
        stage_lo = sem("stage_lo")
        setup_dve = sem("setup_dve")
        setup_pool = sem("setup_pool")
        setup_act = sem("setup_act")
        consts_ready = sem("consts_ready")

        x_ch_in = sem("x_ch_in", 16)
        x_tok_in = sem("x_tok_in", 16)
        front_step = sem("front_step", FRONT_STEPS)
        gn_rhs = sem("gn_rhs", 2)
        gn_ps = sem("gn_ps", 2)
        var_ready = sem("var_ready", 2)
        pow_done = sem("pow_done", 2)
        gn_ready = sem("gn_ready", 1)
        x_relu = sem("x_relu", 2)
        xs_ready = sem("xs_ready", 2)
        q_ps = sem("q_ps", 2 * NB)
        q_relu = sem("q_relu", 2 * NB)
        kv_ps = sem("kv_ps", NT)
        kv_relu = sem("kv_relu", NT)
        q_int = sem("q_int", NB)
        kv_int = sem("kv_int", NT // 2)
        kvm_ps = sem("kvm_ps", 1)
        kv_split = sem("kv_split", 1)
        at_ps = sem("at_ps", NB)
        a_int = sem("a_int", NB)
        p_ps = sem("p_ps", NT // 2)
        t1_ready = sem("t1_ready", 1)
        a_ready = sem("a_ready", NB)
        a_tr = sem("a_tr", NB)
        ah_done = sem("ah_done", NB)
        al_done = sem("al_done", NB)
        qk_ps = sem("qk_ps", 4 * NB)
        qk_hi = sem("qk_hi", 4 * NB)
        qk_lo = sem("qk_lo", 4 * NB)
        heads_in = [sem("heads_in0", 16 * 6 * HEADS), sem("heads_in1", 16 * 6 * HEADS)]
        v_ps = sem("v_ps", NT // 2)
        v_hi = sem("v_hi", NT // 2)
        v_lo = sem("v_lo", NT // 2)
        m_ps = sem("m_ps", NM)
        m_used = sem("m_used", NM)
        m_split = sem("m_split", NB)
        mrow_ps = sem("mrow_ps", NB)
        mrow_done = sem("mrow_done", NB)
        mrow_in = [sem("mrow_in0", 16 * HEADS), sem("mrow_in1", 16 * HEADS)]
        e_ps = sem("e_ps", NE)
        e_done = sem("e_done", NE)
        p_hi = sem("p_hi", NE)
        p_lo_dve = sem("p_lo_dve", (NE + 1) // 2)
        p_lo_pool = sem("p_lo_pool", NE // 2)
        pv_done = sem("pv_done", NE)
        rden_ready = sem("rden_ready", NB * PAIRS)
        o_done = sem("o_done", NB * PAIRS)
        o_hi = sem("o_hi", NB * PAIRS)
        o_lo = sem("o_lo", NB * PAIRS)
        tail_step = sem("tail_step", NB * TAIL_STEPS)
        wo_ps = sem("wo_ps", NT // 2)
        var2_ready = sem("var2_ready", NB)
        pow2_done = sem("pow2_done", NB)
        u_ready = sem("u_ready", NB)
        u_tr = sem("u_tr", NB)
        uh_done = sem("uh_done", NB)
        ul_done = sem("ul_done", NB)
        gate_ps = sem("gate_ps", NB)
        gate_used = sem("gate_used", NB)
        gate_sub = sem("gate_sub", NB)
        gate_exp = sem("gate_exp", NB)
        h_ps = sem("h_ps", NB * CHUNKS)
        h_act = sem("h_act", NB * CHUNKS)
        h_hi = sem("h_hi", NB * CHUNKS)
        h_lo = sem("h_lo", NB * CHUNKS)
        f2_done = sem("f2_done", NB * CHUNKS)
        y_used = sem("y_used", NB * EXPERTS)
        stored = sem("stored", 16 * NB)

        W = 2048
        pieces = [(kind, c0, min(W, IN_COLS - c0)) for kind in ("head", "tail")
                  for c0 in range(0, IN_COLS, W)]
        FLAT = OUT_CHUNKS * C
        pieces += [("out", c0, min(W, FLAT - c0)) for c0 in range(0, FLAT, W)]
        wconv_pieces = 2
        n_small = 7
        wout_h_flat = wout_h[:, :, :].rearrange("p k c -> p (k c)")
        wout_l_flat = wout_l[:, :, :].rearrange("p k c -> p (k c)")

        block = ctx.enter_context(nc.Block())

        @block.sync
        def _(sp):
            def load(img, later):
                if later:
                    sp.wait_ge(xs_ready, at(xs_ready, img, 0))
                sp.dma_start(xc[:, :, :], x_ch[img]).then_inc(x_ch_in, 16)
                if later:
                    sp.wait_ge(t1_ready, at(t1_ready, img, 0))
                sp.dma_start(xt[:, :, :], x_tok[img]).then_inc(x_tok_in, 16)

            def spread(img):
                for b in range(NB):
                    tok = slice(b * QB, (b + 1) * QB)
                    sp.wait_ge(qk_hi, at(qk_hi, img, 4 * (b + 1)))
                    sp.wait_ge(qk_lo, at(qk_lo, img, 4 * (b + 1)))
                    for dst, first, parts in ((k4, 2, (qk_h, qk_l, qk_h)), (q4, 0, (qk_h, qk_h, qk_l))):
                        for h in range(HEADS):
                            row = D * (h % 4)
                            for n, part in enumerate(parts):
                                sp.dma_start(dst[D * n:D * n + D, h, tok],
                                             part[row:row + D, first + h // 4, tok])\
                                  .then_inc(heads_in[b], 16)
                for b in range(NB):
                    sp.wait_ge(mrow_done, at(mrow_done, img, b + 1))
                    for h in range(HEADS):
                        sp.dma_start(q4[3 * D:3 * D + 2, h, b * QB:(b + 1) * QB],
                                     mrow[2 * h:2 * h + 2, b * QB:(b + 1) * QB])\
                          .then_inc(mrow_in[b], 16)

            for dst, src in ((kst[:, :], consts), (bn_st[:, :, :], bn_rows), (bq_st[:, :, :], bn_q),
                             (b1_sb[:, :], b1), (b2_st[:, :], b2), (gb_sb[:, :, :], gate_b),
                             (tmp[0:CC + 1, 0:2 * NCV], w_conv)):
                sp.dma_start(dst, src).then_inc(small_in, 16)
            load(0, False)
            for n, (kind, c0, w) in enumerate(pieces):
                if n >= 2:
                    sp.wait_ge(stage_lo, n - 1)
                src = {"head": w_in[0], "tail": w_in[1], "out": w_out}[kind][:, c0:c0 + w]
                sp.dma_start(stage[:, n % 2, 0:w], src).then_inc(stage_in[n % 2], 16)

            with sp.Fori(0, B - 1) as img:
                spread(img)
                load(img + 1, True)
            spread(B - 1)

        @block.tensor
        def _(pe):
            def project(dst, high, low, cols, tok, tokens_stationary):
                for n, (w, a, c) in enumerate(((win_h, high, 0), (win_l, high, 0), (win_h, low, 0),
                                               (win_t, high, 1), (win_t, low, 1))):
                    lhs, rhs = w[:, cols], a[:, c, tok]
                    if tokens_stationary:
                        lhs, rhs = rhs, lhs
                    mm = pe.matmul(dst, lhs, rhs, start=(n == 0), stop=(n == 4))
                return mm

            def transpose_block(b, bank):
                for t in range(TB):
                    for c in range(2):
                        mm = pe.transpose(ps[:, bank + c, t * P:(t + 1) * P],
                                          u[:, b * TB + t, c * P:(c + 1) * P], ident)
                return mm

            def front(img, later):
                yield FRONT_AT["sums"]
                pe.wait_ge(gn_rhs, at(gn_rhs, img, 1))
                if later:
                    pe.wait_ge(e_done, at(e_done, img, 0))
                pe.matmul(ps[0:CC, 7, 0:2], group, gn_s[:, :], start=True, stop=True)\
                  .then_inc(gn_ps, 1)
                yield FRONT_AT["sums2"]
                pe.wait_ge(gn_rhs, at(gn_rhs, img, 2))
                pe.matmul(ps[0:CC, 7, 2:4], group, gn_v[:, :], start=True, stop=True)\
                  .then_inc(gn_ps, 1)

                for b in range(NB):
                    yield FRONT_AT["q"] + b
                    if b == 0:
                        pe.wait_ge(xs_ready, at(xs_ready, img, 2))
                        if later:
                            pe.wait_ge(gate_used, at(gate_used, img, 0))
                    for m in range(2):
                        for n, (w, c) in enumerate(((wc_h, 0), (wc_l, 0), (wc_h, 1), (wc_l, 1))):
                            mm = pe.matmul(ps[0:CC, 4 + 2 * b + m, :], w[0:CC, c, m * CC:(m + 1) * CC],
                                           xs[0:CC, c, b * QB:(b + 1) * QB], start=(n == 0), stop=(n == 3))
                        mm.then_inc(q_ps, 1)
                for t in range(NT):
                    if t % 2 == 0:
                        yield FRONT_AT["kv"] + t // 2
                    if t < 4:
                        pe.wait_ge(q_relu, at(q_relu, img, t + 1))
                    else:
                        pe.wait_ge(kv_relu, at(kv_relu, img, t - 3))
                    for n, (w, c) in enumerate(((wc_h, 0), (wc_l, 0), (wc_h, 1), (wc_l, 1))):
                        rows = CC + 1 if c == 0 else CC
                        mm = pe.matmul(ps[:, 4 + t % 4, 0:2 * C], xs[0:rows, c, t * P:(t + 1) * P],
                                       w[0:rows, c, C:3 * C], start=(n == 0), stop=(n == 3))
                    mm.then_inc(kv_ps, 1)
                yield FRONT_AT["kvm"]
                pe.wait_ge(kv_int, at(kv_int, img, NT // 2))
                for m in range(2):
                    for t in range(NT):
                        mm = pe.matmul(ps[0:CC, 4, m * CC:(m + 1) * CC], kvi[:, t, m * CC:(m + 1) * CC],
                                       kvi[:, t, C + m * CC:C + (m + 1) * CC],
                                       start=(t == 0), stop=(t == NT - 1))
                mm.then_inc(kvm_ps, 1)
                for b in range(NB):
                    yield FRONT_AT["attn"] + b
                    pe.wait_ge(kv_split, at(kv_split, img, 1))
                    pe.wait_ge(q_int, at(q_int, img, b + 1))
                    for m in range(2):
                        for n, w in enumerate((kv_h, kv_l)):
                            mm = pe.matmul(ps[0:CC, 4 + 2 * b + m, :], w[:, m, :],
                                           qi[:, m, b * QB:(b + 1) * QB], start=(n == 0), stop=(n == 1))
                    mm.then_inc(at_ps, 1)
                for t in range(NT):
                    if t % TB == 0:
                        yield FRONT_AT["p"] + t // TB
                        pe.wait_ge(a_int, at(a_int, img, t // TB + 1))
                    for n, (w, c) in enumerate(((wc_h, 0), (wc_l, 0), (wc_h, 1), (wc_l, 1))):
                        rows = CC + 1 if c == 0 else CC
                        mm = pe.matmul(ps[:, 4 + t // 2, (t % 2) * C:(t % 2 + 1) * C],
                                       ai[0:rows, c, t * P:(t + 1) * P], w[0:rows, c, 3 * C:4 * C],
                                       start=(n == 0), stop=(n == 3))
                    if t % 2:
                        mm.then_inc(p_ps, 1)

                for b in range(NB):
                    yield FRONT_AT["turn"] + b
                    pe.wait_ge(a_ready, at(a_ready, img, b + 1))
                    transpose_block(b, 4 + 2 * b).then_inc(a_tr, 1)
                for b in range(NB):
                    for j in range(4):
                        if j % 2 == 0:
                            yield FRONT_AT["qk"] + 2 * b + j // 2
                        if b == 0:
                            pe.wait_ge(al_done, at(al_done, img, j // 2 + 1))
                        else:
                            pe.wait_ge(qk_lo, at(qk_lo, img, j + 1))
                        col = (COL_Q, COL_K)[j // 2] + (j % 2) * P
                        width = P if j % 2 == 0 else TAIL
                        project(ps[0:width, 4 + j, :], ah, al, slice(col, col + width),
                                slice(b * QB, (b + 1) * QB), False).then_inc(qk_ps, 1)
                for t in range(NT):
                    if t % 4 == 0:
                        yield FRONT_AT["v"] + t // 4
                    if t % 2 == 0:
                        pe.wait_ge(qk_lo, at(qk_lo, img, 4 + t // 2 + 1))
                    mm = project(ps[:, 4 + t // 2, (t % 2) * C:(t % 2 + 1) * C], ah, al,
                                 slice(COL_V, COL_V + C), slice(t * P, (t + 1) * P), True)
                    if t % 2:
                        mm.then_inc(v_ps, 1)

                def maximum_rows(b):
                    pe.wait_ge(m_split, at(m_split, img, b + 1))
                    for t in range(TB):
                        mm = pe.matmul(ps[0:2 * HEADS, 4, t * P:(t + 1) * P],
                                       m16[:, b * TB + t, :, :].rearrange("p h two -> p (h two)"),
                                       ident16[:, :], start=True, stop=True)
                    mm.then_inc(mrow_ps, 1)

                for i, (b, t, half, pair) in enumerate(M_ITEMS):
                    if i % PER_CHUNK == 0:
                        yield FRONT_AT["maxima"] + i // PER_CHUNK
                    if i == 0:
                        pe.wait_ge(heads_in[0], at(heads_in[0], img, whole(heads_in[0])))
                    if i == NM // 3:
                        pe.wait_ge(heads_in[1], at(heads_in[1], img, whole(heads_in[1])))
                    if i < 2:
                        pe.wait_ge(v_lo, at(v_lo, img, 2 * i + 2))
                    else:
                        pe.wait_ge(m_used, at(m_used, img, i - 1))
                    if i == NM // 2:
                        maximum_rows(0)
                        pe.wait_ge(mrow_done, at(mrow_done, img, 1))
                    diagonal = half == b
                    width = (t % TB + 1) * P if diagonal else QB
                    for a in range(2):
                        h = 2 * pair + a
                        bank = 4 + 2 * (i % 2) + a
                        mm = pe.matmul(ps[:, bank, 0:width], q4[0:3 * D, h, t * P:(t + 1) * P],
                                       k4[0:3 * D, h, half * QB:half * QB + width],
                                       start=True, stop=not diagonal)
                        if diagonal:
                            mm = pe.matmul(ps[:, bank, width - P:width], identb[:, :],
                                           mask_qk[:, :], start=False, stop=True)
                    mm.then_inc(m_ps, 1)
                yield FRONT_AT["maxima"] + NM // PER_CHUNK
                pe.wait_ge(m_used, at(m_used, img, NM - 1))
                maximum_rows(1)

            def tail(img, b, later):
                when, bank = TAIL_AT[b], 2 + 2 * b
                yield when["wo"]
                if b:
                    pe.wait_ge(e_done, at(e_done, img, NE))
                pe.wait_ge(o_hi, at(o_hi, img, (b + 1) * PAIRS))
                pe.wait_ge(o_lo, at(o_lo, img, (b + 1) * PAIRS))
                A, BB = CHUNKS, CHUNKS + 1
                for t in range(b * TB, (b + 1) * TB):
                    tok = slice(t * P, (t + 1) * P)
                    terms = ((o_h[:, 0, tok], wout_h[:, A, :]), (o_h[:, 0, tok], wout_l[:, A, :]),
                             (o_l[:, 0, tok], wout_h[:, A, :]),
                             (o_h[0:TAIL + 1, 1, tok], wout_h[0:TAIL + 1, BB, :]),
                             (o_h[0:TAIL + 1, 1, tok], wout_l[0:TAIL + 1, BB, :]),
                             (o_l[0:TAIL + 1, 1, tok], wout_h[0:TAIL + 1, BB, :]))
                    for n, (lhs, rhs) in enumerate(terms):
                        mm = pe.matmul(ps[:, bank + t % TB // 2, (t % 2) * C:(t % 2 + 1) * C], lhs, rhs,
                                       start=(n == 0), stop=(n == 5))
                    if t % 2:
                        mm.then_inc(wo_ps, 1)
                yield when["turn"]
                pe.wait_ge(u_ready, at(u_ready, img, b + 1))
                transpose_block(b, bank).then_inc(u_tr, 1)
                yield when["scores"]
                pe.wait_ge(ul_done, at(ul_done, img, b + 1))
                for t in range(TB):
                    mm = project(ps[:, bank, t * EXPERTS:(t + 1) * EXPERTS], uh, ul,
                                 slice(COL_GATE, COL_GATE + EXPERTS),
                                 slice((b * TB + t) * P, (b * TB + t + 1) * P), True)
                mm.then_inc(gate_ps, 1)

            def attend(img, later):
                def scores(j):
                    b, pair, kc = E_ITEMS[j]
                    if j < 2:
                        pe.wait_ge(m_used, at(m_used, img, NM))
                        pe.wait_ge(mrow_done, at(mrow_done, img, NB))
                    else:
                        pe.wait_ge(e_done, at(e_done, img, j - 1))
                    if pair == 0 and kc == 0:
                        pe.wait_ge(mrow_in[b], at(mrow_in[b], img, whole(mrow_in[b])))
                    q0 = max(0, kc - b * TB) * P
                    for a in range(2):
                        h = 2 * pair + a
                        bank = 4 + 2 * (j % 2) + a
                        diagonal = kc >= b * TB
                        mm = pe.matmul(ps[:, bank, q0:QB], k4[:, h, kc * P:(kc + 1) * P],
                                       q4[:, h, b * QB + q0:(b + 1) * QB], start=True, stop=not diagonal)
                        if diagonal:
                            mm = pe.matmul(ps[:, bank, q0:q0 + P], identb[:, :],
                                           mask_kq[:, :], start=False, stop=True)
                    mm.then_inc(e_ps, 1)

                def weigh(j):
                    b, pair, kc = E_ITEMS[j]
                    run = b * PAIRS + pair
                    bank = run % 2
                    q0 = max(0, kc - b * TB) * P
                    last = kc == (b + 1) * TB - 1
                    if kc == 0:
                        if run >= 2:
                            pe.wait_ge(o_done, at(o_done, img, run - 1))
                        elif later:
                            pe.wait_ge(h_act, at(h_act, img, 0))
                    pe.wait_ge(p_hi, at(p_hi, img, j + 1))
                    if j % 2:
                        pe.wait_ge(p_lo_pool, at(p_lo_pool, img, j // 2 + 1))
                    else:
                        pe.wait_ge(p_lo_dve, at(p_lo_dve, img, j // 2 + 1))
                    s = j % N_P16
                    for n, (probs, low_v) in enumerate(((p_h, False), (p_l, False), (p_h, True))):
                        for a in range(2):
                            h = 2 * pair + a
                            v = (v_l if low_v else v_h)[:, kc, h * D:(h + 1) * D]
                            mm = pe.matmul(ps[a * D:(a + 1) * D, bank, q0:QB], v, probs[:, s, a, q0:QB],
                                           start=(kc == 0 and n == 0), stop=(last and n == 2))
                        if not low_v:
                            for a in range(2):
                                pe.matmul(ps[(2 + a) * D:(3 + a) * D, bank, q0:QB], ones16[:, 0:D],
                                          probs[:, s, a, q0:QB], start=(kc == 0 and n == 0),
                                          stop=(last and n == 1))
                    mm.then_inc(pv_done, 1)

                aside = Aside(tail(img, 0, later))
                for j in range(NE + PV_LAG):
                    if j < NE:
                        scores(j)
                    if j >= PV_LAG:
                        weigh(j - PV_LAG)
                    aside.until(j)
                aside.finish()

            def experts(img, following):
                def hidden(i):
                    b, n = divmod(i, CHUNKS)
                    if i < 2:
                        pe.wait_ge(o_done, at(o_done, img, NB * PAIRS - 1 + i))
                    else:
                        pe.wait_ge(h_act, at(h_act, img, i - 1))
                    if n == 0:
                        pe.wait_ge(ul_done, at(ul_done, img, b + 1))
                    col = COL_W1 + n * P
                    project(ps[:, i % 2, :], uh, ul, slice(col, col + P), slice(b * QB, (b + 1) * QB), False)\
                        .then_inc(h_ps, 1)

                def expert_out(i):
                    b, n = divmod(i, CHUNKS)
                    e, k = divmod(n, HC)
                    if k == 0:
                        if i == 0:
                            pe.wait_ge(gate_used, at(gate_used, img, 1))
                        else:
                            pe.wait_ge(y_used, at(y_used, img, i // HC))
                    pe.wait_ge(h_hi, at(h_hi, img, i + 1))
                    pe.wait_ge(h_lo, at(h_lo, img, i + 1))
                    s = i % N_H
                    for t in range(TB):
                        dst = ps[:, 2 + t // 2, (t % 2) * C:(t % 2 + 1) * C]
                        tok = slice(t * P, (t + 1) * P)
                        for m, (hid, w) in enumerate(((h_h, wout_h), (h_h, wout_l), (h_l, wout_h))):
                            mm = pe.matmul(dst, hid[:, s, tok], w[:, n, :],
                                           start=(k == 0 and m == 0 and t % 2 == 0), stop=False,
                                           skip_group_check=True)
                        if k == HC - 1:
                            mm = pe.matmul(dst, b2_ones[:, :], b2_sb[:, e * C:(e + 1) * C],
                                           start=False, stop=True, skip_group_check=True)
                    mm.then_inc(f2_done, 1)

                aside = Aside(tail(img, 1, True))
                for i in range(NB * CHUNKS + F_LAG):
                    if i < NB * CHUNKS:
                        hidden(i)
                    if i >= F_LAG:
                        expert_out(i - F_LAG)
                    aside.until(i)
                    following.until(i)
                following.finish()

            pe.wait_ge(consts_ready, 1)
            first = Aside(front(0, False))
            first.until(FRONT_AT["turn"])
            pe.wait_ge(stage_lo, len(pieces))
            first.finish()
            attend(0, False)
            with pe.Fori(0, B - 1) as img:
                experts(img, Aside(front(img + 1, True)))
                attend(img + 1, True)
            experts(B - 1, Aside(iter(())))

        @block.scalar
        def _(act):
            def front(img, later):
                yield FRONT_AT["clip"]
                act.wait_ge(gn_ready, at(gn_ready, img, 1))
                if later:
                    act.wait_ge(o_lo, at(o_lo, img, 0))
                tx = tmp[0:CC, 0:2 * N].rearrange("p (c n) -> p c n", c=2)
                for c in range(2):
                    act.activation(tx[:, c, :], xc[:, c, :], ACT.Relu, scale=g_rstd[:, c:c + 1],
                                   bias=gn_b[:, c:c + 1]).then_inc(x_relu, 1)
                for i in range(2 * NB):
                    b, m = divmod(i, 2)
                    if m == 0:
                        yield FRONT_AT["q"] + b
                    act.wait_ge(q_ps, at(q_ps, img, i + 1))
                    act.activation(tx[:, m, b * QB:(b + 1) * QB], ps[0:CC, 4 + i, :], ACT.Relu,
                                   scale=q_sb[:, m, 0:1], bias=q_sb[:, m, 1:2]).then_inc(q_relu, 1)
                for t in range(NT):
                    if t % 2 == 0:
                        yield FRONT_AT["kv"] + t // 2
                    if t == 0:
                        act.wait_ge(q_int, at(q_int, img, NB))
                    act.wait_ge(kv_ps, at(kv_ps, img, t + 1))
                    act.activation(tmp[:, t * 2 * C:(t + 1) * 2 * C], ps[:, 4 + t % 4, 0:2 * C],
                                   ACT.Relu, scale=1 / SPIKE_SCALE).then_inc(kv_relu, 1)
                for b in range(NB):
                    yield FRONT_AT["high"] + b
                    act.wait_ge(a_tr, at(a_tr, img, b + 1))
                    act.activation(ah[:, :, b * QB:(b + 1) * QB], ps[:, 4 + 2 * b:6 + 2 * b, :],
                                   ACT.Copy, scale=U_SCALE).then_inc(ah_done, 1)
                for i in range(4 * NB):
                    b, j = divmod(i, 4)
                    if j % 2 == 0:
                        yield FRONT_AT["qk"] + i // 2
                    width = P if j % 2 == 0 else TAIL
                    act.wait_ge(qk_ps, at(qk_ps, img, i + 1))
                    act.activation(qk_h[0:width, j, b * QB:(b + 1) * QB], ps[0:width, 4 + j, :], ACT.Copy,
                                   scale=A_SCALE / (U_SCALE * W_SCALE)).then_inc(qk_hi, 1)
                for t in range(0, NT, 2):
                    if t % 4 == 0:
                        yield FRONT_AT["v"] + t // 4
                    if t == 0:
                        if later:
                            act.wait_ge(pv_done, at(pv_done, img, 0))
                    act.wait_ge(v_ps, at(v_ps, img, t // 2 + 1))
                    act.activation(v_h[:, t:t + 2, :],
                                   ps[:, 4 + t // 2, 0:2 * C].rearrange("p (t c) -> p t c", t=2), ACT.Copy,
                                   scale=A_SCALE / (U_SCALE * W_SCALE)).then_inc(v_hi, 1)
                for b in range(NB):
                    yield FRONT_AT["maxima"] + (b + 1) * NM // NB // PER_CHUNK
                    act.wait_ge(mrow_ps, at(mrow_ps, img, b + 1))
                    act.activation(mrow[:, b * QB:(b + 1) * QB], ps[0:2 * HEADS, 4, :], ACT.Copy)\
                       .then_inc(mrow_done, 1)

            def tail(img, b, later):
                when, bank = TAIL_AT[b], 2 + 2 * b
                yield when["high"]
                act.wait_ge(u_tr, at(u_tr, img, b + 1))
                act.activation(uh[:, :, b * QB:(b + 1) * QB], ps[:, bank:bank + 2, :],
                               ACT.Copy, scale=U_SCALE).then_inc(uh_done, 1)
                yield when["exp"]
                act.wait_ge(gate_sub, at(gate_sub, img, b + 1))
                act.activation(gex[:, :, :], gsc[:, :, :], ACT.Exp).then_inc(gate_exp, 1)

            def attend(img, later):
                def high_of_output(run):
                    b, pair = divmod(run, PAIRS)
                    act.wait_ge(o_done, at(o_done, img, run + 1))
                    rows = slice(2 * D * (pair % 2), 2 * D * (pair % 2) + 2 * D)
                    act.activation(o_h[rows, pair // 2, b * QB:(b + 1) * QB],
                                   o32[rows, pair // 2, b * QB:(b + 1) * QB], ACT.Copy)\
                       .then_inc(o_hi, 1)

                aside = Aside(tail(img, 0, later))
                ends = run_ends()
                run = 0
                for j, (b, pair, kc) in enumerate(E_ITEMS):
                    act.wait_ge(e_ps, at(e_ps, img, j + 1))
                    if j >= N_P32:
                        act.wait_ge(p_hi, at(p_hi, img, j - N_P32 + 1))
                        i = j - N_P32
                        if i % 2:
                            act.wait_ge(p_lo_pool, at(p_lo_pool, img, i // 2 + 1))
                        else:
                            act.wait_ge(p_lo_dve, at(p_lo_dve, img, i // 2 + 1))
                    q0 = max(0, kc - b * TB) * P
                    bank = 4 + 2 * (j % 2)
                    act.activation(p32[:, j % N_P32, :, q0:QB], ps[:, bank:bank + 2, q0:QB],
                                   ACT.Exp, bias=exp_bias[:, :],
                                   scale=float(1 / (A_SCALE * A_SCALE * np.sqrt(D)))).then_inc(e_done, 1)
                    if run < len(ends) and j == ends[run] + 4:
                        high_of_output(run)
                        run += 1
                    aside.until(j)
                aside.finish()
                for run in range(run, len(ends)):
                    high_of_output(run)

            def experts(img, following):
                def store(b):
                    act.wait_ge(y_used, at(y_used, img, (b + 1) * EXPERTS))
                    act.dma_start(out[img, :, b * TB:(b + 1) * TB, :], acc[:, b * TB:(b + 1) * TB, :])\
                       .then_inc(stored, 16)

                aside = Aside(tail(img, 1, True))
                for i in range(NB * CHUNKS):
                    n = i % CHUNKS
                    act.wait_ge(h_ps, at(h_ps, img, i + 1))
                    if i == 0:
                        act.wait_ge(pv_done, at(pv_done, img, NE))
                    if i >= N_H:
                        act.wait_ge(h_lo, at(h_lo, img, i - N_H + 1))
                    act.activation(h32[:, i % N_H, :], ps[:, i % 2, :], ACT.Gelu,
                                   scale=1 / (U_SCALE * W_SCALE), bias=b1_sb[:, n:n + 1])\
                       .then_inc(h_act, 1)
                    aside.until(i)
                    following.until(i)
                    if i == CHUNKS + 4:
                        store(0)
                following.finish()
                store(1)

            act.wait_ge(setup_dve, 2)
            act.activation(bn_t[:, 1, :], bn_t[:, 0, :], ACT.Sqrt).then_inc(setup_act, 1)
            act.activation(bq_t[:, 1, :], bq_t[:, 0, :], ACT.Sqrt).then_inc(setup_act, 1)
            first = Aside(front(0, False))
            for n, (kind, c0, w) in enumerate(pieces):
                act.wait_ge(stage_in[n % 2], 16 * (n // 2 + 1))
                src = stage[:, n % 2, 0:w]
                dst = {"head": win_h, "tail": win_t, "out": wout_h_flat}[kind][:, c0:c0 + w]
                act.activation(dst, src, ACT.Copy, scale=W_SCALE).then_inc(stage_hi, 1)
                first.until(PIECE_AT[n])
            act.wait_ge(consts_ready, 1)
            first.finish()
            attend(0, False)
            with act.Fori(0, B - 1) as img:
                experts(img, Aside(front(img + 1, True)))
                attend(img + 1, True)
            experts(B - 1, Aside(iter(())))
            act.wait_ge(stored, B * whole(stored))

        @block.gpsimd
        def _(pool):
            fills = ((minus_half[:, :], -0.5), (ones16[:, :], 1.0), (exp_bias[:, :], float(np.log(P_SCALE))),
                     (xs[CC:CC + 1, :, :], 1.0),
                     (k4[3 * D:3 * D + 2, :, :], M_SCALE), (o_h[TAIL:TAIL + 1, 1, :], A_SCALE),
                     (o_l[TAIL:TAIL + 1, 1, :], 0.0), (b2_ones[:, :], A_SCALE))
            for n, (dst, value) in enumerate(fills):
                nc.gpsimd.memset(dst, value).then_inc(setup_pool, 1)
                pool.wait_ge(setup_pool, n + 1)

            with pool.Fori(0, B) as img:
                pool.wait_ge(var_ready, at(var_ready, img, 1))
                nc.gpsimd.tensor_tensor(g_st[1][:, :], g_st[0][:, :], minus_half[0:CC, 0:2], ALU.pow)\
                  .then_inc(pow_done, 1)
                pool.wait_ge(var_ready, at(var_ready, img, 2))
                nc.gpsimd.tensor_tensor(norm1.pow[:, :], norm1.var[:, :], minus_half[:, 0:NT], ALU.pow)\
                  .then_inc(pow_done, 1)

                def low_of_output(run, halves):
                    b, pair = divmod(run, PAIRS)
                    pool.wait_ge(p_lo_pool, at(p_lo_pool, img, halves))
                    if run:
                        pool.wait_ge(o_lo, at(o_lo, img, run))
                    pool.wait_ge(o_hi, at(o_hi, img, run + 1))
                    rows = slice(2 * D * (pair % 2), 2 * D * (pair % 2) + 2 * D)
                    where = (rows, pair // 2, slice(b * QB, (b + 1) * QB))
                    nc.gpsimd.tensor_tensor(o_l[where], o32[where], o_h[where], ALU.subtract).then_inc(o_lo, 1)

                def power_of_tail(b):
                    pool.wait_ge(var2_ready, at(var2_ready, img, b + 1))
                    nc.gpsimd.tensor_tensor(norm2.pow[:, :], norm2.var[:, :], minus_half[:, 0:TB], ALU.pow)\
                      .then_inc(pow2_done, 1)

                ends = run_ends()
                run = 0
                for j in range(1, NE, 2):
                    b, pair, kc = E_ITEMS[j]
                    q0 = max(0, kc - b * TB) * P
                    pool.wait_ge(p_hi, at(p_hi, img, j + 1))
                    if j >= N_P16:
                        pool.wait_ge(pv_done, at(pv_done, img, j - N_P16 + 1))
                    nc.gpsimd.tensor_tensor(p_l[:, j % N_P16, :, q0:QB], p32[:, j % N_P32, :, q0:QB],
                                            p_h[:, j % N_P16, :, q0:QB], ALU.subtract)\
                      .then_inc(p_lo_pool, 1)
                    if run < len(ends) and j >= ends[run] + 5:
                        low_of_output(run, (j + 1) // 2)
                        run += 1
                        pool.wait_ge(o_lo, at(o_lo, img, run))
                    if j in (TAIL_AT[0]["residual"], TAIL_AT[0]["residual"] + 1):
                        power_of_tail(0)
                for run in range(run, len(ends)):
                    low_of_output(run, NE // 2)
                pool.wait_ge(o_lo, at(o_lo, img, len(ends)))
                power_of_tail(1)

        @block.vector
        def _(dve):
            V = nc.vector

            def norm_statistics(norm, img, src, tiles, step, steps, signal):
                for n, t in enumerate(tiles):
                    V.bn_stats(norm.stats[:, n, :], src[:, t, :]).then_inc(step, 1)
                dve.wait_ge(step, at(step, img, steps.more(len(tiles))))
                even, odd = norm.stats[:, :, 0:3], norm.stats[:, :, 3:6]
                V.tensor_tensor(norm.sums[:, 0, :], even[:, :, 1], odd[:, :, 1], ALU.add).then_inc(step, 1)
                V.tensor_tensor(norm.sums[:, 1, :], even[:, :, 1], odd[:, :, 1], ALU.subtract).then_inc(step, 1)
                V.tensor_tensor(norm.sums[:, 2, :], even[:, :, 2], odd[:, :, 2], ALU.add).then_inc(step, 1)
                dve.wait_ge(step, at(step, img, steps.more(3)))
                V.tensor_scalar(norm.mean[:, :], norm.sums[:, 0, :], 1 / 2, None, ALU.mult).then_inc(step, 1)
                V.scalar_tensor_tensor(out=norm.sums[:, 1, :], in0=norm.sums[:, 1, :], scalar=1 / 4,
                                       in1=norm.sums[:, 1, :], op0=ALU.mult, op1=ALU.mult).then_inc(step, 1)
                V.tensor_scalar(norm.sums[:, 2, :], norm.sums[:, 2, :], 1 / C, 1e-5, ALU.mult, ALU.add)\
                 .then_inc(step, 1)
                dve.wait_ge(step, at(step, img, steps.more(3)))
                V.tensor_tensor(norm.var[:, :], norm.sums[:, 1, :], norm.sums[:, 2, :], ALU.add)\
                 .then_inc(signal, 1)

            def refine(img, v, y, a, rstd, step, steps):
                V.tensor_tensor(a, y, y, ALU.mult).then_inc(step, 1)
                dve.wait_ge(step, at(step, img, steps.more(1)))
                V.scalar_tensor_tensor(out=a, in0=a, scalar=-0.5, in1=v, op0=ALU.mult, op1=ALU.mult).then_inc(step, 1)
                dve.wait_ge(step, at(step, img, steps.more(1)))
                V.scalar_tensor_tensor(out=rstd, in0=a, scalar=1.5, in1=y, op0=ALU.add, op1=ALU.mult).then_inc(step, 1)
                dve.wait_ge(step, at(step, img, steps.more(1)))

            def normalized_block(norm, img, src, b, tiles, step, steps, signal):
                for n, t in zip(tiles, range(b * TB, (b + 1) * TB)):
                    V.tensor_scalar(u[:, t, 0:C], src[:, t, :], norm.mean[:, n:n + 1],
                                    norm.rstd[:, n:n + 1], ALU.subtract, ALU.mult).then_inc(step, 1)
                dve.wait_ge(step, at(step, img, steps.more(TB)))
                V.tensor_copy(u[:, b * TB:(b + 1) * TB, C:], u[:, b * TB:(b + 1) * TB, P:C])\
                 .then_inc(signal, 1)

            def front(img, later):
                steps = Count()
                yield FRONT_AT["stats"]
                dve.wait_ge(x_ch_in, at(x_ch_in, img, 16))
                for c in range(2):
                    for s in range(2):
                        V.bn_stats(gn_st[:, c, s, :], xc[:, c, s * 512:(s + 1) * 512]).then_inc(front_step, 1)
                dve.wait_ge(front_step, at(front_step, img, steps.more(4)))
                part = gn_st[:, :, :, :].rearrange("p c s (o k) -> p c (s o) k", o=2)
                V.tensor_reduce(gn_s[:, :], part[:, :, :, 1], AX.X, ALU.add).then_inc(gn_rhs, 1)
                yield FRONT_AT["sums"]
                dve.wait_ge(gn_ps, at(gn_ps, img, 1))
                V.tensor_scalar(gn_m[:, :], ps[0:CC, 7, 0:2], 1 / 4, None, ALU.mult).then_inc(front_step, 1)
                dve.wait_ge(front_step, at(front_step, img, steps.more(1)))
                V.tensor_tensor(gn_d[:, :, :], part[:, :, :, 1],
                                gn_m[:, :, None].broadcast_to([CC, 2, 4]), ALU.subtract).then_inc(front_step, 1)
                dve.wait_ge(front_step, at(front_step, img, steps.more(1)))
                V.tensor_tensor(gn_d[:, :, :], gn_d[:, :, :], gn_d[:, :, :], ALU.mult).then_inc(front_step, 1)
                dve.wait_ge(front_step, at(front_step, img, steps.more(1)))
                V.scalar_tensor_tensor(out=gn_d[:, :, :], in0=part[:, :, :, 2], scalar=4 / N,
                                       in1=gn_d[:, :, :], op0=ALU.mult, op1=ALU.add).then_inc(front_step, 1)
                dve.wait_ge(front_step, at(front_step, img, steps.more(1)))
                V.tensor_reduce(gn_v[:, :], gn_d[:, :, :], AX.X, ALU.add).then_inc(gn_rhs, 1)
                yield FRONT_AT["variance"]
                dve.wait_ge(gn_ps, at(gn_ps, img, 2))
                V.tensor_scalar(g_st[0][:, :], ps[0:CC, 7, 2:4], 1 / 4, 1e-5, ALU.mult, ALU.add)\
                 .then_inc(var_ready, 1)
                yield FRONT_AT["clip"]
                dve.wait_ge(pow_done, at(pow_done, img, 1))
                refine(img, g_st[0][:, :], g_st[1][:, :], g_st[2][:, :], g_rstd[:, :], front_step, steps)
                V.scalar_tensor_tensor(out=gn_b[:, :], in0=gn_m[:, :], scalar=-1.0, in1=g_rstd[:, :],
                                       op0=ALU.mult, op1=ALU.mult).then_inc(gn_ready, 1)

                tx = tmp[0:CC, 0:2 * N].rearrange("p (c n) -> p c n", c=2)

                def spike(dst, t, signal):
                    V.tensor_scalar(t, t, 4.0, MAGIC, ALU.min, ALU.add).then_inc(front_step, 1)
                    dve.wait_ge(front_step, at(front_step, img, steps.more(1)))
                    V.tensor_scalar(dst, t, MAGIC, None, ALU.subtract).then_inc(signal, 1)

                for c in range(2):
                    yield FRONT_AT["xs"] + c
                    dve.wait_ge(x_relu, at(x_relu, img, c + 1))
                    spike(xs[0:CC, c, :], tx[:, c, :], xs_ready)
                for b in range(NB):
                    yield FRONT_AT["q_int"] + b
                    if b == 0:
                        if later:
                            dve.wait_ge(p_lo_pool, at(p_lo_pool, img, 0))
                    dve.wait_ge(q_relu, at(q_relu, img, 2 * b + 2))
                    spike(qi[:, :, b * QB:(b + 1) * QB], tx[:, :, b * QB:(b + 1) * QB], q_int)
                for i in range(NT // 2):
                    yield FRONT_AT["kv_int"] + i
                    dve.wait_ge(kv_relu, at(kv_relu, img, 2 * i + 2))
                    spike(kvi[:, 2 * i:2 * i + 2, :].rearrange("p t c -> p (t c)"),
                          tmp[:, i * 4 * C:(i + 1) * 4 * C], kv_int)
                yield FRONT_AT["kvm_split"]
                dve.wait_ge(kvm_ps, at(kvm_ps, img, 1))
                V.tensor_tensor(kv32[:, :, :], ps[0:CC, 4, 0:C].rearrange("p (m e) -> p m e", m=2),
                                block_diag[:, None, :].broadcast_to([CC, 2, CC]), ALU.mult).then_inc(front_step, 1)
                dve.wait_ge(front_step, at(front_step, img, steps.more(1)))
                V.tensor_copy(kv_h[:, :, :], kv32[:, :, :]).then_inc(front_step, 1)
                dve.wait_ge(front_step, at(front_step, img, steps.more(1)))
                V.tensor_tensor(kv_l[:, :, :], kv32[:, :, :], kv_h[:, :, :], ALU.subtract)\
                 .then_inc(kv_split, 1)
                for b in range(NB):
                    yield FRONT_AT["attn_int"] + b
                    dve.wait_ge(at_ps, at(at_ps, img, b + 1))
                    V.tensor_scalar(tx[:, :, b * QB:(b + 1) * QB], ps[0:CC, 4 + 2 * b:6 + 2 * b, :],
                                    SPIKE_ATTN, 4.0, ALU.mult, ALU.min).then_inc(front_step, 1)
                    dve.wait_ge(front_step, at(front_step, img, steps.more(1)))
                    V.tensor_scalar(ai[0:CC, :, b * QB:(b + 1) * QB], tx[:, :, b * QB:(b + 1) * QB],
                                    MAGIC, MAGIC, ALU.add, ALU.subtract).then_inc(a_int, 1)
                yield FRONT_AT["residual"]
                dve.wait_ge(x_tok_in, at(x_tok_in, img, 16))
                for i in range(NT // 2):
                    dve.wait_ge(p_ps, at(p_ps, img, i + 1))
                    ins = V.scalar_tensor_tensor(
                        out=t1[:, 2 * i:2 * i + 2, :],
                        in0=ps[:, 4 + i, 0:2 * C].rearrange("p (t c) -> p t c", t=2), scalar=1 / SPIKE_SCALE,
                        in1=xt[:, 2 * i:2 * i + 2, :], op0=ALU.mult, op1=ALU.add)
                ins.then_inc(t1_ready, 1)
                dve.wait_ge(t1_ready, at(t1_ready, img, 1))

                norm_statistics(norm1, img, t1, range(NT), front_step, steps, var_ready)
                yield FRONT_AT["norm"]
                dve.wait_ge(pow_done, at(pow_done, img, 2))
                refine(img, norm1.var[:, :], norm1.pow[:, :], norm1.tmp[:, :], norm1.rstd[:, :],
                       front_step, steps)
                if later:
                    dve.wait_ge(u_tr, at(u_tr, img, 0))
                for b in range(NB):
                    yield FRONT_AT["norm"] + b
                    normalized_block(norm1, img, t1, b, range(b * TB, (b + 1) * TB), front_step, steps, a_ready)
                for b in range(NB):
                    yield FRONT_AT["low"] + b
                    dve.wait_ge(ah_done, at(ah_done, img, b + 1))
                    V.scalar_tensor_tensor(out=al[:, :, b * QB:(b + 1) * QB],
                                           in0=ps[:, 4 + 2 * b:6 + 2 * b, :], scalar=U_SCALE,
                                           in1=ah[:, :, b * QB:(b + 1) * QB], op0=ALU.mult,
                                           op1=ALU.subtract).then_inc(al_done, 1)
                for i in range(4 * NB):
                    b, j = divmod(i, 4)
                    if j % 2 == 0:
                        yield FRONT_AT["qk_lo"] + i // 2
                    width = P if j % 2 == 0 else TAIL
                    dve.wait_ge(qk_hi, at(qk_hi, img, i + 1))
                    V.scalar_tensor_tensor(out=qk_l[0:width, j, b * QB:(b + 1) * QB],
                                           in0=ps[0:width, 4 + j, :], scalar=A_SCALE / (U_SCALE * W_SCALE),
                                           in1=qk_h[0:width, j, b * QB:(b + 1) * QB], op0=ALU.mult,
                                           op1=ALU.subtract).then_inc(qk_lo, 1)
                for t in range(0, NT, 2):
                    if t % 4 == 0:
                        yield FRONT_AT["v_lo"] + t // 4
                    dve.wait_ge(v_hi, at(v_hi, img, t // 2 + 1))
                    V.scalar_tensor_tensor(out=v_l[:, t:t + 2, :],
                                           in0=ps[:, 4 + t // 2, 0:2 * C].rearrange("p (t c) -> p t c", t=2),
                                           scalar=A_SCALE / (U_SCALE * W_SCALE), in1=v_h[:, t:t + 2, :],
                                           op0=ALU.mult, op1=ALU.subtract).then_inc(v_lo, 1)
                for i, (b, t, half, pair) in enumerate(M_ITEMS):
                    if i % PER_CHUNK == 0:
                        yield FRONT_AT["maxima"] + i // PER_CHUNK
                    dve.wait_ge(m_ps, at(m_ps, img, i + 1))
                    width = (t % TB + 1) * P if half == b else QB
                    bank = 4 + 2 * (i % 2)
                    V.tensor_reduce(mx[:, half, t, 2 * pair:2 * pair + 2],
                                    ps[:, bank:bank + 2, 0:width], AX.X, ALU.max)\
                     .then_inc(m_used, 1)
                    if i + 1 in (NM // 3, NM):
                        dve.wait_ge(m_used, at(m_used, img, i + 1))
                        rows = slice(b * TB, (b + 1) * TB)
                        if b:
                            V.tensor_tensor(mx[:, 0, rows, :], mx[:, 0, rows, :], mx[:, 1, rows, :], ALU.max)\
                             .then_inc(front_step, 1)
                            dve.wait_ge(front_step, at(front_step, img, steps.more(1)))
                        V.tensor_scalar(m16[:, rows, :, 0], mx[:, 0, rows, :], -1 / M_SCALE, None, ALU.mult)\
                         .then_inc(front_step, 1)
                        dve.wait_ge(front_step, at(front_step, img, steps.more(1)))
                        V.scalar_tensor_tensor(out=m16[:, rows, :, 1], in0=mx[:, 0, rows, :],
                                               scalar=-1 / M_SCALE, in1=m16[:, rows, :, 0],
                                               op0=ALU.mult, op1=ALU.subtract).then_inc(m_split, 1)
                assert steps.n == FRONT_STEPS, steps.n

            def tail(img, b, later):
                steps = Count()
                steps.more(b * TAIL_STEPS)
                when, bank = TAIL_AT[b], 2 + 2 * b
                yield when["residual"]
                if b == 0 and later:
                    dve.wait_ge(stored, at(stored, img, 0))
                for i in range(2):
                    n = b * TB + 2 * i
                    dve.wait_ge(wo_ps, at(wo_ps, img, 2 * b + i + 1))
                    V.scalar_tensor_tensor(
                        out=acc[:, n:n + 2, :],
                        in0=ps[:, bank + i, 0:2 * C].rearrange("p (t c) -> p t c", t=2),
                        scalar=1 / (A_SCALE * W_SCALE), in1=t1[:, n:n + 2, :],
                        op0=ALU.mult, op1=ALU.add).then_inc(tail_step, 1)
                dve.wait_ge(tail_step, at(tail_step, img, steps.more(2)))
                norm_statistics(norm2, img, acc, range(b * TB, (b + 1) * TB), tail_step, steps, var2_ready)
                yield when["norm"]
                dve.wait_ge(pow2_done, at(pow2_done, img, b + 1))
                refine(img, norm2.var[:, :], norm2.pow[:, :], norm2.tmp[:, :], norm2.rstd[:, :],
                       tail_step, steps)
                normalized_block(norm2, img, acc, b, range(TB), tail_step, steps, u_ready)
                yield when["low"]
                dve.wait_ge(uh_done, at(uh_done, img, b + 1))
                V.scalar_tensor_tensor(out=ul[:, :, b * QB:(b + 1) * QB],
                                       in0=ps[:, bank:bank + 2, :], scalar=U_SCALE,
                                       in1=uh[:, :, b * QB:(b + 1) * QB], op0=ALU.mult,
                                       op1=ALU.subtract).then_inc(ul_done, 1)

                yield when["gate"]
                tiles = slice(b * TB, (b + 1) * TB)
                dve.wait_ge(gate_ps, at(gate_ps, img, b + 1))
                V.scalar_tensor_tensor(
                    out=gsc[:, :, :], in0=ps[:, bank, 0:TB * EXPERTS].rearrange("p (t e) -> p t e", t=TB),
                    scalar=1 / (U_SCALE * W_SCALE), in1=gb_sb[:, tiles, :], op0=ALU.mult, op1=ALU.add)\
                 .then_inc(tail_step, 1)
                dve.wait_ge(tail_step, at(tail_step, img, steps.more(1)))
                V.tensor_reduce(gt1[:, :], gsc[:, :, :], AX.X, ALU.max).then_inc(gate_used, 1)
                dve.wait_ge(gate_used, at(gate_used, img, b + 1))
                each = [P, TB, EXPERTS]
                V.tensor_tensor(gsc[:, :, :], gsc[:, :, :], gt1[:, :, None].broadcast_to(each), ALU.subtract)\
                 .then_inc(gate_sub, 1)
                yield when["best"]
                dve.wait_ge(gate_exp, at(gate_exp, img, b + 1))
                V.tensor_reduce(gt1[:, :], gex[:, :, :], AX.X, ALU.add).then_inc(tail_step, 1)
                dve.wait_ge(tail_step, at(tail_step, img, steps.more(1)))
                V.reciprocal(gt2[:, :], gt1[:, :]).then_inc(tail_step, 1)
                dve.wait_ge(tail_step, at(tail_step, img, steps.more(1)))
                V.tensor_tensor(gpr[:, :, :], gex[:, :, :], gt2[:, :, None].broadcast_to(each), ALU.mult)\
                 .then_inc(tail_step, 1)
                dve.wait_ge(tail_step, at(tail_step, img, steps.more(1)))
                square = [P, TB, EXPERTS, EXPERTS]
                other = gpr[:, :, None, :].broadcast_to(square)
                own = gpr[:, :, :, None].broadcast_to(square)
                tie = kst[:, None, K_TIE:K_TIE + EXPERTS * EXPERTS].broadcast_to([P, TB, EXPERTS * EXPERTS])
                flat = "p t i j -> p t (i j)"
                V.tensor_tensor(gcmp[:, :, :, :], other, own, ALU.is_equal).then_inc(tail_step, 1)
                dve.wait_ge(tail_step, at(tail_step, img, steps.more(1)))
                V.tensor_tensor(gcmp[:, :, :, :].rearrange(flat), gcmp[:, :, :, :].rearrange(flat),
                                tie, ALU.mult).then_inc(tail_step, 1)
                V.tensor_tensor(gcm2[:, :, :, :], other, own, ALU.is_gt).then_inc(tail_step, 1)
                dve.wait_ge(tail_step, at(tail_step, img, steps.more(2)))
                V.tensor_tensor(gcmp[:, :, :, :], gcmp[:, :, :, :], gcm2[:, :, :, :], ALU.add).then_inc(tail_step, 1)
                dve.wait_ge(tail_step, at(tail_step, img, steps.more(1)))
                V.tensor_reduce(gcnt[:, :, :], gcmp[:, :, :, :], AX.X, ALU.add).then_inc(tail_step, 1)
                dve.wait_ge(tail_step, at(tail_step, img, steps.more(1)))
                V.scalar_tensor_tensor(out=gpr[:, :, :], in0=gcnt[:, :, :], scalar=2.0,
                                       in1=gpr[:, :, :], op0=ALU.is_lt, op1=ALU.mult).then_inc(tail_step, 1)
                dve.wait_ge(tail_step, at(tail_step, img, steps.more(1)))
                V.tensor_reduce(gt1[:, :], gpr[:, :, :], AX.X, ALU.add).then_inc(tail_step, 1)
                dve.wait_ge(tail_step, at(tail_step, img, steps.more(1)))
                V.tensor_scalar(gt1[:, :], gt1[:, :], 1e-9, None, ALU.add).then_inc(tail_step, 1)
                dve.wait_ge(tail_step, at(tail_step, img, steps.more(1)))
                V.reciprocal(gt2[:, :], gt1[:, :]).then_inc(tail_step, 1)
                dve.wait_ge(tail_step, at(tail_step, img, steps.more(1)))
                V.scalar_tensor_tensor(out=gate[:, tiles, :], in0=gpr[:, :, :],
                                       scalar=1 / (A_SCALE * W_SCALE),
                                       in1=gt2[:, :, None].broadcast_to(each),
                                       op0=ALU.mult, op1=ALU.mult).then_inc(tail_step, 1)
                dve.wait_ge(tail_step, at(tail_step, img, steps.more(1)))
                assert steps.n == (b + 1) * TAIL_STEPS, steps.n

            def attend(img, later):
                def normalize(run):
                    b, pair = divmod(run, PAIRS)
                    dve.wait_ge(pv_done, at(pv_done, img, run_ends()[run] + 1))
                    bank = run % 2
                    V.reciprocal(rden[:, :], ps[2 * D:4 * D, bank, :]).then_inc(rden_ready, 1)
                    dve.wait_ge(rden_ready, at(rden_ready, img, run + 1))
                    rows = slice(2 * D * (pair % 2), 2 * D * (pair % 2) + 2 * D)
                    V.tensor_tensor(o32[rows, pair // 2, b * QB:(b + 1) * QB], ps[0:2 * D, bank, :],
                                    rden[:, :], ALU.mult).then_inc(o_done, 1)

                aside = Aside(tail(img, 0, later))
                if later:
                    dve.wait_ge(f2_done, at(f2_done, img, 0))
                ends = run_ends()
                run = 0
                for j, (b, pair, kc) in enumerate(E_ITEMS):
                    q0 = max(0, kc - b * TB) * P
                    dve.wait_ge(e_done, at(e_done, img, j + 1))
                    if j >= N_P16:
                        dve.wait_ge(pv_done, at(pv_done, img, j - N_P16 + 1))
                    V.tensor_copy(p_h[:, j % N_P16, :, q0:QB], p32[:, j % N_P32, :, q0:QB])\
                     .then_inc(p_hi, 1)
                    if j % 2 == 0:
                        dve.wait_ge(p_hi, at(p_hi, img, j + 1))
                        V.tensor_tensor(p_l[:, j % N_P16, :, q0:QB], p32[:, j % N_P32, :, q0:QB],
                                        p_h[:, j % N_P16, :, q0:QB], ALU.subtract).then_inc(p_lo_dve, 1)
                    if run < len(ends) and j == ends[run] + 3:
                        normalize(run)
                        run += 1
                    aside.until(j)
                aside.finish()
                for run in range(run, len(ends)):
                    normalize(run)

            def experts(img, following):
                def add_expert(y):
                    b, e = divmod(y, EXPERTS)
                    dve.wait_ge(f2_done, at(f2_done, img, (y + 1) * HC))
                    for t in range(TB):
                        n = b * TB + t
                        if y and t == 0:
                            dve.wait_ge(y_used, at(y_used, img, y))
                        ins = V.scalar_tensor_tensor(
                            out=acc[:, n, :], in0=ps[:, 2 + t // 2, (t % 2) * C:(t % 2 + 1) * C],
                            scalar=gate[:, n, e:e + 1], in1=acc[:, n, :], op0=ALU.mult, op1=ALU.add)
                    ins.then_inc(y_used, 1)

                aside = Aside(tail(img, 1, True))
                for i in range(NB * CHUNKS + F_LAG):
                    if i < NB * CHUNKS:
                        dve.wait_ge(h_act, at(h_act, img, i + 1))
                        if i >= N_H:
                            dve.wait_ge(f2_done, at(f2_done, img, i - N_H + 1))
                        s = i % N_H
                        V.tensor_scalar(h_h[:, s, :], h32[:, s, :], A_SCALE, None, ALU.mult)\
                         .then_inc(h_hi, 1)
                        dve.wait_ge(h_hi, at(h_hi, img, i + 1))
                        V.scalar_tensor_tensor(out=h_l[:, s, :], in0=h32[:, s, :], scalar=A_SCALE,
                                               in1=h_h[:, s, :], op0=ALU.mult, op1=ALU.subtract)\
                         .then_inc(h_lo, 1)
                    if i >= F_LAG and (i - F_LAG) % HC == HC - 1:
                        add_expert((i - F_LAG) // HC)
                    aside.until(i)
                    following.until(i)
                following.finish()

            dve.wait_ge(small_in, 16 * n_small)
            setup = Count()
            V.tensor_scalar(bn_t[:, 0, :], bn_st[:, 3, :], 1e-5, None, ALU.add).then_inc(setup_dve, 1)
            dve.wait_ge(setup_dve, setup.more(1))
            V.tensor_scalar(bq_t[:, 0, :], bq_st[:, :, 3], 1e-5, None, ALU.add).then_inc(setup_dve, 1)
            dve.wait_ge(setup_dve, setup.more(1))
            V.tensor_copy(ident16[:, :], ident).then_inc(setup_dve, 1)
            dve.wait_ge(setup_dve, setup.more(1))
            V.tensor_copy(identb[:, :], ident).then_inc(setup_dve, 1)
            dve.wait_ge(setup_dve, setup.more(1))
            V.tensor_scalar(mask_kq[:, :], kst[:, K_MKQ:K_MKQ + P], MASKED, None, ALU.mult).then_inc(setup_dve, 1)
            dve.wait_ge(setup_dve, setup.more(1))
            V.tensor_scalar(mask_qk[:, :], kst[:, K_MQK:K_MQK + P], MASKED, None, ALU.mult).then_inc(setup_dve, 1)
            dve.wait_ge(setup_dve, setup.more(1))
            V.tensor_scalar(b2_t[:, :], b2_st[:, :], W_SCALE, None, ALU.mult).then_inc(setup_dve, 1)
            dve.wait_ge(setup_dve, setup.more(1))
            V.tensor_scalar(b2_st[:, :], b2_st[:, :], W_SCALE, None, ALU.mult).then_inc(setup_dve, 1)
            dve.wait_ge(setup_dve, setup.more(1))
            V.tensor_scalar(b2_t[:, :], b2_t[:, :], kst[0:2, K_ROW:K_ROW + 1], None, ALU.mult).then_inc(setup_dve, 1)
            dve.wait_ge(setup_dve, setup.more(1))
            V.tensor_tensor(b2_sb[:, :], b2_st[:, :], b2_t[:, :], ALU.subtract).then_inc(setup_dve, 1)
            dve.wait_ge(setup_dve, setup.more(1))

            def newton(y, v, a, into):
                V.tensor_tensor(a, y, y, ALU.mult).then_inc(setup_dve, 1)
                dve.wait_ge(setup_dve, setup.more(1))
                V.scalar_tensor_tensor(out=a, in0=a, scalar=-0.5, in1=v, op0=ALU.mult, op1=ALU.mult).then_inc(setup_dve, 1)
                dve.wait_ge(setup_dve, setup.more(1))
                V.scalar_tensor_tensor(out=into, in0=a, scalar=1.5, in1=y, op0=ALU.add, op1=ALU.mult).then_inc(setup_dve, 1)
                dve.wait_ge(setup_dve, setup.more(1))

            dve.wait_ge(setup_act, 2)
            V.reciprocal(bq_t[:, 1, :], bq_t[:, 1, :]).then_inc(setup_dve, 1)
            dve.wait_ge(setup_dve, setup.more(1))
            newton(bq_t[:, 1, :], bq_t[:, 0, :], bq_t[:, 2, :], bq_t[:, 1, :])
            V.tensor_tensor(bq_t[:, 2, :], bq_t[:, 1, :], bq_st[:, :, 0], ALU.mult).then_inc(setup_dve, 1)
            dve.wait_ge(setup_dve, setup.more(1))
            V.tensor_tensor(bq_t[:, 3, :], bq_t[:, 2, :], bq_st[:, :, 2], ALU.mult).then_inc(setup_dve, 1)
            dve.wait_ge(setup_dve, setup.more(1))
            V.tensor_tensor(q_sb[:, :, 1], bq_st[:, :, 1], bq_t[:, 3, :], ALU.subtract).then_inc(setup_dve, 1)
            dve.wait_ge(setup_dve, setup.more(1))
            V.tensor_scalar(q_sb[:, :, 0], bq_t[:, 2, :], 1 / SPIKE_SCALE, None, ALU.mult).then_inc(setup_dve, 1)
            dve.wait_ge(setup_dve, setup.more(1))
            V.reciprocal(bn_t[:, 1, :], bn_t[:, 1, :]).then_inc(setup_dve, 1)
            dve.wait_ge(setup_dve, setup.more(1))
            newton(bn_t[:, 1, :], bn_t[:, 0, :], bn_t[:, 2, :], bn_t[:, 1, :])
            V.tensor_tensor(bn_t[:, 0, :], bn_t[:, 1, :], bn_st[:, 0, :], ALU.mult).then_inc(setup_dve, 1)
            dve.wait_ge(setup_dve, setup.more(1))
            V.tensor_tensor(bn_t[:, 1, :], bn_t[:, 0, :], bn_st[:, 2, :], ALU.mult).then_inc(setup_dve, 1)
            dve.wait_ge(setup_dve, setup.more(1))
            V.tensor_tensor(bn_t[:, 2, :], bn_st[:, 1, :], bn_t[:, 1, :], ALU.subtract).then_inc(setup_dve, 1)
            dve.wait_ge(setup_dve, setup.more(1))
            wc = tmp[0:CC + 1, 0:2 * NCV].rearrange("p (c n) -> p c n", c=2)
            for c in range(2):
                V.tensor_scalar(wc[0:CC, c, 0:C], wc[0:CC, c, 0:C], W_SCALE, None, ALU.mult).then_inc(setup_dve, 1)
                dve.wait_ge(setup_dve, setup.more(1))
                V.scalar_tensor_tensor(out=wc[0:CC, c, C:], in0=wc[0:CC, c, C:], scalar=W_SCALE,
                                            in1=bn_t[0:CC, 0, :], op0=ALU.mult, op1=ALU.mult).then_inc(setup_dve, 1)
                dve.wait_ge(setup_dve, setup.more(1))
            V.tensor_scalar(wc[CC:CC + 1, 0, C:], bn_t[CC:CC + 1, 2, :], SPIKE_SCALE, None, ALU.mult).then_inc(setup_dve, 1)
            dve.wait_ge(setup_dve, setup.more(1))
            V.tensor_copy(wc_h[:, :, :], wc).then_inc(setup_dve, 1)
            dve.wait_ge(setup_dve, setup.more(1))
            V.tensor_tensor(wc_l[:, :, :], wc, wc_h[:, :, :], ALU.subtract).then_inc(setup_dve, 1)
            dve.wait_ge(setup_dve, setup.more(1))
            V.memset(gate[:, :, :], 0.0).then_inc(consts_ready, 1)
            first = Aside(front(0, False))
            for n, (kind, c0, w) in enumerate(pieces):
                dve.wait_ge(stage_hi, n + 1)
                rows = slice(TAIL, P) if kind == "tail" else slice(0, P)
                hi = {"head": win_h, "tail": win_t, "out": wout_h_flat}[kind][rows, c0:c0 + w]
                lo = {"head": win_l, "tail": win_t, "out": wout_l_flat}[kind][rows, c0:c0 + w]
                V.scalar_tensor_tensor(out=lo, in0=stage[rows, n % 2, 0:w], scalar=W_SCALE, in1=hi,
                                       op0=ALU.mult, op1=ALU.subtract).then_inc(stage_lo, 1)
                first.until(PIECE_AT[n])
            first.finish()
            attend(0, False)
            with dve.Fori(0, B - 1) as img:
                experts(img, Aside(front(img + 1, True)))
                attend(img + 1, True)
            experts(B - 1, Aside(iter(())))


def constants():
    k = np.zeros((P, K_COLS), np.float32)
    i = np.arange(P)
    k[:, K_ID:K_ID + P] = np.eye(P)
    k[:, K_MKQ:K_MKQ + P] = i[:, None] > i[None, :]
    k[:, K_MQK:K_MQK + P] = i[None, :] > i[:, None]
    c = np.arange(CC)
    per = C // GROUPS
    k[:CC, K_GRP:K_GRP + CC] = (c[:, None] // per == c[None, :] // per) / per
    hd = C // SPIKE_HEADS
    k[:CC, K_BLK:K_BLK + CC] = c[:, None] // hd == c[None, :] // hd
    k[:, K_ROW] = i
    e = np.arange(EXPERTS)
    k[:, K_TIE:] = (e[None, :] < e[:, None]).ravel()
    return k


def kernel(**inputs):
    import concourse.bacc as bacc
    from concourse.bass_utils import run_bass_kernel_spmd

    g = {k: np.asarray(v) for k, v in inputs.items()}
    x = g["x"].reshape(B, C, N)

    def halves(a):
        return a.reshape(2, CC, -1).transpose(1, 0, 2)

    conv = np.concatenate([g[f"L0_conv_{p}_w"].T for p in "qkvp"], axis=1)
    conv = np.concatenate([halves(conv), np.zeros((1, 2, 4 * C), np.float32)])
    rows = np.stack([np.concatenate([g[f"L0_conv_{p}_{what}"] for p in "kvp"])
                     for what in ("gamma", "beta", "mean", "var")])
    bn_q = halves(np.stack([g[f"L0_conv_q_{what}"] for what in ("gamma", "beta", "mean", "var")], axis=1))
    w_in = np.concatenate([g["L1_attn_Wq"], g["L1_attn_Wk"], g["L1_attn_Wv"], g["L1_ffn_gate_w"],
                           g["L1_ffn_w1"].transpose(1, 0, 2).reshape(C, EXPERTS * HID)], axis=1)
    w_in = np.stack([w_in[:P], np.concatenate([w_in[P:], w_in[P:]])])
    w_out = np.zeros((P, OUT_CHUNKS, C), np.float32)
    w_out[:, :CHUNKS] = g["L1_ffn_w2"].reshape(CHUNKS, P, C).transpose(1, 0, 2)
    w_out[:, CHUNKS] = g["L1_attn_Wo"][:P]
    w_out[:TAIL, CHUNKS + 1] = g["L1_attn_Wo"][P:]
    w_out[TAIL, CHUNKS + 1] = g["L1_attn_bo"]
    arrays = {
        "x_ch": x.reshape(B, 2, CC, N).transpose(0, 2, 1, 3),
        "x_tok": x.transpose(0, 2, 1).reshape(B, NT, P, C).transpose(0, 2, 1, 3),
        "consts": constants(),
        "w_conv": conv.reshape(CC + 1, 8 * C),
        "bn_rows": np.broadcast_to(rows, (CC + 1, 4, 3 * C)),
        "bn_q": bn_q,
        "w_in": w_in,
        "w_out": w_out.reshape(P, OUT_CHUNKS * C),
        "b1": g["L1_ffn_b1"].reshape(CHUNKS, P).T,
        "b2": np.broadcast_to(g["L1_ffn_b2"].reshape(1, EXPERTS * C), (2, EXPERTS * C)),
        "gate_b": np.broadcast_to(g["L1_ffn_gate_b"], (P, NT, EXPERTS)),
    }
    arrays = {k: np.ascontiguousarray(v) for k, v in arrays.items()}

    nc = bacc.Bacc("TRN2", target_bir_lowering=False, num_devices=1)
    aps = [nc.dram_tensor(k, a.shape, mybir.dt.from_np(a.dtype), kind="ExternalInput").ap()
           for k, a in arrays.items()]
    out = nc.dram_tensor("out", (B, P, NT, C), F32, kind="ExternalOutput").ap()
    build(nc, *aps, out)
    r = run_bass_kernel_spmd(nc, [arrays], core_ids=[0])
    y = r.results[0]["out"]
    return y.transpose(0, 3, 2, 1).reshape(B, C, 32, 32)
```

```python
from contextlib import ExitStack

import numpy as np

import concourse.bass as bass
from concourse import mybir

F32 = mybir.dt.float32
F16 = mybir.dt.float16
BF16 = mybir.dt.bfloat16
ALU = mybir.AluOpType
ACT = mybir.ActivationFunctionType
AX = mybir.AxisListType

B, C, N = 8, 192, 1024
P = 128
CC = C // 2
NT = N // P
QB = 512
NB = N // QB
TB = QB // P
TAIL = C - P
GROUPS = 32
SPIKE_HEADS = 8
HEADS, D = 6, C // 6
PAIRS = HEADS // 2
EXPERTS, HID = 4, 4 * C
HC = HID // P
CHUNKS = EXPERTS * HC

QK_PARTS = 3
COL_QK, COL_V = 0, 2 * C
COL_GATE = 3 * C
COL_W1 = COL_GATE + EXPERTS
IN_COLS = COL_W1 + EXPERTS * HID
OUT_CHUNKS = CHUNKS + 2

W_SCALE = 2.0 ** 6
U_SCALE = 2.0 ** 8
A_SCALE = 2.0 ** 4
P_SCALE = 2.0 ** 10
M_SCALE = 2.0 ** 8
SPIKE_SCALE = W_SCALE * 4
MAGIC = 1.5 * 2.0 ** 23
MASKED = -1.0e30
SPIKE_ATTN = float(np.float32((C // SPIKE_HEADS) ** -0.5 * 2)) / 64

K_ID, K_MKQ, K_MQK, K_GRP, K_BLK = 0, P, 2 * P, 3 * P, 3 * P + CC
K_ROW, K_TIE = 3 * P + 2 * CC, 3 * P + 2 * CC + 1
K_COLS = K_TIE + EXPERTS * EXPERTS

FRONT_STEPS, TAIL_STEPS = 51, 33

M_ITEMS = [(b, t, half, pair) for b in range(NB) for t in range(b * TB, (b + 1) * TB)
           for half in range(b + 1) for pair in range(PAIRS)]
E_ITEMS = [(b, pair, kc) for b in range(NB) for pair in range(PAIRS) for kc in range((b + 1) * TB)]
NM, NE = len(M_ITEMS), len(E_ITEMS)
PV_LAG = 3
F_LAG = 3
N_P32, N_P16, N_H = 3, 4, 4

TAIL_AT = ({"wo": 22, "residual": 21, "norm": 23, "turn": 26, "high": 27, "low": 27, "scores": 29,
            "gate": 29, "best": 33},
           {"wo": 4, "residual": 4, "norm": 6, "turn": 9, "high": 9, "low": 9, "scores": 10,
            "gate": 10, "best": 13})
FRONT_AT = {"stats": 3, "sums": 4.5, "sums2": 5.5, "variance": 5.5, "clip": 5.5, "xs": 8.5,
            "q": 10.5, "q_int": 11.5, "kv": 12.5, "kv_int": 13, "kvm": 16.5, "kvm_split": 17.5,
            "attn": 18.5, "attn_int": 18.5, "p": 19.5, "residual": 19.5, "norm": 22, "turn": 24,
            "high": 25, "low": 25, "qk": 26, "qk_lo": 26, "v": 30, "v_lo": 29, "maxima": 34.5}
PIECE_AT = tuple(3 * (n + 1) for n in range(7))
PER_CHUNK = 2.75
NORM_PARTS = 3
PV_BANK = (0, 1, 0, 1, 0, 3)


def high_by_act(j):
    return j not in (4, 12, 14, 18, 20, 26, 28, 30)


def highs(j, by_act):
    return sum(high_by_act(i) == by_act for i in range(j + 1))


def maximum_step(i):
    return FRONT_AT["maxima"] + int(2 * i / PER_CHUNK) / 2


class Aside:

    def __init__(self, part):
        self.part = part
        self.due = next(part, None)

    def until(self, step):
        while self.due is not None and self.due <= step:
            self.due = next(self.part, None)

    def finish(self):
        while self.due is not None:
            self.due = next(self.part, None)


class Count:

    def __init__(self):
        self.n = 0

    def more(self, n):
        self.n += n
        return self.n


def run_ends():
    return [j for j, (b, pair, kc) in enumerate(E_ITEMS) if kc == (b + 1) * TB - 1]


def build(nc, x_ch, x_tok, consts, w_conv, bn_rows, bn_q, w_in, w_out, b1, b2, gate_b, out):
    with ExitStack() as ctx:
        def sb(name, shape, dt):
            return ctx.enter_context(nc.sbuf_tensor(name, shape, dt))

        per_image = {}

        def sem(name, gain=0):
            handle = ctx.enter_context(nc.semaphore(name))
            per_image[handle.name] = gain
            return handle

        def at(s, img, n):
            return img * per_image[s.name] + n

        def whole(s):
            return per_image[s.name]

        kst = sb("kst", [P, K_COLS], F32)
        ident16 = sb("ident16", [P, P], F16)
        identb = sb("identb", [P, P], BF16)
        mask_kq = sb("mask_kq", [P, P], BF16)
        mask_qk = sb("mask_qk", [P, P], BF16)
        ones16 = sb("ones16", [P, P], F16)
        exp_bias = sb("exp_bias", [P, 1], F32)
        ident = kst[:, K_ID:K_ID + P]
        group = kst[0:CC, K_GRP:K_GRP + CC]
        block_diag = kst[0:CC, K_BLK:K_BLK + CC]
        NCV = 4 * C
        wc_h = sb("wc_h", [CC + 1, 2, NCV], F16)
        wc_l = sb("wc_l", [CC + 1, 2, NCV], F16)
        q_sb = sb("q_sb", [CC, 2, 2], F32)
        win_h = sb("win_h", [P, IN_COLS], F16)
        win_l = sb("win_l", [P, IN_COLS], F16)
        win_t = sb("win_t", [P, IN_COLS], F16)
        wout_h = sb("wout_h", [P, OUT_CHUNKS, C], F16)
        wout_l = sb("wout_l", [P, OUT_CHUNKS, C], F16)
        b1_sb = sb("b1_sb", [P, CHUNKS], F32)
        b2_sb = sb("b2_sb", [2, EXPERTS * C], F16)
        gb_sb = sb("gb_sb", [P, NT, EXPERTS], F32)

        xc = sb("xc", [CC, 2, N], F32)
        xt = sb("xt", [P, NT, C], F32)
        tmp = sb("tmp", [P, NT * 2 * C], F32)
        xs = sb("xs", [CC + 1, 2, N], F16)
        ai = xs
        kv32 = sb("kv32", [CC, 2, CC], F32)
        kv_h = sb("kv_h", [CC, 2, CC], F16)
        kv_l = sb("kv_l", [CC, 2, CC], F16)
        t1 = sb("t1", [P, NT, C], F32)
        acc = sb("acc", [P, NT, C], F32)
        u = sb("u", [P, NT, 2 * P], F32)
        ah = sb("ah", [P, 2, N], F16)
        al = sb("al", [P, 2, N], F16)
        uh = sb("uh", [P, 2, N], F16)
        ul = sb("ul", [P, 2, N], F16)
        qk_all = sb("qk_all", [P, 2 * QK_PARTS * N], F16)
        qk = qk_all[:, :].rearrange("p (half j n) -> p half j n", half=2, j=QK_PARTS)
        qk4 = sb("qk4", [CC + 2, 2, HEADS, N], F16)
        q4, k4 = qk4[:, 0, :, :], qk4[:, 1, :, :]
        ROWS = ((0, 0), (0, 1), (1, 0))
        v_h = sb("v_h", [P, NT, C], F16)
        v_l = sb("v_l", [P, NT, C], F16)
        room32 = sb("room32", [P, N_P32 * 2 * QB], F32)
        p32 = room32[:, :].rearrange("p (s a n) -> p s a n", s=N_P32, a=2)
        as16 = room32[:, :].bitcast(F16)
        kvi = as16[:, 0:NT * 2 * C].rearrange("p (t c) -> p t c", t=NT)
        qi = as16[0:CC, 2 * NT * C:2 * NT * C + 2 * N].rearrange("p (c n) -> p c n", c=2)
        room16 = sb("room16", [P, 2 * N_P16 * 2 * QB], F16)
        half = N_P16 * 2 * QB
        p_h = room16[:, 0:half].rearrange("p (s a n) -> p s a n", s=N_P16, a=2)
        p_l = room16[:, half:2 * half].rearrange("p (s a n) -> p s a n", s=N_P16, a=2)
        h32 = room16[:, 0:half].bitcast(F32).rearrange("p (s n) -> p s n", s=N_H)
        h_h = room16[:, half:half + N_H * QB].rearrange("p (s n) -> p s n", s=N_H)
        h_l = room16[:, half + N_H * QB:2 * half].rearrange("p (s n) -> p s n", s=N_H)
        stage = room16[:, :].bitcast(F32).rearrange("p (s n) -> p s n", s=2)
        o32 = tmp[:, 0:2 * N].rearrange("p (c n) -> p c n", c=2)
        rden = tmp[0:2 * D, 2 * N:2 * N + QB]
        o_h = sb("o_h", [P, 2, N], F16)
        o_l = sb("o_l", [P, 2, N], F16)

        gn_st = sb("gn_st", [CC, 2, 2, 6], F32)
        gn_s = sb("gn_s", [CC, 2], F32)
        gn_d = sb("gn_d", [CC, 2, 4], F32)
        gn_v = sb("gn_v", [CC, 2], F32)
        gn_m = sb("gn_m", [CC, 2], F32)
        gn_b = sb("gn_b", [CC, 2], F32)
        g_st = [sb("g_var", [CC, 2], F32), sb("g_pow", [CC, 2], F32), sb("g_tmp", [CC, 2], F32)]
        g_rstd = sb("g_rstd", [CC, 2], F32)

        class Norm:

            def __init__(self, name, tiles):
                self.stats = sb(name + "_stats", [P, tiles, 6], F32)
                self.sums = sb(name + "_sums", [P, 3, tiles], F32)
                self.mean = sb(name + "_mean", [P, tiles], F32)
                self.var = sb(name + "_var", [P, tiles], F32)
                self.pow = sb(name + "_pow", [P, tiles], F32)
                self.tmp = sb(name + "_tmp", [P, tiles], F32)
                self.rstd = sb(name + "_rstd", [P, tiles], F32)

        norm1, norm2 = Norm("norm1", NT), Norm("norm2", TB)
        minus_half = sb("minus_half", [P, NT], F32)
        euler = sb("euler", [P, TB, EXPERTS], F32)
        mx = sb("mx", [P, 2, NT, HEADS], F32)
        m16 = sb("m16", [P, NT, HEADS, 2], F16)
        mrow = sb("mrow", [2 * HEADS, N], F16)
        gsc = sb("gsc", [P, TB, EXPERTS], F32)
        gex = sb("gex", [P, TB, EXPERTS], F32)
        gpr = sb("gpr", [P, TB, EXPERTS], F32)
        gt1 = sb("gt1", [P, TB], F32)
        gt2 = sb("gt2", [P, TB], F32)
        gcmp = sb("gcmp", [P, TB, EXPERTS, EXPERTS], F32)
        gcm2 = sb("gcm2", [P, TB, EXPERTS, EXPERTS], F32)
        gcnt = sb("gcnt", [P, TB, EXPERTS], F32)
        gate = sb("gate", [P, NT, EXPERTS], F32)

        b2_ones = sb("b2_ones", [2, P], F16)

        bn_st = qk_all[0:CC + 1, 0:24 * C].bitcast(F32).rearrange("p (k c) -> p k c", k=4)
        bn_t = room32[0:CC + 1, 0:9 * C].rearrange("p (k c) -> p k c", k=3)
        bq_st = sb("bq_st", [CC, 2, 4], F32)
        bq_t = sb("bq_t", [CC, 4, 2], F32)
        b2_st = room32[0:2, 9 * C:13 * C]
        b2_t = room32[0:2, 13 * C:15 * C].bitcast(F16)

        ps = ctx.enter_context(nc.psum_tensor("ps", [P, 8, QB], F32))

        small_in = sem("small_in")
        stage_in = [sem("stage_in0"), sem("stage_in1")]
        stage_hi = sem("stage_hi")
        stage_lo = sem("stage_lo")
        setup_dve = sem("setup_dve")
        setup_pool = sem("setup_pool")
        setup_act = sem("setup_act")
        consts_ready = sem("consts_ready")

        x_ch_in = sem("x_ch_in", 16)
        x_tok_in = sem("x_tok_in", 16)
        front_step = sem("front_step", FRONT_STEPS)
        gn_rhs = sem("gn_rhs", 2)
        gn_ps = sem("gn_ps", 2)
        var_ready = sem("var_ready", 2)
        pow_done = sem("pow_done", 2)
        gn_ready = sem("gn_ready", 1)
        x_relu = sem("x_relu", 2)
        xs_ready = sem("xs_ready", 2)
        q_ps = sem("q_ps", 2 * NB)
        q_relu = sem("q_relu", 2 * NB)
        kv_ps = sem("kv_ps", NT)
        kv_relu = sem("kv_relu", NT)
        q_int = sem("q_int", NB)
        kv_int = sem("kv_int", NT // 2)
        kvm_ps = sem("kvm_ps", 1)
        kv_split = sem("kv_split", 1)
        at_ps = sem("at_ps", NB)
        a_int = sem("a_int", NB)
        p_ps = sem("p_ps", NT // 2)
        t1_ready = sem("t1_ready", 1)
        a_ready = sem("a_ready", NB)
        a_tr = sem("a_tr", NB)
        ah_done = sem("ah_done", NB)
        al_done = sem("al_done", NB)
        qk_ps = sem("qk_ps", QK_PARTS * NB)
        qk_hi = sem("qk_hi", QK_PARTS * NB)
        qk_lo = sem("qk_lo", QK_PARTS * NB)
        heads_in = [sem("heads_in0", 16 * 2 * 3 * 4), sem("heads_in1", 16 * 2 * 3 * 4)]
        v_ps = sem("v_ps", NT // 2)
        v_hi = sem("v_hi", NT // 2)
        v_lo = sem("v_lo", NT // 2)
        m_ps = sem("m_ps", NM)
        m_used = sem("m_used", NM)
        m_split = sem("m_split", NB)
        mrow_ps = sem("mrow_ps", NB)
        mrow_done = sem("mrow_done", NB)
        mrow_in = [sem("mrow_in0", 16 * HEADS), sem("mrow_in1", 16 * HEADS)]
        e_ps = sem("e_ps", NE)
        e_done = sem("e_done", NE)
        p_hi_dve = sem("p_hi_dve", highs(NE - 1, False))
        p_hi_act = sem("p_hi_act", highs(NE - 1, True))
        p_lo_dve = sem("p_lo_dve", (NE + 1) // 2)
        p_lo_pool = sem("p_lo_pool", NE // 2)
        pv_done = sem("pv_done", NE)
        rden_ready = sem("rden_ready", NORM_PARTS * NB * PAIRS)
        o_done = sem("o_done", NB * PAIRS)
        o_hi = sem("o_hi", NB * PAIRS)
        o_lo = sem("o_lo", NB * PAIRS)
        tail_step = sem("tail_step", NB * TAIL_STEPS)
        wo_ps = sem("wo_ps", NT // 2)
        var2_ready = sem("var2_ready", NB)
        pow2_done = sem("pow2_done", NB)
        u_ready = sem("u_ready", NB)
        u_tr = sem("u_tr", NB)
        uh_done = sem("uh_done", NB)
        ul_done = sem("ul_done", NB)
        gate_ps = sem("gate_ps", NB)
        gate_used = sem("gate_used", NB)
        gate_sub = sem("gate_sub", NB)
        gate_exp = sem("gate_exp", NB)
        h_ps = sem("h_ps", NB * CHUNKS)
        h_act = sem("h_act", NB * CHUNKS)
        h_hi = sem("h_hi", NB * CHUNKS)
        h_lo = sem("h_lo", NB * CHUNKS)
        f2_done = sem("f2_done", NB * CHUNKS)
        y_used = sem("y_used", NB * EXPERTS)
        stored = sem("stored", 16 * NB)

        W = 2048
        pieces = [(kind, c0, min(W, IN_COLS - c0)) for kind in ("head", "tail")
                  for c0 in range(0, IN_COLS, W)]
        FLAT = OUT_CHUNKS * C
        pieces += [("out", c0, min(W, FLAT - c0)) for c0 in range(0, FLAT, W)]
        n_small = 7
        wout_h_flat = wout_h[:, :, :].rearrange("p k c -> p (k c)")
        wout_l_flat = wout_l[:, :, :].rearrange("p k c -> p (k c)")

        block = ctx.enter_context(nc.Block())

        @block.sync
        def _(sp):
            def load(img, later):
                if later:
                    sp.wait_ge(xs_ready, at(xs_ready, img, 0))
                sp.dma_start(xc[:, :, :], x_ch[img]).then_inc(x_ch_in, 16)
                if later:
                    sp.wait_ge(t1_ready, at(t1_ready, img, 0))
                sp.dma_start(xt[:, :, :], x_tok[img]).then_inc(x_tok_in, 16)

            def spread(img):
                for b in range(NB):
                    tok = slice(b * QB, (b + 1) * QB)
                    sp.wait_ge(qk_hi, at(qk_hi, img, QK_PARTS * (b + 1)))
                    sp.wait_ge(qk_lo, at(qk_lo, img, QK_PARTS * (b + 1)))
                    for r in range(4):
                        row = slice(D * r, D * r + D)
                        for n, (q, k) in enumerate(ROWS):
                            dst = slice(D * n, D * n + D)
                            if r < 2:
                                sp.dma_start(q4[dst, r:HEADS:4, tok], qk[row, q, 0:3:2, tok])\
                                  .then_inc(heads_in[b], 16)
                                sp.dma_start(k4[dst, r, tok], qk[row, k, 1, tok]).then_inc(heads_in[b], 16)
                            else:
                                sp.dma_start(q4[dst, r, tok], qk[row, q, 0, tok]).then_inc(heads_in[b], 16)
                                sp.dma_start(k4[dst, r:HEADS:2, tok], qk[row, k, 1:3, tok])\
                                  .then_inc(heads_in[b], 16)
                for b in range(NB):
                    sp.wait_ge(mrow_done, at(mrow_done, img, b + 1))
                    for h in range(HEADS):
                        sp.dma_start(q4[3 * D:3 * D + 2, h, b * QB:(b + 1) * QB],
                                     mrow[2 * h:2 * h + 2, b * QB:(b + 1) * QB])\
                          .then_inc(mrow_in[b], 16)

            for dst, src in ((kst[:, :], consts), (bn_st[:, :, :], bn_rows), (bq_st[:, :, :], bn_q),
                             (b1_sb[:, :], b1), (b2_st[:, :], b2), (gb_sb[:, :, :], gate_b),
                             (tmp[0:CC + 1, 0:2 * NCV], w_conv)):
                sp.dma_start(dst, src).then_inc(small_in, 16)
            load(0, False)
            for n, (kind, c0, w) in enumerate(pieces):
                if n >= 2:
                    sp.wait_ge(stage_lo, n - 1)
                src = {"head": w_in[0], "tail": w_in[1], "out": w_out}[kind][:, c0:c0 + w]
                sp.dma_start(stage[:, n % 2, 0:w], src).then_inc(stage_in[n % 2], 16)

            with sp.Fori(0, B - 1) as img:
                spread(img)
                load(img + 1, True)
            spread(B - 1)

        @block.tensor
        def _(pe):
            def project(dst, high, low, cols, tok, tokens_stationary):
                for n, (w, a, c) in enumerate(((win_h, high, 0), (win_l, high, 0), (win_h, low, 0),
                                               (win_t, high, 1), (win_t, low, 1))):
                    lhs, rhs = w[:, cols], a[:, c, tok]
                    if tokens_stationary:
                        lhs, rhs = rhs, lhs
                    mm = pe.matmul(dst, lhs, rhs, start=(n == 0), stop=(n == 4))
                return mm

            def transpose_block(b, bank):
                for t in range(TB):
                    for c in range(2):
                        mm = pe.transpose(ps[:, bank + c, t * P:(t + 1) * P],
                                          u[:, b * TB + t, c * P:(c + 1) * P], ident)
                return mm

            def maximum_rows(img, b, bank):
                pe.wait_ge(m_split, at(m_split, img, b + 1))
                for t in range(TB):
                    mm = pe.matmul(ps[0:2 * HEADS, bank, t * P:(t + 1) * P],
                                   m16[:, b * TB + t, :, :].rearrange("p h two -> p (h two)"),
                                   ident16[:, :], start=True, stop=True)
                mm.then_inc(mrow_ps, 1)

            def scores(img, j):
                b, pair, kc = E_ITEMS[j]
                if j < 2:
                    pe.wait_ge(m_used, at(m_used, img, NM))
                else:
                    pe.wait_ge(e_done, at(e_done, img, j - 1))
                if pair == 0 and kc == 0:
                    pe.wait_ge(mrow_in[b], at(mrow_in[b], img, whole(mrow_in[b])))
                q0 = max(0, kc - b * TB) * P
                for a in range(2):
                    h = 2 * pair + a
                    bank = 4 + 2 * (j % 2) + a
                    diagonal = kc >= b * TB
                    mm = pe.matmul(ps[:, bank, q0:QB], k4[:, h, kc * P:(kc + 1) * P],
                                   q4[:, h, b * QB + q0:(b + 1) * QB], start=True, stop=not diagonal)
                    if diagonal:
                        mm = pe.matmul(ps[:, bank, q0:q0 + P], identb[:, :],
                                       mask_kq[:, :], start=False, stop=True)
                mm.then_inc(e_ps, 1)

            def front(img, later):
                yield FRONT_AT["sums"]
                pe.wait_ge(gn_rhs, at(gn_rhs, img, 1))
                if later:
                    pe.wait_ge(e_done, at(e_done, img, 0))
                pe.matmul(ps[0:CC, 7, 0:2], group, gn_s[:, :], start=True, stop=True)\
                  .then_inc(gn_ps, 1)
                yield FRONT_AT["sums2"]
                pe.wait_ge(gn_rhs, at(gn_rhs, img, 2))
                pe.matmul(ps[0:CC, 7, 2:4], group, gn_v[:, :], start=True, stop=True)\
                  .then_inc(gn_ps, 1)

                for b in range(NB):
                    yield FRONT_AT["q"] + 2 * b
                    if b == 0:
                        pe.wait_ge(xs_ready, at(xs_ready, img, 2))
                    elif later:
                        pe.wait_ge(gate_used, at(gate_used, img, 0))
                    for m in range(2):
                        for n, (w, c) in enumerate(((wc_h, 0), (wc_l, 0), (wc_h, 1), (wc_l, 1))):
                            mm = pe.matmul(ps[0:CC, 6 - 2 * b + m, :], w[0:CC, c, m * CC:(m + 1) * CC],
                                           xs[0:CC, c, b * QB:(b + 1) * QB], start=(n == 0), stop=(n == 3))
                        mm.then_inc(q_ps, 1)
                for t in range(NT):
                    if t % 2 == 0:
                        yield FRONT_AT["kv"] + t // 2
                    if t < 4:
                        pe.wait_ge(q_relu, at(q_relu, img, t + 1))
                    else:
                        pe.wait_ge(kv_relu, at(kv_relu, img, t - 3))
                    for n, (w, c) in enumerate(((wc_h, 0), (wc_l, 0), (wc_h, 1), (wc_l, 1))):
                        rows = CC + 1 if c == 0 else CC
                        mm = pe.matmul(ps[:, 4 + (t + 2) % 4, 0:2 * C], xs[0:rows, c, t * P:(t + 1) * P],
                                       w[0:rows, c, C:3 * C], start=(n == 0), stop=(n == 3))
                    mm.then_inc(kv_ps, 1)
                yield FRONT_AT["kvm"] + 0.5
                pe.wait_ge(kv_int, at(kv_int, img, NT // 2))
                for m in range(2):
                    for t in range(NT):
                        mm = pe.matmul(ps[0:CC, 4, m * CC:(m + 1) * CC], kvi[:, t, m * CC:(m + 1) * CC],
                                       kvi[:, t, C + m * CC:C + (m + 1) * CC],
                                       start=(t == 0), stop=(t == NT - 1))
                mm.then_inc(kvm_ps, 1)
                for b in range(NB):
                    yield FRONT_AT["attn"] + b
                    pe.wait_ge(kv_split, at(kv_split, img, 1))
                    pe.wait_ge(q_int, at(q_int, img, b + 1))
                    for m in range(2):
                        for n, w in enumerate((kv_h, kv_l)):
                            mm = pe.matmul(ps[0:CC, 4 + 2 * b + m, :], w[:, m, :],
                                           qi[:, m, b * QB:(b + 1) * QB], start=(n == 0), stop=(n == 1))
                    mm.then_inc(at_ps, 1)
                for t in range(NT):
                    if t % TB == 0:
                        yield FRONT_AT["p"] + t // TB
                        pe.wait_ge(a_int, at(a_int, img, t // TB + 1))
                    for n, (w, c) in enumerate(((wc_h, 0), (wc_l, 0), (wc_h, 1), (wc_l, 1))):
                        rows = CC + 1 if c == 0 else CC
                        mm = pe.matmul(ps[:, 4 + t // 2, (t % 2) * C:(t % 2 + 1) * C],
                                       ai[0:rows, c, t * P:(t + 1) * P], w[0:rows, c, 3 * C:4 * C],
                                       start=(n == 0), stop=(n == 3))
                    if t % 2:
                        mm.then_inc(p_ps, 1)

                for b in range(NB):
                    yield FRONT_AT["turn"] + b + 0.5
                    pe.wait_ge(a_ready, at(a_ready, img, b + 1))
                    transpose_block(b, 4 + 2 * b).then_inc(a_tr, 1)
                for i in range(QK_PARTS * NB):
                    b, j = divmod(i, QK_PARTS)
                    yield FRONT_AT["qk"] + i // 2 + (0.5 if i % 2 else 0)
                    pe.wait_ge(al_done, at(al_done, img, 1 if i < 2 else 2))
                    if i >= 4:
                        pe.wait_ge(qk_lo, at(qk_lo, img, i - 3))
                    project(ps[:, 4 + i % 4, :], ah, al, slice(COL_QK + j * P, COL_QK + (j + 1) * P),
                            slice(b * QB, (b + 1) * QB), False).then_inc(qk_ps, 1)
                for t in range(NT):
                    if t % 4 == 0:
                        yield FRONT_AT["v"] + t // 4
                    if t % 2 == 0:
                        pe.wait_ge(qk_lo, at(qk_lo, img, min(5 + t // 2, QK_PARTS * NB)))
                    mm = project(ps[:, 4 + t // 2, (t % 2) * C:(t % 2 + 1) * C], ah, al,
                                 slice(COL_V, COL_V + C), slice(t * P, (t + 1) * P), True)
                    if t % 2:
                        mm.then_inc(v_ps, 1)

                for i, (b, t, half, pair) in enumerate(M_ITEMS):
                    yield maximum_step(i)
                    if i == 0:
                        pe.wait_ge(heads_in[0], at(heads_in[0], img, whole(heads_in[0])))
                    if i == NM // 3:
                        pe.wait_ge(heads_in[1], at(heads_in[1], img, whole(heads_in[1])))
                    if i < 2:
                        pe.wait_ge(v_lo, at(v_lo, img, 2 * i + 2))
                    else:
                        pe.wait_ge(m_used, at(m_used, img, i - 1))
                    if i == NM // 2:
                        pe.wait_ge(mrow_done, at(mrow_done, img, 1))
                    diagonal = half == b
                    width = (t % TB + 1) * P if diagonal else QB
                    for a in range(2):
                        h = 2 * pair + a
                        bank = 4 + 2 * (i % 2) + a
                        mm = pe.matmul(ps[:, bank, 0:width], q4[0:3 * D, h, t * P:(t + 1) * P],
                                       k4[0:3 * D, h, half * QB:half * QB + width],
                                       start=True, stop=not diagonal)
                        if diagonal:
                            mm = pe.matmul(ps[:, bank, width - P:width], identb[:, :],
                                           mask_qk[:, :], start=False, stop=True)
                    mm.then_inc(m_ps, 1)
                    if i == NM // 2 - 1:
                        pe.wait_ge(m_used, at(m_used, img, i))
                        maximum_rows(img, 0, 4)
                for j in range(2):
                    yield NB * CHUNKS + j + 0.5
                    scores(img, j)

            def tail(img, b, later):
                when, bank = TAIL_AT[b], 2 + 2 * b
                yield when["wo"]
                if b:
                    pe.wait_ge(e_done, at(e_done, img, NE))
                pe.wait_ge(o_hi, at(o_hi, img, (b + 1) * PAIRS))
                pe.wait_ge(o_lo, at(o_lo, img, (b + 1) * PAIRS))
                A, BB = CHUNKS, CHUNKS + 1
                for t in range(b * TB, (b + 1) * TB):
                    tok = slice(t * P, (t + 1) * P)
                    terms = ((o_h[:, 0, tok], wout_h[:, A, :]), (o_h[:, 0, tok], wout_l[:, A, :]),
                             (o_l[:, 0, tok], wout_h[:, A, :]),
                             (o_h[0:TAIL + 1, 1, tok], wout_h[0:TAIL + 1, BB, :]),
                             (o_h[0:TAIL + 1, 1, tok], wout_l[0:TAIL + 1, BB, :]),
                             (o_l[0:TAIL + 1, 1, tok], wout_h[0:TAIL + 1, BB, :]))
                    for n, (lhs, rhs) in enumerate(terms):
                        mm = pe.matmul(ps[:, bank + t % TB // 2, (t % 2) * C:(t % 2 + 1) * C], lhs, rhs,
                                       start=(n == 0), stop=(n == 5))
                    if t % 2:
                        mm.then_inc(wo_ps, 1)
                yield when["turn"]
                pe.wait_ge(u_ready, at(u_ready, img, b + 1))
                transpose_block(b, bank).then_inc(u_tr, 1)
                yield when["scores"]
                pe.wait_ge(ul_done, at(ul_done, img, b + 1))
                for t in range(TB):
                    mm = project(ps[:, bank, t * EXPERTS:(t + 1) * EXPERTS], uh, ul,
                                 slice(COL_GATE, COL_GATE + EXPERTS),
                                 slice((b * TB + t) * P, (b * TB + t + 1) * P), True)
                mm.then_inc(gate_ps, 1)

            def attend(img, later):
                def weigh(j):
                    b, pair, kc = E_ITEMS[j]
                    run = b * PAIRS + pair
                    bank = PV_BANK[run]
                    q0 = max(0, kc - b * TB) * P
                    last = kc == (b + 1) * TB - 1
                    if kc == 0:
                        if run == NB * PAIRS - 1:
                            pe.wait_ge(ul_done, at(ul_done, img, 1))
                        elif run >= 2:
                            pe.wait_ge(o_done, at(o_done, img, run - 1))
                        elif later:
                            pe.wait_ge(h_act, at(h_act, img, 0))
                    if high_by_act(j):
                        pe.wait_ge(p_hi_act, at(p_hi_act, img, highs(j, True)))
                    else:
                        pe.wait_ge(p_hi_dve, at(p_hi_dve, img, highs(j, False)))
                    s = j % N_P16
                    for n, (probs, low_v) in enumerate(((p_h, True), (p_h, False), (p_l, False))):
                        if n == 2:
                            if j % 2:
                                pe.wait_ge(p_lo_pool, at(p_lo_pool, img, j // 2 + 1))
                            else:
                                pe.wait_ge(p_lo_dve, at(p_lo_dve, img, j // 2 + 1))
                        for a in range(2):
                            h = 2 * pair + a
                            v = (v_l if low_v else v_h)[:, kc, h * D:(h + 1) * D]
                            mm = pe.matmul(ps[a * D:(a + 1) * D, bank, q0:QB], v, probs[:, s, a, q0:QB],
                                           start=(kc == 0 and n == 0), stop=(last and n == 2))
                        if not low_v:
                            for a in range(2):
                                mm = pe.matmul(ps[(2 + a) * D:(3 + a) * D, bank, q0:QB], ones16[:, 0:D],
                                               probs[:, s, a, q0:QB], start=(kc == 0 and n == 1),
                                               stop=(last and n == 2))
                    mm.then_inc(pv_done, 1)

                aside = Aside(tail(img, 0, later))
                for j in range(NE + PV_LAG):
                    if 2 <= j < NE:
                        scores(img, j)
                    if j == 4:
                        if later:
                            pe.wait_ge(y_used, at(y_used, img, 0))
                        maximum_rows(img, 1, 3)
                    if j >= PV_LAG:
                        weigh(j - PV_LAG)
                    aside.until(j)
                aside.finish()

            def experts(img, following):
                def hidden(i):
                    b, n = divmod(i, CHUNKS)
                    if i < 2:
                        pe.wait_ge(o_done, at(o_done, img, NB * PAIRS - 1 - i))
                    else:
                        pe.wait_ge(h_act, at(h_act, img, i - 1))
                    if n == 0:
                        pe.wait_ge(ul_done, at(ul_done, img, b + 1))
                    col = COL_W1 + n * P
                    project(ps[:, i % 2, :], uh, ul, slice(col, col + P), slice(b * QB, (b + 1) * QB), False)\
                        .then_inc(h_ps, 1)

                def expert_out(i):
                    b, n = divmod(i, CHUNKS)
                    e, k = divmod(n, HC)
                    if k == 0:
                        if i == 0:
                            pe.wait_ge(gate_used, at(gate_used, img, 1))
                            pe.wait_ge(o_done, at(o_done, img, NB * PAIRS))
                        else:
                            pe.wait_ge(y_used, at(y_used, img, i // HC))
                    pe.wait_ge(h_lo, at(h_lo, img, i + 1))
                    s = i % N_H
                    for t in range(TB):
                        dst = ps[:, 2 + t // 2, (t % 2) * C:(t % 2 + 1) * C]
                        tok = slice(t * P, (t + 1) * P)
                        for m, (hid, w) in enumerate(((h_h, wout_h), (h_h, wout_l), (h_l, wout_h))):
                            mm = pe.matmul(dst, hid[:, s, tok], w[:, n, :],
                                           start=(k == 0 and m == 0 and t % 2 == 0), stop=False,
                                           skip_group_check=True)
                        if k == HC - 1:
                            mm = pe.matmul(dst, b2_ones[:, :], b2_sb[:, e * C:(e + 1) * C],
                                           start=False, stop=True, skip_group_check=True)
                    mm.then_inc(f2_done, 1)

                aside = Aside(tail(img, 1, True))
                for i in range(NB * CHUNKS + F_LAG):
                    if i < NB * CHUNKS:
                        hidden(i)
                    following.until(i - 0.5)
                    if i >= F_LAG and (i - F_LAG) % HC == 0:
                        aside.until(i)
                        following.until(i)
                    if i >= F_LAG:
                        expert_out(i - F_LAG)
                    aside.until(i)
                    following.until(i)
                following.finish()

            pe.wait_ge(consts_ready, 1)
            first = Aside(front(0, False))
            first.until(FRONT_AT["turn"])
            pe.wait_ge(stage_lo, len(pieces))
            first.finish()
            attend(0, False)
            with pe.Fori(0, B - 1) as img:
                experts(img, Aside(front(img + 1, True)))
                attend(img + 1, True)
            experts(B - 1, Aside(iter(())))

        @block.scalar
        def _(act):
            def rows_of_maxima(img, b, bank):
                act.wait_ge(mrow_ps, at(mrow_ps, img, b + 1))
                act.activation(mrow[:, b * QB:(b + 1) * QB], ps[0:2 * HEADS, bank, :], ACT.Copy)\
                   .then_inc(mrow_done, 1)

            def front(img, later):
                yield FRONT_AT["xs"] - 1
                act.wait_ge(gn_ready, at(gn_ready, img, 1))
                if later:
                    act.wait_ge(o_lo, at(o_lo, img, 0))
                tx = tmp[0:CC, 0:2 * N].rearrange("p (c n) -> p c n", c=2)
                for c in range(2):
                    yield FRONT_AT["xs"] - 1 + c
                    act.activation(tx[:, c, :], xc[:, c, :], ACT.Relu, scale=g_rstd[:, c:c + 1],
                                   bias=gn_b[:, c:c + 1]).then_inc(x_relu, 1)
                for i in range(2 * NB):
                    b, m = divmod(i, 2)
                    if m == 0:
                        yield FRONT_AT["q"] + 2 * b
                    act.wait_ge(q_ps, at(q_ps, img, i + 1))
                    act.activation(tx[:, m, b * QB:(b + 1) * QB], ps[0:CC, 6 - 2 * b + m, :], ACT.Relu,
                                   scale=q_sb[:, m, 0:1], bias=q_sb[:, m, 1:2]).then_inc(q_relu, 1)
                for t in range(NT):
                    if t % 2 == 0:
                        yield FRONT_AT["kv"] + t // 2
                    if t == 0:
                        act.wait_ge(q_int, at(q_int, img, NB))
                    act.wait_ge(kv_ps, at(kv_ps, img, t + 1))
                    act.activation(tmp[:, t * 2 * C:(t + 1) * 2 * C], ps[:, 4 + (t + 2) % 4, 0:2 * C],
                                   ACT.Relu, scale=1 / SPIKE_SCALE).then_inc(kv_relu, 1)
                for b in range(NB):
                    yield FRONT_AT["high"] + b
                    act.wait_ge(a_tr, at(a_tr, img, b + 1))
                    act.activation(ah[:, :, b * QB:(b + 1) * QB], ps[:, 4 + 2 * b:6 + 2 * b, :],
                                   ACT.Copy, scale=U_SCALE).then_inc(ah_done, 1)
                for i in range(QK_PARTS * NB):
                    b, j = divmod(i, QK_PARTS)
                    yield FRONT_AT["qk"] + (i + 1) // 2
                    act.wait_ge(qk_ps, at(qk_ps, img, i + 1))
                    act.activation(qk[:, 0, j, b * QB:(b + 1) * QB], ps[:, 4 + i % 4, :], ACT.Copy,
                                   scale=A_SCALE / (U_SCALE * W_SCALE)).then_inc(qk_hi, 1)
                for t in range(0, NT, 2):
                    if t % 4 == 0:
                        yield FRONT_AT["v"] + t // 4
                    if t == 0:
                        if later:
                            act.wait_ge(pv_done, at(pv_done, img, 0))
                    act.wait_ge(v_ps, at(v_ps, img, t // 2 + 1))
                    act.activation(v_h[:, t:t + 2, :],
                                   ps[:, 4 + t // 2, 0:2 * C].rearrange("p (t c) -> p t c", t=2), ACT.Copy,
                                   scale=A_SCALE / (U_SCALE * W_SCALE)).then_inc(v_hi, 1)
                yield maximum_step(NM // 2 - 1)
                rows_of_maxima(img, 0, 4)

            def high_of_output(img, run):
                b, pair = divmod(run, PAIRS)
                act.wait_ge(o_done, at(o_done, img, run + 1))
                rows = slice(2 * D * (pair % 2), 2 * D * (pair % 2) + 2 * D)
                act.activation(o_h[rows, pair // 2, b * QB:(b + 1) * QB],
                               o32[rows, pair // 2, b * QB:(b + 1) * QB], ACT.Copy)\
                   .then_inc(o_hi, 1)

            def store(img, b):
                act.wait_ge(y_used, at(y_used, img, (b + 1) * EXPERTS))
                act.dma_start(out[img, :, b * TB:(b + 1) * TB, :], acc[:, b * TB:(b + 1) * TB, :])\
                   .then_inc(stored, 16)

            def tail(img, b):
                when, bank = TAIL_AT[b], 2 + 2 * b
                if b == 1:
                    yield 1
                    high_of_output(img, NB * PAIRS - 1)
                yield when["high"]
                act.wait_ge(u_tr, at(u_tr, img, b + 1))
                act.activation(uh[:, :, b * QB:(b + 1) * QB], ps[:, bank:bank + 2, :],
                               ACT.Copy, scale=U_SCALE).then_inc(uh_done, 1)
                if b == 0:
                    yield when["gate"]
                    act.wait_ge(gate_sub, at(gate_sub, img, 1))
                    act.activation(gex[:, :, :], gsc[:, :, :], ACT.Exp).then_inc(gate_exp, 1)

            def attend(img, previous=None):
                aside = Aside(tail(img, 0))
                if previous is not None:
                    act.wait_ge(h_lo, at(h_lo, img, 0))
                ends = run_ends()
                run = 0
                for j, (b, pair, kc) in enumerate(E_ITEMS):
                    act.wait_ge(e_ps, at(e_ps, img, j + 1))
                    q0 = max(0, kc - b * TB) * P
                    bank = 4 + 2 * (j % 2)
                    scale = float(1 / (A_SCALE * A_SCALE * np.sqrt(D)))
                    if j == 1 and previous is not None:
                        act.wait_ge(f2_done, at(f2_done, img, 0))
                    if high_by_act(j):
                        if j >= N_P16:
                            act.wait_ge(pv_done, at(pv_done, img, j - N_P16 + 1))
                        act.activation(p_h[:, j % N_P16, :, q0:QB], ps[:, bank:bank + 2, q0:QB],
                                       ACT.Exp, bias=exp_bias[:, :], scale=scale).then_inc(p_hi_act, 1)
                    if j >= N_P32:
                        i = j - N_P32
                        if i % 2:
                            act.wait_ge(p_lo_pool, at(p_lo_pool, img, i // 2 + 1))
                        else:
                            act.wait_ge(p_lo_dve, at(p_lo_dve, img, i // 2 + 1))
                    act.activation(p32[:, j % N_P32, :, q0:QB], ps[:, bank:bank + 2, q0:QB],
                                   ACT.Exp, bias=exp_bias[:, :], scale=scale).then_inc(e_done, 1)
                    if j == 4 and previous is not None:
                        store(previous, 1)
                    if j == 5:
                        rows_of_maxima(img, 1, 3)
                    if run < len(ends) and j == ends[run] + 4 + NORM_PARTS:
                        high_of_output(img, run)
                        run += 1
                    aside.until(j)
                aside.finish()
                assert run == len(ends) - 1

            def experts(img, following):
                aside = Aside(tail(img, 1))
                for i in range(NB * CHUNKS):
                    n = i % CHUNKS
                    act.wait_ge(h_ps, at(h_ps, img, i + 1))
                    if i == 0:
                        act.wait_ge(pv_done, at(pv_done, img, NE))
                    if i >= N_H:
                        act.wait_ge(h_lo, at(h_lo, img, i - N_H + 1))
                    act.activation(h32[:, i % N_H, :], ps[:, i % 2, :], ACT.Gelu,
                                   scale=1 / (U_SCALE * W_SCALE), bias=b1_sb[:, n:n + 1])\
                       .then_inc(h_act, 1)
                    if i >= N_H:
                        act.wait_ge(f2_done, at(f2_done, img, i - N_H + 1))
                    act.wait_ge(h_act, at(h_act, img, i + 1))
                    act.activation(h_h[:, i % N_H, :], h32[:, i % N_H, :], ACT.Copy, scale=A_SCALE)\
                       .then_inc(h_hi, 1)
                    aside.until(i)
                    following.until(i)
                    if i == CHUNKS + 4:
                        store(img, 0)
                following.finish()

            act.wait_ge(setup_dve, 2)
            act.activation(bn_t[:, 1, :], bn_t[:, 0, :], ACT.Sqrt).then_inc(setup_act, 1)
            act.activation(bq_t[:, 1, :], bq_t[:, 0, :], ACT.Sqrt).then_inc(setup_act, 1)
            first = Aside(front(0, False))
            for n, (kind, c0, w) in enumerate(pieces):
                act.wait_ge(stage_in[n % 2], 16 * (n // 2 + 1))
                src = stage[:, n % 2, 0:w]
                dst = {"head": win_h, "tail": win_t, "out": wout_h_flat}[kind][:, c0:c0 + w]
                act.activation(dst, src, ACT.Copy, scale=W_SCALE).then_inc(stage_hi, 1)
                first.until(PIECE_AT[n])
            act.wait_ge(consts_ready, 1)
            first.finish()
            attend(0)
            with act.Fori(0, B - 1) as img:
                experts(img, Aside(front(img + 1, True)))
                attend(img + 1, img)
            experts(B - 1, Aside(iter(())))
            store(B - 1, 1)
            act.wait_ge(stored, B * whole(stored))

        @block.gpsimd
        def _(pool):
            fills = ((minus_half[:, :], -0.5), (euler[:, :, :], float(np.e)), (ones16[:, :], 1.0), (exp_bias[:, :], float(np.log(P_SCALE))),
                     (xs[CC:CC + 1, :, :], 1.0),
                     (k4[3 * D:3 * D + 2, :, :], M_SCALE), (o_h[TAIL:TAIL + 1, 1, :], A_SCALE),
                     (o_l[TAIL:TAIL + 1, 1, :], 0.0), (b2_ones[:, :], A_SCALE))
            for n, (dst, value) in enumerate(fills):
                nc.gpsimd.memset(dst, value).then_inc(setup_pool, 1)
                pool.wait_ge(setup_pool, n + 1)

            def group_power(img):
                pool.wait_ge(var_ready, at(var_ready, img, 1))
                nc.gpsimd.tensor_tensor(g_st[1][:, :], g_st[0][:, :], minus_half[0:CC, 0:2], ALU.pow)\
                  .then_inc(pow_done, 1)

            def attend(img):
                pool.wait_ge(var_ready, at(var_ready, img, 2))
                nc.gpsimd.tensor_tensor(norm1.pow[:, :], norm1.var[:, :], minus_half[:, 0:NT], ALU.pow)\
                  .then_inc(pow_done, 1)

                def low_of_output(run, halves):
                    b, pair = divmod(run, PAIRS)
                    pool.wait_ge(p_lo_pool, at(p_lo_pool, img, halves))
                    if run:
                        pool.wait_ge(o_lo, at(o_lo, img, run))
                    pool.wait_ge(o_hi, at(o_hi, img, run + 1))
                    rows = slice(2 * D * (pair % 2), 2 * D * (pair % 2) + 2 * D)
                    where = (rows, pair // 2, slice(b * QB, (b + 1) * QB))
                    nc.gpsimd.tensor_tensor(o_l[where], o32[where], o_h[where], ALU.subtract).then_inc(o_lo, 1)

                def power_of_tail(b):
                    pool.wait_ge(var2_ready, at(var2_ready, img, b + 1))
                    nc.gpsimd.tensor_tensor(norm2.pow[:, :], norm2.var[:, :], minus_half[:, 0:TB], ALU.pow)\
                      .then_inc(pow2_done, 1)

                ends = run_ends()
                run = 0
                for j in range(1, NE, 2):
                    b, pair, kc = E_ITEMS[j]
                    q0 = max(0, kc - b * TB) * P
                    pool.wait_ge(p_hi_act, at(p_hi_act, img, highs(j, True)))
                    pool.wait_ge(e_done, at(e_done, img, j + 1))
                    if j >= N_P16:
                        pool.wait_ge(pv_done, at(pv_done, img, j - N_P16 + 1))
                    nc.gpsimd.tensor_tensor(p_l[:, j % N_P16, :, q0:QB], p32[:, j % N_P32, :, q0:QB],
                                            p_h[:, j % N_P16, :, q0:QB], ALU.subtract)\
                      .then_inc(p_lo_pool, 1)
                    if run < len(ends) and j >= ends[run] + 5 + NORM_PARTS:
                        low_of_output(run, (j + 1) // 2)
                        run += 1
                        pool.wait_ge(o_lo, at(o_lo, img, run))
                    if j in (TAIL_AT[0]["residual"], TAIL_AT[0]["residual"] + 1):
                        power_of_tail(0)
                for run in range(run, len(ends)):
                    low_of_output(run, NE // 2)
                pool.wait_ge(o_lo, at(o_lo, img, len(ends)))
                power_of_tail(1)

            def gate_exp_of_block_1(img):
                pool.wait_ge(gate_sub, at(gate_sub, img, 2))
                nc.gpsimd.tensor_tensor(gex[:, :, :], euler[:, :, :], gsc[:, :, :], ALU.pow)\
                  .then_inc(gate_exp, 1)

            group_power(0)
            with pool.Fori(0, B - 1) as img:
                attend(img)
                group_power(img + 1)
                gate_exp_of_block_1(img)
            attend(B - 1)
            gate_exp_of_block_1(B - 1)

        @block.vector
        def _(dve):
            V = nc.vector

            def norm_statistics(norm, img, src, tiles, step, steps, signal):
                for n, t in enumerate(tiles):
                    V.bn_stats(norm.stats[:, n, :], src[:, t, :]).then_inc(step, 1)
                dve.wait_ge(step, at(step, img, steps.more(len(tiles))))
                even, odd = norm.stats[:, :, 0:3], norm.stats[:, :, 3:6]
                V.tensor_tensor(norm.sums[:, 0, :], even[:, :, 1], odd[:, :, 1], ALU.add).then_inc(step, 1)
                V.tensor_tensor(norm.sums[:, 1, :], even[:, :, 1], odd[:, :, 1], ALU.subtract).then_inc(step, 1)
                V.tensor_tensor(norm.sums[:, 2, :], even[:, :, 2], odd[:, :, 2], ALU.add).then_inc(step, 1)
                dve.wait_ge(step, at(step, img, steps.more(3)))
                V.tensor_scalar(norm.mean[:, :], norm.sums[:, 0, :], 1 / 2, None, ALU.mult).then_inc(step, 1)
                V.scalar_tensor_tensor(out=norm.sums[:, 1, :], in0=norm.sums[:, 1, :], scalar=1 / 4,
                                       in1=norm.sums[:, 1, :], op0=ALU.mult, op1=ALU.mult).then_inc(step, 1)
                V.tensor_scalar(norm.sums[:, 2, :], norm.sums[:, 2, :], 1 / C, 1e-5, ALU.mult, ALU.add)\
                 .then_inc(step, 1)
                dve.wait_ge(step, at(step, img, steps.more(3)))
                V.tensor_tensor(norm.var[:, :], norm.sums[:, 1, :], norm.sums[:, 2, :], ALU.add)\
                 .then_inc(signal, 1)

            def refine(img, v, y, a, rstd, step, steps):
                V.tensor_tensor(a, y, y, ALU.mult).then_inc(step, 1)
                dve.wait_ge(step, at(step, img, steps.more(1)))
                V.scalar_tensor_tensor(out=a, in0=a, scalar=-0.5, in1=v, op0=ALU.mult, op1=ALU.mult).then_inc(step, 1)
                dve.wait_ge(step, at(step, img, steps.more(1)))
                V.scalar_tensor_tensor(out=rstd, in0=a, scalar=1.5, in1=y, op0=ALU.add, op1=ALU.mult).then_inc(step, 1)
                dve.wait_ge(step, at(step, img, steps.more(1)))

            def normalized_block(norm, img, src, b, tiles, step, steps, signal):
                for n, t in zip(tiles, range(b * TB, (b + 1) * TB)):
                    V.tensor_scalar(u[:, t, 0:C], src[:, t, :], norm.mean[:, n:n + 1],
                                    norm.rstd[:, n:n + 1], ALU.subtract, ALU.mult).then_inc(step, 1)
                dve.wait_ge(step, at(step, img, steps.more(TB)))
                V.tensor_copy(u[:, b * TB:(b + 1) * TB, C:], u[:, b * TB:(b + 1) * TB, P:C])\
                 .then_inc(signal, 1)

            def front(img, later):
                steps = Count()
                yield FRONT_AT["stats"]
                dve.wait_ge(x_ch_in, at(x_ch_in, img, 16))
                for c in range(2):
                    for s in range(2):
                        V.bn_stats(gn_st[:, c, s, :], xc[:, c, s * 512:(s + 1) * 512]).then_inc(front_step, 1)
                dve.wait_ge(front_step, at(front_step, img, steps.more(4)))
                part = gn_st[:, :, :, :].rearrange("p c s (o k) -> p c (s o) k", o=2)
                V.tensor_reduce(gn_s[:, :], part[:, :, :, 1], AX.X, ALU.add).then_inc(gn_rhs, 1)
                yield FRONT_AT["sums"]
                dve.wait_ge(gn_ps, at(gn_ps, img, 1))
                V.tensor_scalar(gn_m[:, :], ps[0:CC, 7, 0:2], 1 / 4, None, ALU.mult).then_inc(front_step, 1)
                dve.wait_ge(front_step, at(front_step, img, steps.more(1)))
                V.tensor_tensor(gn_d[:, :, :], part[:, :, :, 1],
                                gn_m[:, :, None].broadcast_to([CC, 2, 4]), ALU.subtract).then_inc(front_step, 1)
                dve.wait_ge(front_step, at(front_step, img, steps.more(1)))
                V.tensor_tensor(gn_d[:, :, :], gn_d[:, :, :], gn_d[:, :, :], ALU.mult).then_inc(front_step, 1)
                dve.wait_ge(front_step, at(front_step, img, steps.more(1)))
                V.scalar_tensor_tensor(out=gn_d[:, :, :], in0=part[:, :, :, 2], scalar=4 / N,
                                       in1=gn_d[:, :, :], op0=ALU.mult, op1=ALU.add).then_inc(front_step, 1)
                dve.wait_ge(front_step, at(front_step, img, steps.more(1)))
                V.tensor_reduce(gn_v[:, :], gn_d[:, :, :], AX.X, ALU.add).then_inc(gn_rhs, 1)
                yield FRONT_AT["variance"]
                dve.wait_ge(gn_ps, at(gn_ps, img, 2))
                V.tensor_scalar(g_st[0][:, :], ps[0:CC, 7, 2:4], 1 / 4, 1e-5, ALU.mult, ALU.add)\
                 .then_inc(var_ready, 1)
                yield FRONT_AT["clip"]
                dve.wait_ge(pow_done, at(pow_done, img, 1))
                refine(img, g_st[0][:, :], g_st[1][:, :], g_st[2][:, :], g_rstd[:, :], front_step, steps)
                V.scalar_tensor_tensor(out=gn_b[:, :], in0=gn_m[:, :], scalar=-1.0, in1=g_rstd[:, :],
                                       op0=ALU.mult, op1=ALU.mult).then_inc(gn_ready, 1)

                tx = tmp[0:CC, 0:2 * N].rearrange("p (c n) -> p c n", c=2)

                def spike(dst, t, signal):
                    V.tensor_scalar(t, t, 4.0, MAGIC, ALU.min, ALU.add).then_inc(front_step, 1)
                    dve.wait_ge(front_step, at(front_step, img, steps.more(1)))
                    V.tensor_scalar(dst, t, MAGIC, None, ALU.subtract).then_inc(signal, 1)

                for c in range(2):
                    yield FRONT_AT["xs"] + c
                    dve.wait_ge(x_relu, at(x_relu, img, c + 1))
                    spike(xs[0:CC, c, :], tx[:, c, :], xs_ready)
                for b in range(NB):
                    yield FRONT_AT["q_int"] + 2 * b
                    if b == 0:
                        if later:
                            dve.wait_ge(p_lo_pool, at(p_lo_pool, img, 0))
                    dve.wait_ge(q_relu, at(q_relu, img, 2 * b + 2))
                    spike(qi[:, :, b * QB:(b + 1) * QB], tx[:, :, b * QB:(b + 1) * QB], q_int)
                for i in range(NT // 2):
                    yield FRONT_AT["kv_int"] + i
                    dve.wait_ge(kv_relu, at(kv_relu, img, 2 * i + 2))
                    spike(kvi[:, 2 * i:2 * i + 2, :].rearrange("p t c -> p (t c)"),
                          tmp[:, i * 4 * C:(i + 1) * 4 * C], kv_int)
                yield FRONT_AT["kvm_split"]
                dve.wait_ge(kvm_ps, at(kvm_ps, img, 1))
                V.tensor_tensor(kv32[:, :, :], ps[0:CC, 4, 0:C].rearrange("p (m e) -> p m e", m=2),
                                block_diag[:, None, :].broadcast_to([CC, 2, CC]), ALU.mult).then_inc(front_step, 1)
                dve.wait_ge(front_step, at(front_step, img, steps.more(1)))
                V.tensor_copy(kv_h[:, :, :], kv32[:, :, :]).then_inc(front_step, 1)
                dve.wait_ge(front_step, at(front_step, img, steps.more(1)))
                V.tensor_tensor(kv_l[:, :, :], kv32[:, :, :], kv_h[:, :, :], ALU.subtract)\
                 .then_inc(kv_split, 1)
                for b in range(NB):
                    yield FRONT_AT["attn_int"] + b
                    dve.wait_ge(at_ps, at(at_ps, img, b + 1))
                    V.tensor_scalar(tx[:, :, b * QB:(b + 1) * QB], ps[0:CC, 4 + 2 * b:6 + 2 * b, :],
                                    SPIKE_ATTN, 4.0, ALU.mult, ALU.min).then_inc(front_step, 1)
                    dve.wait_ge(front_step, at(front_step, img, steps.more(1)))
                    V.tensor_scalar(ai[0:CC, :, b * QB:(b + 1) * QB], tx[:, :, b * QB:(b + 1) * QB],
                                    MAGIC, MAGIC, ALU.add, ALU.subtract).then_inc(a_int, 1)
                for i in range(NT // 2):
                    if i % 2 == 0:
                        yield FRONT_AT["residual"] + i // 2
                    if i == 0:
                        dve.wait_ge(x_tok_in, at(x_tok_in, img, 16))
                    dve.wait_ge(p_ps, at(p_ps, img, i + 1))
                    ins = V.scalar_tensor_tensor(
                        out=t1[:, 2 * i:2 * i + 2, :],
                        in0=ps[:, 4 + i, 0:2 * C].rearrange("p (t c) -> p t c", t=2), scalar=1 / SPIKE_SCALE,
                        in1=xt[:, 2 * i:2 * i + 2, :], op0=ALU.mult, op1=ALU.add)
                ins.then_inc(t1_ready, 1)
                dve.wait_ge(t1_ready, at(t1_ready, img, 1))

                yield FRONT_AT["residual"] + 2
                norm_statistics(norm1, img, t1, range(NT), front_step, steps, var_ready)
                yield FRONT_AT["norm"]
                dve.wait_ge(pow_done, at(pow_done, img, 2))
                refine(img, norm1.var[:, :], norm1.pow[:, :], norm1.tmp[:, :], norm1.rstd[:, :],
                       front_step, steps)
                if later:
                    dve.wait_ge(u_tr, at(u_tr, img, 0))
                for b in range(NB):
                    yield FRONT_AT["norm"] + b
                    normalized_block(norm1, img, t1, b, range(b * TB, (b + 1) * TB), front_step, steps, a_ready)
                for b in range(NB):
                    yield FRONT_AT["low"] + b
                    dve.wait_ge(ah_done, at(ah_done, img, b + 1))
                    V.scalar_tensor_tensor(out=al[:, :, b * QB:(b + 1) * QB],
                                           in0=ps[:, 4 + 2 * b:6 + 2 * b, :], scalar=U_SCALE,
                                           in1=ah[:, :, b * QB:(b + 1) * QB], op0=ALU.mult,
                                           op1=ALU.subtract).then_inc(al_done, 1)
                for i in range(QK_PARTS * NB):
                    b, j = divmod(i, QK_PARTS)
                    yield FRONT_AT["qk_lo"] + (i + 1) // 2
                    tok = slice(b * QB, (b + 1) * QB)
                    dve.wait_ge(qk_hi, at(qk_hi, img, i + 1))
                    V.scalar_tensor_tensor(out=qk[:, 1, j, tok], in0=ps[:, 4 + i % 4, :],
                                           scalar=A_SCALE / (U_SCALE * W_SCALE), in1=qk[:, 0, j, tok],
                                           op0=ALU.mult, op1=ALU.subtract).then_inc(qk_lo, 1)
                for t in range(0, NT, 2):
                    if t % 4 == 0:
                        yield FRONT_AT["v_lo"] + t // 4
                    dve.wait_ge(v_hi, at(v_hi, img, t // 2 + 1))
                    V.scalar_tensor_tensor(out=v_l[:, t:t + 2, :],
                                           in0=ps[:, 4 + t // 2, 0:2 * C].rearrange("p (t c) -> p t c", t=2),
                                           scalar=A_SCALE / (U_SCALE * W_SCALE), in1=v_h[:, t:t + 2, :],
                                           op0=ALU.mult, op1=ALU.subtract).then_inc(v_lo, 1)
                for i, (b, t, half, pair) in enumerate(M_ITEMS):
                    yield maximum_step(i)
                    dve.wait_ge(m_ps, at(m_ps, img, i + 1))
                    width = (t % TB + 1) * P if half == b else QB
                    bank = 4 + 2 * (i % 2)
                    V.tensor_reduce(mx[:, half, t, 2 * pair:2 * pair + 2],
                                    ps[:, bank:bank + 2, 0:width], AX.X, ALU.max)\
                     .then_inc(m_used, 1)
                    if i + 1 in (NM // 3, NM):
                        dve.wait_ge(m_used, at(m_used, img, i + 1))
                        rows = slice(b * TB, (b + 1) * TB)
                        if b:
                            V.tensor_tensor(mx[:, 0, rows, :], mx[:, 0, rows, :], mx[:, 1, rows, :], ALU.max)\
                             .then_inc(front_step, 1)
                            dve.wait_ge(front_step, at(front_step, img, steps.more(1)))
                        V.tensor_scalar(m16[:, rows, :, 0], mx[:, 0, rows, :], -1 / M_SCALE, None, ALU.mult)\
                         .then_inc(front_step, 1)
                        dve.wait_ge(front_step, at(front_step, img, steps.more(1)))
                        V.scalar_tensor_tensor(out=m16[:, rows, :, 1], in0=mx[:, 0, rows, :],
                                               scalar=-1 / M_SCALE, in1=m16[:, rows, :, 0],
                                               op0=ALU.mult, op1=ALU.subtract).then_inc(m_split, 1)
                assert steps.n == FRONT_STEPS, steps.n

            def tail(img, b, later):
                steps = Count()
                steps.more(b * TAIL_STEPS)
                when, bank = TAIL_AT[b], 2 + 2 * b
                yield when["residual"]
                if b == 0 and later:
                    dve.wait_ge(stored, at(stored, img, 0))
                for i in range(2):
                    n = b * TB + 2 * i
                    dve.wait_ge(wo_ps, at(wo_ps, img, 2 * b + i + 1))
                    V.scalar_tensor_tensor(
                        out=acc[:, n:n + 2, :],
                        in0=ps[:, bank + i, 0:2 * C].rearrange("p (t c) -> p t c", t=2),
                        scalar=1 / (A_SCALE * W_SCALE), in1=t1[:, n:n + 2, :],
                        op0=ALU.mult, op1=ALU.add).then_inc(tail_step, 1)
                dve.wait_ge(tail_step, at(tail_step, img, steps.more(2)))
                norm_statistics(norm2, img, acc, range(b * TB, (b + 1) * TB), tail_step, steps, var2_ready)
                yield when["norm"]
                dve.wait_ge(pow2_done, at(pow2_done, img, b + 1))
                refine(img, norm2.var[:, :], norm2.pow[:, :], norm2.tmp[:, :], norm2.rstd[:, :],
                       tail_step, steps)
                normalized_block(norm2, img, acc, b, range(TB), tail_step, steps, u_ready)
                yield when["low"]
                dve.wait_ge(uh_done, at(uh_done, img, b + 1))
                V.scalar_tensor_tensor(out=ul[:, :, b * QB:(b + 1) * QB],
                                       in0=ps[:, bank:bank + 2, :], scalar=U_SCALE,
                                       in1=uh[:, :, b * QB:(b + 1) * QB], op0=ALU.mult,
                                       op1=ALU.subtract).then_inc(ul_done, 1)

                yield when["gate"]
                tiles = slice(b * TB, (b + 1) * TB)
                dve.wait_ge(gate_ps, at(gate_ps, img, b + 1))
                V.scalar_tensor_tensor(
                    out=gsc[:, :, :], in0=ps[:, bank, 0:TB * EXPERTS].rearrange("p (t e) -> p t e", t=TB),
                    scalar=1 / (U_SCALE * W_SCALE), in1=gb_sb[:, tiles, :], op0=ALU.mult, op1=ALU.add)\
                 .then_inc(tail_step, 1)
                dve.wait_ge(tail_step, at(tail_step, img, steps.more(1)))
                V.tensor_reduce(gt1[:, :], gsc[:, :, :], AX.X, ALU.max).then_inc(gate_used, 1)
                dve.wait_ge(gate_used, at(gate_used, img, b + 1))
                each = [P, TB, EXPERTS]
                V.tensor_tensor(gsc[:, :, :], gsc[:, :, :], gt1[:, :, None].broadcast_to(each), ALU.subtract)\
                 .then_inc(gate_sub, 1)
                yield when["best"]
                dve.wait_ge(gate_exp, at(gate_exp, img, b + 1))
                V.tensor_reduce(gt1[:, :], gex[:, :, :], AX.X, ALU.add).then_inc(tail_step, 1)
                dve.wait_ge(tail_step, at(tail_step, img, steps.more(1)))
                V.reciprocal(gt2[:, :], gt1[:, :]).then_inc(tail_step, 1)
                dve.wait_ge(tail_step, at(tail_step, img, steps.more(1)))
                V.tensor_tensor(gpr[:, :, :], gex[:, :, :], gt2[:, :, None].broadcast_to(each), ALU.mult)\
                 .then_inc(tail_step, 1)
                dve.wait_ge(tail_step, at(tail_step, img, steps.more(1)))
                yield when["best"] + 1
                square = [P, TB, EXPERTS, EXPERTS]
                other = gpr[:, :, None, :].broadcast_to(square)
                own = gpr[:, :, :, None].broadcast_to(square)
                tie = kst[:, None, K_TIE:K_TIE + EXPERTS * EXPERTS].broadcast_to([P, TB, EXPERTS * EXPERTS])
                flat = "p t i j -> p t (i j)"
                V.tensor_tensor(gcmp[:, :, :, :], other, own, ALU.is_equal).then_inc(tail_step, 1)
                dve.wait_ge(tail_step, at(tail_step, img, steps.more(1)))
                V.tensor_tensor(gcmp[:, :, :, :].rearrange(flat), gcmp[:, :, :, :].rearrange(flat),
                                tie, ALU.mult).then_inc(tail_step, 1)
                V.tensor_tensor(gcm2[:, :, :, :], other, own, ALU.is_gt).then_inc(tail_step, 1)
                dve.wait_ge(tail_step, at(tail_step, img, steps.more(2)))
                V.tensor_tensor(gcmp[:, :, :, :], gcmp[:, :, :, :], gcm2[:, :, :, :], ALU.add).then_inc(tail_step, 1)
                dve.wait_ge(tail_step, at(tail_step, img, steps.more(1)))
                V.tensor_reduce(gcnt[:, :, :], gcmp[:, :, :, :], AX.X, ALU.add).then_inc(tail_step, 1)
                dve.wait_ge(tail_step, at(tail_step, img, steps.more(1)))
                V.scalar_tensor_tensor(out=gpr[:, :, :], in0=gcnt[:, :, :], scalar=2.0,
                                       in1=gpr[:, :, :], op0=ALU.is_lt, op1=ALU.mult).then_inc(tail_step, 1)
                dve.wait_ge(tail_step, at(tail_step, img, steps.more(1)))
                V.tensor_reduce(gt1[:, :], gpr[:, :, :], AX.X, ALU.add).then_inc(tail_step, 1)
                dve.wait_ge(tail_step, at(tail_step, img, steps.more(1)))
                V.tensor_scalar(gt1[:, :], gt1[:, :], 1e-9, None, ALU.add).then_inc(tail_step, 1)
                dve.wait_ge(tail_step, at(tail_step, img, steps.more(1)))
                V.reciprocal(gt2[:, :], gt1[:, :]).then_inc(tail_step, 1)
                dve.wait_ge(tail_step, at(tail_step, img, steps.more(1)))
                V.scalar_tensor_tensor(out=gate[:, tiles, :], in0=gpr[:, :, :],
                                       scalar=1 / (A_SCALE * W_SCALE),
                                       in1=gt2[:, :, None].broadcast_to(each),
                                       op0=ALU.mult, op1=ALU.mult).then_inc(tail_step, 1)
                dve.wait_ge(tail_step, at(tail_step, img, steps.more(1)))
                assert steps.n == (b + 1) * TAIL_STEPS, steps.n

            def attend(img, later):
                def normalize(run, part):
                    b, pair = divmod(run, PAIRS)
                    dve.wait_ge(pv_done, at(pv_done, img, run_ends()[run] + 1))
                    bank = PV_BANK[run]
                    c0, c1 = part * QB // NORM_PARTS, (part + 1) * QB // NORM_PARTS
                    V.reciprocal(rden[:, c0:c1], ps[2 * D:4 * D, bank, c0:c1]).then_inc(rden_ready, 1)
                    dve.wait_ge(rden_ready, at(rden_ready, img, NORM_PARTS * run + part + 1))
                    rows = slice(2 * D * (pair % 2), 2 * D * (pair % 2) + 2 * D)
                    ins = V.tensor_tensor(o32[rows, pair // 2, b * QB + c0:b * QB + c1],
                                          ps[0:2 * D, bank, c0:c1], rden[:, c0:c1], ALU.mult)
                    if part == NORM_PARTS - 1:
                        ins.then_inc(o_done, 1)

                aside = Aside(tail(img, 0, later))
                if later:
                    dve.wait_ge(f2_done, at(f2_done, img, 0))
                ends = run_ends()
                run = 0
                for j, (b, pair, kc) in enumerate(E_ITEMS):
                    q0 = max(0, kc - b * TB) * P
                    if j % 2 == 0:
                        dve.wait_ge(e_done, at(e_done, img, j + 1))
                        if j >= N_P16:
                            dve.wait_ge(pv_done, at(pv_done, img, j - N_P16 + 1))
                        if high_by_act(j):
                            dve.wait_ge(p_hi_act, at(p_hi_act, img, highs(j, True)))
                        else:
                            V.tensor_copy(p_h[:, j % N_P16, :, q0:QB], p32[:, j % N_P32, :, q0:QB])\
                             .then_inc(p_hi_dve, 1)
                            dve.wait_ge(p_hi_dve, at(p_hi_dve, img, highs(j, False)))
                        V.tensor_tensor(p_l[:, j % N_P16, :, q0:QB], p32[:, j % N_P32, :, q0:QB],
                                        p_h[:, j % N_P16, :, q0:QB], ALU.subtract).then_inc(p_lo_dve, 1)
                    if run < len(ends) and j >= ends[run] + 3:
                        part = j - ends[run] - 3
                        normalize(run, part)
                        run += part == NORM_PARTS - 1
                    aside.until(j)
                aside.finish()
                for run in range(run, len(ends)):
                    for part in range(NORM_PARTS):
                        normalize(run, part)

            def experts(img, following):
                def add_expert(y):
                    b, e = divmod(y, EXPERTS)
                    dve.wait_ge(f2_done, at(f2_done, img, (y + 1) * HC))
                    for t in range(TB):
                        n = b * TB + t
                        if y and t == 0:
                            dve.wait_ge(y_used, at(y_used, img, y))
                        ins = V.scalar_tensor_tensor(
                            out=acc[:, n, :], in0=ps[:, 2 + t // 2, (t % 2) * C:(t % 2 + 1) * C],
                            scalar=gate[:, n, e:e + 1], in1=acc[:, n, :], op0=ALU.mult, op1=ALU.add)
                    ins.then_inc(y_used, 1)

                aside = Aside(tail(img, 1, True))
                for i in range(NB * CHUNKS + F_LAG):
                    following.until(i - 0.5)
                    if i >= F_LAG and (i - F_LAG) % HC == HC - 1:
                        add_expert((i - F_LAG) // HC)
                    if i < NB * CHUNKS:
                        if i >= N_H:
                            dve.wait_ge(f2_done, at(f2_done, img, i - N_H + 1))
                        s = i % N_H
                        dve.wait_ge(h_hi, at(h_hi, img, i + 1))
                        V.scalar_tensor_tensor(out=h_l[:, s, :], in0=h32[:, s, :], scalar=A_SCALE,
                                               in1=h_h[:, s, :], op0=ALU.mult, op1=ALU.subtract)\
                         .then_inc(h_lo, 1)
                    aside.until(i)
                    following.until(i)
                following.finish()

            dve.wait_ge(small_in, 16 * n_small)
            setup = Count()
            V.tensor_scalar(bn_t[:, 0, :], bn_st[:, 3, :], 1e-5, None, ALU.add).then_inc(setup_dve, 1)
            dve.wait_ge(setup_dve, setup.more(1))
            V.tensor_scalar(bq_t[:, 0, :], bq_st[:, :, 3], 1e-5, None, ALU.add).then_inc(setup_dve, 1)
            dve.wait_ge(setup_dve, setup.more(1))
            V.tensor_copy(ident16[:, :], ident).then_inc(setup_dve, 1)
            dve.wait_ge(setup_dve, setup.more(1))
            V.tensor_copy(identb[:, :], ident).then_inc(setup_dve, 1)
            dve.wait_ge(setup_dve, setup.more(1))
            V.tensor_scalar(mask_kq[:, :], kst[:, K_MKQ:K_MKQ + P], MASKED, None, ALU.mult).then_inc(setup_dve, 1)
            dve.wait_ge(setup_dve, setup.more(1))
            V.tensor_scalar(mask_qk[:, :], kst[:, K_MQK:K_MQK + P], MASKED, None, ALU.mult).then_inc(setup_dve, 1)
            dve.wait_ge(setup_dve, setup.more(1))
            V.tensor_scalar(b2_t[:, :], b2_st[:, :], W_SCALE, None, ALU.mult).then_inc(setup_dve, 1)
            dve.wait_ge(setup_dve, setup.more(1))
            V.tensor_scalar(b2_st[:, :], b2_st[:, :], W_SCALE, None, ALU.mult).then_inc(setup_dve, 1)
            dve.wait_ge(setup_dve, setup.more(1))
            V.tensor_scalar(b2_t[:, :], b2_t[:, :], kst[0:2, K_ROW:K_ROW + 1], None, ALU.mult).then_inc(setup_dve, 1)
            dve.wait_ge(setup_dve, setup.more(1))
            V.tensor_tensor(b2_sb[:, :], b2_st[:, :], b2_t[:, :], ALU.subtract).then_inc(setup_dve, 1)
            dve.wait_ge(setup_dve, setup.more(1))

            def newton(y, v, a, into):
                V.tensor_tensor(a, y, y, ALU.mult).then_inc(setup_dve, 1)
                dve.wait_ge(setup_dve, setup.more(1))
                V.scalar_tensor_tensor(out=a, in0=a, scalar=-0.5, in1=v, op0=ALU.mult, op1=ALU.mult).then_inc(setup_dve, 1)
                dve.wait_ge(setup_dve, setup.more(1))
                V.scalar_tensor_tensor(out=into, in0=a, scalar=1.5, in1=y, op0=ALU.add, op1=ALU.mult).then_inc(setup_dve, 1)
                dve.wait_ge(setup_dve, setup.more(1))

            dve.wait_ge(setup_act, 2)
            V.reciprocal(bq_t[:, 1, :], bq_t[:, 1, :]).then_inc(setup_dve, 1)
            dve.wait_ge(setup_dve, setup.more(1))
            newton(bq_t[:, 1, :], bq_t[:, 0, :], bq_t[:, 2, :], bq_t[:, 1, :])
            V.tensor_tensor(bq_t[:, 2, :], bq_t[:, 1, :], bq_st[:, :, 0], ALU.mult).then_inc(setup_dve, 1)
            dve.wait_ge(setup_dve, setup.more(1))
            V.tensor_tensor(bq_t[:, 3, :], bq_t[:, 2, :], bq_st[:, :, 2], ALU.mult).then_inc(setup_dve, 1)
            dve.wait_ge(setup_dve, setup.more(1))
            V.tensor_tensor(q_sb[:, :, 1], bq_st[:, :, 1], bq_t[:, 3, :], ALU.subtract).then_inc(setup_dve, 1)
            dve.wait_ge(setup_dve, setup.more(1))
            V.tensor_scalar(q_sb[:, :, 0], bq_t[:, 2, :], 1 / SPIKE_SCALE, None, ALU.mult).then_inc(setup_dve, 1)
            dve.wait_ge(setup_dve, setup.more(1))
            V.reciprocal(bn_t[:, 1, :], bn_t[:, 1, :]).then_inc(setup_dve, 1)
            dve.wait_ge(setup_dve, setup.more(1))
            newton(bn_t[:, 1, :], bn_t[:, 0, :], bn_t[:, 2, :], bn_t[:, 1, :])
            V.tensor_tensor(bn_t[:, 0, :], bn_t[:, 1, :], bn_st[:, 0, :], ALU.mult).then_inc(setup_dve, 1)
            dve.wait_ge(setup_dve, setup.more(1))
            V.tensor_tensor(bn_t[:, 1, :], bn_t[:, 0, :], bn_st[:, 2, :], ALU.mult).then_inc(setup_dve, 1)
            dve.wait_ge(setup_dve, setup.more(1))
            V.tensor_tensor(bn_t[:, 2, :], bn_st[:, 1, :], bn_t[:, 1, :], ALU.subtract).then_inc(setup_dve, 1)
            dve.wait_ge(setup_dve, setup.more(1))
            wc = tmp[0:CC + 1, 0:2 * NCV].rearrange("p (c n) -> p c n", c=2)
            for c in range(2):
                V.tensor_scalar(wc[0:CC, c, 0:C], wc[0:CC, c, 0:C], W_SCALE, None, ALU.mult).then_inc(setup_dve, 1)
                dve.wait_ge(setup_dve, setup.more(1))
                V.scalar_tensor_tensor(out=wc[0:CC, c, C:], in0=wc[0:CC, c, C:], scalar=W_SCALE,
                                            in1=bn_t[0:CC, 0, :], op0=ALU.mult, op1=ALU.mult).then_inc(setup_dve, 1)
                dve.wait_ge(setup_dve, setup.more(1))
            V.tensor_scalar(wc[CC:CC + 1, 0, C:], bn_t[CC:CC + 1, 2, :], SPIKE_SCALE, None, ALU.mult).then_inc(setup_dve, 1)
            dve.wait_ge(setup_dve, setup.more(1))
            V.tensor_copy(wc_h[:, :, :], wc).then_inc(setup_dve, 1)
            dve.wait_ge(setup_dve, setup.more(1))
            V.tensor_tensor(wc_l[:, :, :], wc, wc_h[:, :, :], ALU.subtract).then_inc(setup_dve, 1)
            dve.wait_ge(setup_dve, setup.more(1))
            V.memset(gate[:, :, :], 0.0).then_inc(consts_ready, 1)
            first = Aside(front(0, False))
            for n, (kind, c0, w) in enumerate(pieces):
                dve.wait_ge(stage_hi, n + 1)
                rows = slice(TAIL, P) if kind == "tail" else slice(0, P)
                hi = {"head": win_h, "tail": win_t, "out": wout_h_flat}[kind][rows, c0:c0 + w]
                lo = {"head": win_l, "tail": win_t, "out": wout_l_flat}[kind][rows, c0:c0 + w]
                V.scalar_tensor_tensor(out=lo, in0=stage[rows, n % 2, 0:w], scalar=W_SCALE, in1=hi,
                                       op0=ALU.mult, op1=ALU.subtract).then_inc(stage_lo, 1)
                first.until(PIECE_AT[n])
            first.finish()
            attend(0, False)
            with dve.Fori(0, B - 1) as img:
                experts(img, Aside(front(img + 1, True)))
                attend(img + 1, True)
            experts(B - 1, Aside(iter(())))


def constants():
    k = np.zeros((P, K_COLS), np.float32)
    i = np.arange(P)
    k[:, K_ID:K_ID + P] = np.eye(P)
    k[:, K_MKQ:K_MKQ + P] = i[:, None] > i[None, :]
    k[:, K_MQK:K_MQK + P] = i[None, :] > i[:, None]
    c = np.arange(CC)
    per = C // GROUPS
    k[:CC, K_GRP:K_GRP + CC] = (c[:, None] // per == c[None, :] // per) / per
    hd = C // SPIKE_HEADS
    k[:CC, K_BLK:K_BLK + CC] = c[:, None] // hd == c[None, :] // hd
    k[:, K_ROW] = i
    e = np.arange(EXPERTS)
    k[:, K_TIE:] = (e[None, :] < e[:, None]).ravel()
    return k


def kernel(**inputs):
    import concourse.bacc as bacc
    from concourse.bass_utils import run_bass_kernel_spmd

    g = {k: np.asarray(v) for k, v in inputs.items()}
    x = g["x"].reshape(B, C, N)

    def halves(a):
        return a.reshape(2, CC, -1).transpose(1, 0, 2)

    conv = np.concatenate([g[f"L0_conv_{p}_w"].T for p in "qkvp"], axis=1)
    conv = np.concatenate([halves(conv), np.zeros((1, 2, 4 * C), np.float32)])
    rows = np.stack([np.concatenate([g[f"L0_conv_{p}_{what}"] for p in "kvp"])
                     for what in ("gamma", "beta", "mean", "var")])
    bn_q = halves(np.stack([g[f"L0_conv_q_{what}"] for what in ("gamma", "beta", "mean", "var")], axis=1))
    wq, wk = g["L1_attn_Wq"], g["L1_attn_Wk"]
    w_in = np.concatenate([wq[:, :P], wk[:, :P], wq[:, P:], wk[:, P:], g["L1_attn_Wv"], g["L1_ffn_gate_w"],
                           g["L1_ffn_w1"].transpose(1, 0, 2).reshape(C, EXPERTS * HID)], axis=1)
    w_in = np.stack([w_in[:P], np.concatenate([w_in[P:], w_in[P:]])])
    w_out = np.zeros((P, OUT_CHUNKS, C), np.float32)
    w_out[:, :CHUNKS] = g["L1_ffn_w2"].reshape(CHUNKS, P, C).transpose(1, 0, 2)
    w_out[:, CHUNKS] = g["L1_attn_Wo"][:P]
    w_out[:TAIL, CHUNKS + 1] = g["L1_attn_Wo"][P:]
    w_out[TAIL, CHUNKS + 1] = g["L1_attn_bo"]
    arrays = {
        "x_ch": x.reshape(B, 2, CC, N).transpose(0, 2, 1, 3),
        "x_tok": x.transpose(0, 2, 1).reshape(B, NT, P, C).transpose(0, 2, 1, 3),
        "consts": constants(),
        "w_conv": conv.reshape(CC + 1, 8 * C),
        "bn_rows": np.broadcast_to(rows, (CC + 1, 4, 3 * C)),
        "bn_q": bn_q,
        "w_in": w_in,
        "w_out": w_out.reshape(P, OUT_CHUNKS * C),
        "b1": g["L1_ffn_b1"].reshape(CHUNKS, P).T,
        "b2": np.broadcast_to(g["L1_ffn_b2"].reshape(1, EXPERTS * C), (2, EXPERTS * C)),
        "gate_b": np.broadcast_to(g["L1_ffn_gate_b"], (P, NT, EXPERTS)),
    }
    arrays = {k: np.ascontiguousarray(v) for k, v in arrays.items()}

    nc = bacc.Bacc("TRN2", target_bir_lowering=False, num_devices=1)
    aps = [nc.dram_tensor(k, a.shape, mybir.dt.from_np(a.dtype), kind="ExternalInput").ap()
           for k, a in arrays.items()]
    out = nc.dram_tensor("out", (B, P, NT, C), F32, kind="ExternalOutput").ap()
    build(nc, *aps, out)
    r = run_bass_kernel_spmd(nc, [arrays], core_ids=[0])
    y = r.results[0]["out"]
    return y.transpose(0, 3, 2, 1).reshape(B, C, 32, 32)
```
